# Optimizing a Trainium2 kernel written in Bass

```python
import numpy as np
import jax
import jax.numpy as jnp

def _softmax(x, axis=-1):
    return jax.nn.softmax(x, axis=axis)

def _gelu(x):
    return jax.nn.gelu(x, approximate=True)

def _silu(x):
    return jax.nn.silu(x)

def _sigmoid(x):
    return jax.nn.sigmoid(x)

def _layernorm(x, axis=-1, eps=1e-05):
    m = jnp.mean(x, axis=axis, keepdims=True)
    v = jnp.var(x, axis=axis, keepdims=True)
    return (x - m) / jnp.sqrt(v + eps)

def _scatter_add(tgt, idx, src, axis=0):
    return tgt.at[idx].add(src)

def _segment_sum(src, seg, n):
    return jax.ops.segment_sum(src, seg, n)
kernel_name = 'mk_adj_ffn_d1_adj_r2_ccd89c'

def setup_inputs(seed: int=0):
    np.random.seed(seed)
    _w = jnp.asarray

    def _rec_inputs():
        import jax
        import jax.numpy as jnp
        _gk = jax.random.key(seed)
        x = -0.0005207 + 1.001 * jax.random.normal(jax.random.fold_in(_gk, 1), (3327, 128), jnp.float32)
        _a = jax.random.bernoulli(jax.random.fold_in(_gk, 2), 0.00120228, (3327, 3327))
        adj = _a.astype(jnp.int32)
        return (x, adj)
    x, adj = _rec_inputs()

    def _L0_gnn_setup():
        import jax, jax.numpy as jnp
        import numpy as np
        N, D, H = (4096, 128, 128)
        KEEP_RATIO = 0.5
        TEMP = 1.0
        COS_EPS = 0.0001
        NEG = -9000000000000000.0

        def _cos_normalize(x):
            n = jnp.linalg.norm(x, axis=-1, keepdims=True)
            return x / jnp.maximum(n, COS_EPS)
        key = jax.random.key(seed)
        k1, k2, k3, k4 = jax.random.split(key, 4)
        features = jax.random.normal(k1, (N, D), dtype=jnp.float32)
        adj = jax.random.randint(k2, (N, N), 0, 2, dtype=jnp.int32)
        Wq = jax.random.normal(k3, (H, D), dtype=jnp.float32) * 0.001
        Wk = jax.random.normal(k4, (H, D), dtype=jnp.float32) * 0.001
        return {'features': features, 'adj': adj, 'Wq': Wq, 'Wk': Wk}
    _L0_gnn_all = _L0_gnn_setup()
    _L0_gnn_in = {k: v for k, v in _L0_gnn_all.items() if k in ('Wq', 'Wk')}
    del _L0_gnn_all

    def _L0_ffn_setup():
        import jax, jax.numpy as jnp
        import numpy as np
        D_MODEL = 128
        N_EXPERTS = 16
        HIDDEN = 256
        SCALE = 0.02
        key = jax.random.key(seed)
        ks = jax.random.split(key, 5)
        x = jax.random.normal(ks[0], (4, 4096, D_MODEL), dtype=jnp.float32)
        gate_w = jax.random.normal(ks[1], (D_MODEL, N_EXPERTS), dtype=jnp.float32) * SCALE
        gate_b = jnp.zeros((N_EXPERTS,), dtype=jnp.float32)
        w1 = jax.random.normal(ks[2], (N_EXPERTS, D_MODEL, HIDDEN), dtype=jnp.float32) * SCALE
        w2 = jax.random.normal(ks[3], (N_EXPERTS, D_MODEL, HIDDEN), dtype=jnp.float32) * SCALE
        w3 = jax.random.normal(ks[4], (N_EXPERTS, HIDDEN, D_MODEL), dtype=jnp.float32) * SCALE
        return {'x': x, 'gate_w': gate_w, 'gate_b': gate_b, 'w1': w1, 'w2': w2, 'w3': w3}
    _L0_ffn_all = _L0_ffn_setup()
    _L0_ffn_in = {k: v for k, v in _L0_ffn_all.items() if k in ('gate_w', 'gate_b', 'w1', 'w2', 'w3')}
    del _L0_ffn_all
    return {'x': x, 'adj': adj, 'L0_gnn_Wq': _L0_gnn_in['Wq'], 'L0_gnn_Wk': _L0_gnn_in['Wk'], 'L0_ffn_gate_w': _L0_ffn_in['gate_w'], 'L0_ffn_gate_b': _L0_ffn_in['gate_b'], 'L0_ffn_w1': _L0_ffn_in['w1'], 'L0_ffn_w2': _L0_ffn_in['w2'], 'L0_ffn_w3': _L0_ffn_in['w3']}

def reference(x, adj, L0_gnn_Wq, L0_gnn_Wk, L0_ffn_gate_w, L0_ffn_gate_b, L0_ffn_w1, L0_ffn_w2, L0_ffn_w3):
    import jax
    import jax.numpy as jnp

    def _L0_gnn_ref(features, adj, Wq, Wk):
        import jax, jax.numpy as jnp
        import numpy as np
        N, D, H = (4096, 128, 128)
        KEEP_RATIO = 0.5
        TEMP = 1.0
        COS_EPS = 0.0001
        NEG = -9000000000000000.0

        def _cos_normalize(x):
            n = jnp.linalg.norm(x, axis=-1, keepdims=True)
            return x / jnp.maximum(n, COS_EPS)
        Qn = _cos_normalize(features @ Wq.T)
        Kn = _cos_normalize(features @ Wk.T)
        raw_att = Kn @ Qn.T
        att = jnp.where(adj > 0, raw_att, NEG) * TEMP
        att = jax.nn.softmax(att, axis=1)
        prop_fea = att @ features
        adj_mask = (jnp.sum(adj, axis=1) > 0).astype(features.dtype)[:, None]
        prop_fea = adj_mask * prop_fea + (1.0 - adj_mask) * features
        return (1.0 - KEEP_RATIO) * prop_fea + KEEP_RATIO * features

    def _L0_ffn_ref(x, gate_w, gate_b, w1, w2, w3):
        import jax, jax.numpy as jnp
        import numpy as np
        D_MODEL = 128
        N_EXPERTS = 16
        HIDDEN = 256
        SCALE = 0.02
        n_experts = w1.shape[0]
        logits = jnp.einsum('bsd,de->bse', x, gate_w) + gate_b
        probs = jax.nn.softmax(logits, axis=-1)
        top_probs, top_idx = jax.lax.top_k(probs, 2)
        top_probs = top_probs / jnp.sum(top_probs, axis=-1, keepdims=True)
        dispatch = jnp.sum(jax.nn.one_hot(top_idx, n_experts, dtype=x.dtype) * top_probs[..., None], axis=-2)
        h1 = jnp.einsum('bsd,edh->bseh', x, w1)
        h2 = jnp.einsum('bsd,edh->bseh', x, w2)
        hidden = jax.nn.silu(h1) * h2
        expert_out = jnp.einsum('bseh,eho->bseo', hidden, w3)
        return jnp.einsum('bseo,bse->bso', expert_out, dispatch)
    x = x + _L0_gnn_ref(_layernorm(x, axis=-1), adj, L0_gnn_Wq, L0_gnn_Wk)
    x = x + _L0_ffn_ref(_layernorm(x, axis=-1)[None], L0_ffn_gate_w, L0_ffn_gate_b, L0_ffn_w1, L0_ffn_w2, L0_ffn_w3)[0]
    return x

_drawn_inputs = setup_inputs


def setup_inputs(seed=0):
    import zlib

    import numpy as np

    out = dict(_drawn_inputs(seed))
    spreads = {'L0_ffn_gate_b': (0.0, 0.8)}
    factors = {'L0_gnn_Wq': 4.798,
     'L0_gnn_Wk': 4.757,
     'L0_ffn_gate_w': 8.0,
     'L0_ffn_w1': 8.0,
     'L0_ffn_w2': 8.0,
     'L0_ffn_w3': 8.0}
    for name, (base, spread) in spreads.items():
        noise = np.random.default_rng([zlib.crc32(name.encode()), seed]).standard_normal(out[name].shape)
        drawn = base * np.exp(spread * noise) if base else spread * noise
        out[name] = jnp.asarray(drawn.astype(out[name].dtype))
    for name, factor in factors.items():
        out[name] = (out[name] * factor).astype(out[name].dtype)
    return out
```

```python
from contextlib import ExitStack

import concourse.bass as bass
from concourse import mybir

F32 = mybir.dt.float32
F16 = mybir.dt.float16
I32 = mybir.dt.int32
U32 = mybir.dt.uint32
ALU = mybir.AluOpType
ACT = mybir.ActivationFunctionType
AX_X = mybir.AxisListType.X

P = 128
LN_EPS = 1e-5
COS_EPS = 1e-4
MASKED = -30000.0
NO_ROW = 1 << 20


def spread(eng, body, count, unroll, lead, trail):
    assert lead % unroll == 0
    turns = (count - trail - lead) // unroll
    for i in range(lead):
        body(i, i % unroll)
    if turns > 0:
        with eng.Fori(0, turns) as turn:
            for k in range(unroll):
                body(turn * unroll + (lead + k), k)
    for i in range(lead + max(turns, 0) * unroll, count):
        body(i, i % unroll)


def at_least(i, n):
    return not isinstance(i, int) or i >= n


def before(i, n):
    return not isinstance(i, int) or i < n


def graph_attention_moe(nc, x, adj, Wq, Wk, gate_w, gate_b, w1, w2, w3, out):
    N, D = x.shape
    E, _, H = w1.shape
    T = -(-N // P)
    NP = T * P
    G = T // 2
    CH = 2 * P
    LAST = N - (T - 1) * P
    LAST16 = LAST // 16 * 16
    assert D == P and Wq.shape[0] == P and T % 2 == 0 and H == 2 * P and 0 < LAST < P and LAST > LAST16
    ROW = D + 2
    REGION = NP + P
    SLOTS = (2 * NP + E * (P - 1)) // P
    SLOTS += SLOTS % 2
    BLOCK = P // (P // E)
    PARTS = [0, 4, 14, T]
    AW = 2 * D + 2
    SEGS = [0, 4, 7, 10, G]
    BUF = [u % 3 for u in range(G - 1)] + [3]
    assert G % 3 == 1 and REGION % BLOCK == 0 and SLOTS <= P and BLOCK == 16

    with ExitStack() as ctx:
        def sb(name, shape, dt):
            return ctx.enter_context(nc.sbuf_tensor(name, shape, dt))

        def sem(name):
            return ctx.enter_context(nc.semaphore(name))

        routed = nc.dram_tensor("routed_rows", [(E + 1) * REGION, ROW], F32).ap()
        expert_out = nc.dram_tensor("expert_rows", [2 * NP, D], F32).ap()

        x_sb = sb("x_sb", [P, T * D], F32)
        f_sb = sb("f_sb", [P, T * D], F32)
        f_aug = sb("f_aug", [P, T, AW], F16)
        qk_hi = sb("qk_hi", [P, G, 2, CH], F16)
        qk_lo = sb("qk_lo", [P, G, 2, CH], F16)
        adj_sb = sb("adj_sb", [P, 2, NP], I32)
        mask = sb("mask", [P, 2, NP], F16)
        p_full = sb("p_full", [P, 4, 2 * CH], F32)
        p_hi = sb("p_hi", [P, 4, 2 * CH], F16)
        p_lo = sb("p_lo", [P, 4, 2 * CH], F16)
        w12_hi = sb("w12_hi", [P, E, 2 * H], F16)
        w12_lo = sb("w12_lo", [P, E, 2 * H], F16)
        w3_hi = sb("w3_hi", [P, E, 2 * D], F16)
        w3_lo = sb("w3_lo", [P, E, 2 * D], F16)
        w_raw = sb("w_raw", [P, 4, H], F32)
        id32 = sb("id32", [P, P], F32)
        id16 = sb("id16", [P, P], F16)
        before16 = sb("before16", [P, P], F16)
        ones16 = sb("ones16", [P, P], F16)
        one_row = sb("one_row", [1, P], F32)
        wqk = sb("wqk", [P, 2, D], F32)
        wqk_t = sb("wqk_t", [P, 2 * P], F32)
        gate_sb = sb("gate_sb", [P, E], F32)
        gate_bias = sb("gate_bias", [1, E], F32)
        expert_i = sb("expert_i", [P, E], I32)
        expert_f = sb("expert_f", [P, E], F32)
        start_f = sb("start_f", [P, E], F32)
        next_row = sb("next_row", [P, E], F32)
        dest_i = sb("dest_i", [P, 2, 2], I32)
        dest_f = sb("dest_f", [P, 2, 2], F32)
        neg_half = sb("neg_half", [P, T], F32)
        stats = sb("stats", [P, T, 6], F32)
        mean_var = sb("mean_var", [P, T, 2], F32)
        var_eps = sb("var_eps", [P, T], F32)
        rstd = sb("rstd", [P, T], F32)
        ft_sb = p_full[:, 0:1, :].rearrange("p a (b n) -> p (a b) n", b=2)
        sq_sb = p_full[:, 1, :]
        qn_sb = p_full[:, 2:4, :]
        ss = sb("ss", [P, 2, 4], F32)
        ss_max = sb("ss_max", [P, 2, 4], F32)
        rnorm = sb("rnorm", [P, 2, 4], F32)
        o_sb = sb("o_sb", [P, 2, 2 * D + 1], F32)
        mix = sb("mix", [P, 2, D], F32)
        keep = sb("keep", [P, 2, D], F32)
        small = sb("small", [P, 16, 2], F32)
        stats2 = sb("stats2", [P, 2, 6], F32)
        mean_var2 = sb("mean_var2", [P, 2, 2], F32)
        f2 = sb("f2", [P, 2, D], F32)
        f2_t = sb("f2_t", [P, CH], F32)
        logits = sb("logits", [P, 2, E], F32)
        top_v = sb("top_v", [P, 2, 8], F32)
        top_i = sb("top_i", [P, 2, 8], U32)
        top_f = sb("top_f", [P, 2, 2], F32)
        one_hot = sb("one_hot", [P, 4, E], F32)
        one_hot_sum = sb("one_hot_sum", [P, 2, E], F16)
        row_of = sb("row_of", [P, 2, E], F32)
        row_pick = sb("row_pick", [P, 4, E], F32)
        row_f = sb("row_f", [P, 4], F32)
        row_i = sb("row_i", [P, 4], I32)
        rows = sb("rows", [P, 4, ROW], F32)
        pad_rows = sb("pad_rows", [P, BLOCK, ROW], F32)
        tri_e = sb("tri_e", [P, E, E], F32)
        grid = sb("grid", [P, E, E], F32)
        part_i = sb("part_i", [P, 4], I32)
        part_f = sb("part_f", [P, 1], F32)
        pad_of = sb("pad_of", [P, 1], F32)
        pad_of2 = sb("pad_of2", [P, 2], F32)
        pad_e = sb("pad_e", [P, E], F32)
        ends = sb("ends", [P, 2, E], F32)
        ends_i = sb("ends_i", [P, E], I32)
        pad_pick = sb("pad_pick", [P, 2, E], F32)
        pad_end = sb("pad_end", [P, 2], F32)
        pad_row = sb("pad_row", [P, 2, 2], F32)
        pad_idx = sb("pad_idx", [P, 3], I32)
        tiles_i = sb("tiles_i", [P, E], I32)
        tiles_f = sb("tiles_f", [P, E], F32)
        cum_f = sb("cum_f", [P, E], F32)
        done_e = sb("done_e", [P, 2, E], F32)
        sched = sb("sched", [P, 8], F32)
        slot_table = sb("slot_table", [1, 2, P], I32)
        y_idx = sb("y_idx", [P, 8], I32)
        adj_f = adj_sb[:, :, :].bitcast(F32).rearrange("p a n -> p (a n)")
        x_rows = adj_f[:, 0:8 * ROW].rearrange("p (b n) -> p b n", b=8)
        y_sb = adj_f[:, 2048:2048 + 4 * D].rearrange("p (b n) -> p b n", b=4)
        act_sb = adj_f[:, 3072:3072 + 2 * H].rearrange("p (b n) -> p b n", b=2)
        hid_sb = adj_f[:, 4096:4096 + 2 * H].rearrange("p (b n) -> p b n", b=2)
        mask_flat = mask[:, :, :].rearrange("p a n -> p (a n)")
        xt_sb = mask_flat[:, 0:2 * CH].rearrange("p (b n) -> p b n", b=2)
        ht_hi = mask_flat[:, 1024:1024 + 2 * H].rearrange("p (b n) -> p b n", b=2)
        ht_lo = mask_flat[:, 2048:2048 + 2 * H].rearrange("p (b n) -> p b n", b=2)
        ya_sb = qk_hi[:, :, :, :].rearrange("p g a n -> p (g a n)").bitcast(F32)
        yb_sb = qk_lo[:, :, :, :].rearrange("p g a n -> p (g a n)").bitcast(F32)

        bank = [ctx.enter_context(nc.psum_tensor(f"bank{i}", [P, 512], F32)) for i in range(4)]
        o_ps = ctx.enter_context(nc.psum_tensor("o_ps", [P, 2, 512], F32))
        misc = [ctx.enter_context(nc.psum_tensor(f"misc{i}", [P, 512], F32)) for i in range(2)]

        x_in = [sem(f"x_in{i}") for i in range(len(PARTS) - 1)]
        w_in, gate_in = sem("w_in"), sem("gate_in")
        adj_in = [sem(f"adj_in{s}") for s in range(len(SEGS) - 1)]
        w_raw_in, w_split = sem("w_raw_in"), sem("w_split")
        waited = sem("waited")
        x_padded, adj_padded, const_steps, consts = sem("x_padded"), sem("adj_padded"), sem("const_steps"), sem("consts")
        stats_done, aggr_done, var_done, rstd_done = sem("stats_done"), sem("aggr_done"), sem("var_done"), sem("rstd_done")
        id_ready = sem("id_ready")
        f_done, f_hi_done, f_lo_done = sem("f_done"), sem("f_hi_done"), sem("f_lo_done")
        wt_ps, wt_done = sem("wt_ps"), sem("wt_done")
        ft_ps, ft_copied, proj_ps, squared = sem("ft_ps"), sem("ft_copied"), sem("proj_ps"), sem("squared")
        ss_summed, ss_clamped, rnorm_done = sem("ss_summed"), sem("ss_clamped"), sem("rnorm_done")
        qn_scaled, qt_ps, q_hi_done, q_lo_done = sem("qn_scaled"), sem("qt_ps"), sem("q_hi_done"), sem("q_lo_done")
        mask0_done = sem("mask0_done")
        mask_done, s_done, p_done, p_hi_done = sem("mask_done"), sem("s_done"), sem("p_done"), sem("p_hi_done")
        p_lo_done, pv_done, o_evac = sem("p_lo_done"), sem("pv_done"), sem("o_evac")
        pool_ep, dve_ep = sem("pool_ep"), sem("dve_ep")
        weights_ready, x2_ready, var2_ready, rstd2_ready = sem("weights_ready"), sem("x2_ready"), sem("var2_ready"), sem("rstd2_ready")
        f2_ready, gap_ready, one_hot_ready = sem("f2_ready"), sem("gap_ready"), sem("one_hot_ready")
        tails_ready, parts_ready, places_ready = sem("tails_ready"), sem("parts_ready"), sem("places_ready")
        f2t_ps, f2t_done, logits_ps, gate_exp, rank_ps = sem("f2t_ps"), sem("f2t_done"), sem("logits_ps"), sem("gate_exp"), sem("rank_ps")
        rows_stored, pad_stored = sem("rows_stored"), sem("pad_stored")
        sched_steps, slots_ready, slots_ps, sched_done, pads_ready = sem("sched_steps"), sem("slots_ready"), sem("slots_ps"), sem("sched_done"), sem("pads_ready")
        x_rows_in = [sem(f"x_rows_in{b}") for b in range(8)]
        idx_done = sem("idx_done")
        xt_ps, xt_done, h_ps, act_done, hid_done = sem("xt_ps"), sem("xt_done"), sem("h_ps"), sem("act_done"), sem("hid_done")
        ht_ps, ht_hi_done, ht_lo_done, y_ps, y_done = sem("ht_ps"), sem("ht_hi_done"), sem("ht_lo_done"), sem("y_ps"), sem("y_done")
        y_stored = [sem(f"y_stored{b}") for b in range(4)]
        ya_in = [sem(f"ya_in{i}") for i in range(5)]
        yb_in = [sem(f"yb_in{i}") for i in range(5)]
        CUTS = [0, 5, 10, 15, 20, T]
        sum_a, sum_done, out_stored = sem("sum_a"), sem("sum_done"), sem("out_stored")

        POOL_EP = 4
        DVE_EP = 22

        def wait_alone(eng, what, value):
            eng.wait_ge(what, value)
            if not isinstance(value, int):
                eng.sem_inc(waited, 1)

        block = ctx.enter_context(nc.Block())

        @block.sync
        def _(sp):
            for i in range(len(PARTS) - 1):
                a, b = PARTS[i], min(PARTS[i + 1], T - 1)
                sp.dma_start(x_sb[:, a * D:b * D].rearrange("p (t d) -> p t d", d=D),
                             x[a * P:b * P, :].rearrange("(t p) d -> p t d", p=P)).then_inc(x_in[i], 16)
                if i == 0:
                    sp.dma_start(wqk[:, 0, :], Wq[:, :]).then_inc(w_in, 16)
                    sp.dma_start(wqk[:, 1, :], Wk[:, :]).then_inc(w_in, 16)
            sp.wait_ge(x_padded, 1)
            for a, b in ((0, LAST16), (LAST16, LAST)):
                sp.dma_start(x_sb[a:b, (T - 1) * D:], x[(T - 1) * P + a:(T - 1) * P + b, :]).then_inc(x_in[-1], 16)
            sp.dma_start(gate_sb[:, :], gate_w[:, :]).then_inc(gate_in, 16)
            sp.dma_start(gate_bias[:, :], gate_b.rearrange("(a e) -> a e", a=1)).then_inc(gate_in, 16)

            def load_adj(c, last=False):
                for s in range(len(SEGS) - 1):
                    a, b = SEGS[s] * CH, min(SEGS[s + 1] * CH, N)
                    if isinstance(c, int) and c == 1:
                        sp.wait_ge(mask0_done, SEGS[s + 1])
                    elif at_least(c, 2):
                        wait_alone(sp, mask_done, (c - 2) * G + SEGS[s + 1])
                    if last:
                        r = c * CH
                        sp.dma_start(adj_sb[:, 0, a:b], adj[r:r + P, a:b]).then_inc(adj_in[s], 16)
                        sp.dma_start(adj_sb[0:LAST16, 1, a:b], adj[r + P:r + P + LAST16, a:b]).then_inc(adj_in[s], 16)
                        sp.dma_start(adj_sb[LAST16:LAST, 1, a:b], adj[r + P + LAST16:N, a:b]).then_inc(adj_in[s], 16)
                    else:
                        sp.dma_start(adj_sb[:, :, a:b],
                                     adj[bass.ds(c * CH, CH), a:b].rearrange("(i p) n -> p i n", p=P)).then_inc(adj_in[s], 16)

            sp.wait_ge(adj_padded, 1)
            load_adj(0)
            load_adj(1)
            with sp.Fori(2, G - 1) as c:
                load_adj(c)
            load_adj(G - 1, last=True)
            sp.wait_ge(rows_stored, 16 * 4 * G)
            sp.wait_ge(pad_stored, 16 * 4)
            sp.wait_ge(sched_done, 1)

            def load_rows(t, b):
                if at_least(t, 8):
                    wait_alone(sp, y_done, t - 7)
                at = sp.value_load(slot_table[0:1, 0, bass.ds(t, 1)], min_val=0, max_val=(E + 1) * REGION - P)
                sp.dma_start(x_rows[:, b, :], routed[bass.ds(at, P), :]).then_inc(x_rows_in[b], 16)

            spread(sp, load_rows, SLOTS, 8, 8, 0)
            for b in range(4):
                sp.wait_ge(y_stored[b], 16 * len(range(b, SLOTS, 4)))
            for i in range(5):
                a, b = CUTS[i], CUTS[i + 1]
                sp.dma_start(ya_sb[:, a * D:b * D].rearrange("p (t d) -> p t d", d=D),
                             expert_out[a * P:b * P, :].rearrange("(t p) d -> p t d", p=P)).then_inc(ya_in[i], 16)
            for i in range(5):
                a, b = CUTS[i], min(CUTS[i + 1], T - 1)
                sp.wait_ge(sum_done, i + 1)
                sp.dma_start(out[a * P:b * P, :].rearrange("(t p) d -> p t d", p=P),
                             x_sb[:, a * D:b * D].rearrange("p (t d) -> p t d", d=D)).then_inc(out_stored, 16)
            for a, b in ((0, LAST16), (LAST16, LAST)):
                sp.dma_start(out[(T - 1) * P + a:(T - 1) * P + b, :], x_sb[a:b, (T - 1) * D:]).then_inc(out_stored, 16)
            sp.wait_ge(out_stored, 16 * 7)

        def mix_output(c, ns, ep):
            xc = x_sb[:, bass.ds(c * CH, CH)].rearrange("p (a d) -> p a d", a=2)
            fc = f_sb[:, bass.ds(c * CH, CH)].rearrange("p (a d) -> p a d", a=2)
            wide = [P, 2, D]
            ep(ns.tensor_tensor(mix[:, :, :], mix[:, :, :], small[:, 3, :].unsqueeze(2).to_broadcast(wide), ALU.mult))
            ep(ns.tensor_tensor(keep[:, :, :], fc, small[:, 4, :].unsqueeze(2).to_broadcast(wide), ALU.mult))
            ep(ns.tensor_tensor(mix[:, :, :], mix[:, :, :], keep[:, :, :], ALU.add))
            ns.tensor_tensor(xc, xc, mix[:, :, :], ALU.add).then_inc(x2_ready, 1)

        rows_hi = rows[:, :, 0:D // 2].bitcast(F16).rearrange("p (a k) d -> p a k d", a=2)
        rows_lo = rows[:, :, D // 2:D].bitcast(F16).rearrange("p (a k) d -> p a k d", a=2)
        f2_twice = f2[:, :, :].unsqueeze(2).to_broadcast([P, 2, 2, D])

        @block.gpsimd
        def _(pool):
            n = [0]

            def step(ins):
                n[0] += 1
                ins.then_inc(const_steps, 1)
                pool.wait_ge(const_steps, n[0])

            nc.gpsimd.memset(x_sb[:, (T - 1) * D:], 0.0).then_inc(x_padded, 1)
            nc.gpsimd.memset(adj_sb[:, :, N:NP], 0).then_inc(adj_padded, 1)
            step(nc.gpsimd.memset(neg_half[:, :], -0.5))
            step(nc.gpsimd.memset(id32[:, :], 0.0))
            nc.gpsimd.affine_select(out=id32[:, :], in_=id32[:, :], compare_op=ALU.not_equal, fill=1.0,
                                    base=0, pattern=[[-1, P]], channel_multiplier=1).then_inc(id_ready, 1)
            step(nc.gpsimd.memset(f_aug[:, :, D:D + 1], 1.0))
            step(nc.gpsimd.memset(ones16[:, :], 1.0))
            step(nc.gpsimd.memset(one_row[:, :], 1.0))
            step(nc.gpsimd.affine_select(out=before16[:, :], in_=ones16[:, :], compare_op=ALU.is_gt, fill=0.0,
                                         base=0, pattern=[[1, P]], channel_multiplier=-1))
            pool.wait_ge(id_ready, 1)
            step(nc.gpsimd.tensor_copy(id16[:, :], id32[:, :]))
            step(nc.gpsimd.iota(expert_i[:, :], pattern=[[1, E]], base=0, channel_multiplier=0))
            step(nc.gpsimd.tensor_copy(expert_f[:, :], expert_i[:, :]))
            step(nc.gpsimd.tensor_scalar(start_f[:, :], expert_f[:, :], float(REGION), 0.0, ALU.mult, ALU.add))
            step(nc.gpsimd.tensor_copy(next_row[:, :], start_f[:, :]))
            step(nc.gpsimd.iota(dest_i[:, :, :], pattern=[[P, 2], [NP, 2]], base=0, channel_multiplier=1))
            nc.gpsimd.tensor_copy(dest_f[:, :, :], dest_i[:, :, :]).then_inc(consts, 1)

            def rstd_part(i):
                pool.wait_ge(var_done, i + 1)
                at = slice(PARTS[i], PARTS[i + 1])
                nc.gpsimd.tensor_tensor(rstd[:, at], var_eps[:, at], neg_half[:, at], ALU.pow).then_inc(rstd_done, 1)

            for i in range(len(PARTS) - 1):
                rstd_part(i)

            def norms(g, b):
                pool.wait_ge(ss_clamped, g + 1)
                if at_least(g, 2):
                    pool.wait_ge(qn_scaled, g - 1)
                nc.gpsimd.tensor_tensor(rnorm[:, b, :], ss_max[:, b, :], neg_half[:, 0:4], ALU.pow).then_inc(rnorm_done, 1)
                pool.wait_ge(f_hi_done, part_of(g))
                two = f_aug[:, bass.ds(2 * g, 2), :]
                nc.gpsimd.tensor_tensor(two[:, :, D + 1:2 * D + 1], f_sb[:, bass.ds(g * CH, CH)].rearrange("p (a d) -> p a d", a=2),
                                        two[:, :, 0:D], ALU.subtract).then_inc(f_lo_done, 1)

            def part_of(g):
                if not isinstance(g, int):
                    return len(PARTS) - 1
                return next(i for i in range(1, len(PARTS)) if 2 * g + 2 <= PARTS[i])

            spread(pool, norms, G, 2, 4, 1)

            step(nc.gpsimd.memset(pad_rows[:, :, :], 0.0))
            step(nc.gpsimd.memset(pad_rows[:, :, D + 1:D + 2].bitcast(I32), NO_ROW))
            step(nc.gpsimd.memset(tri_e[:, :, :], 1.0))
            step(nc.gpsimd.affine_select(out=tri_e[:, :, :], in_=tri_e[:, :, :], compare_op=ALU.is_ge, fill=0.0,
                                         base=0, pattern=[[1, E], [-1, E]], channel_multiplier=0))
            step(nc.gpsimd.iota(part_i[:, 0:1], pattern=[[0, 1]], base=0, channel_multiplier=1))
            step(nc.gpsimd.tensor_copy(part_f[:, :], part_i[:, 0:1]))
            per = P // E
            step(nc.gpsimd.memset(pad_e[:, :], 1.0))
            step(nc.gpsimd.affine_select(out=pad_e[:, :], in_=pad_e[:, :], compare_op=ALU.is_ge, fill=0.0,
                                         base=0, pattern=[[-per, E]], channel_multiplier=1))
            step(nc.gpsimd.affine_select(out=pad_e[:, :], in_=pad_e[:, :], compare_op=ALU.is_ge, fill=0.0,
                                         base=per - 1, pattern=[[per, E]], channel_multiplier=-1))
            step(nc.gpsimd.tensor_tensor(pad_pick[:, 0, :], pad_e[:, :], expert_f[:, :], ALU.mult))
            nc.gpsimd.tensor_scalar(pad_pick[:, 1, :], pad_pick[:, 0, :], float(-per), 0.0, ALU.mult, ALU.add).then_inc(consts, 1)
            pool.dma_start(routed[E * REGION:E * REGION + P, :], pad_rows[:, 0, :]).then_inc(pad_stored, 16)

            def epilogue(c, weight=None):
                k = [0]

                def ep(ins):
                    k[0] += 1
                    ins.then_inc(pool_ep, 1)
                    pool.wait_ge(pool_ep, c * POOL_EP + k[0])

                if weight:
                    kind, e, n_w = weight
                    if kind < 2:
                        dst = [t[:, bass.ds(e, 4), kind * H:(kind + 1) * H] for t in (w12_hi, w12_lo)]
                        pool.dma_start(w_raw[:, :, :], (w1, w2)[kind][bass.ds(e, 4)].rearrange("e d h -> d e h")).then_inc(w_raw_in, 16)
                    else:
                        dst = [t[:, bass.ds(e, 4), :] for t in (w3_hi, w3_lo)]
                        pool.dma_start(w_raw[:, :, :].rearrange("p e (c o) -> p e c o", c=2),
                                       w3[bass.ds(e, 4)].rearrange("e (c p) o -> p e c o", p=P)).then_inc(w_raw_in, 16)
                pool.wait_ge(o_evac, c + 1)
                ep(nc.gpsimd.tensor_tensor(mix[:, :, :], o_sb[:, :, 0:D], o_sb[:, :, D + 1:2 * D + 1], ALU.add))
                pool.wait_ge(weights_ready, c + 1)
                mix_output(c, nc.gpsimd, ep)
                assert k[0] == POOL_EP
                pool.wait_ge(var2_ready, c + 1)
                nc.gpsimd.tensor_tensor(small[:, 6, :], small[:, 5, :], neg_half[:, 0:2], ALU.pow).then_inc(rstd2_ready, 1)
                wait_alone(pool, f2_ready, c + 1)
                nc.gpsimd.tensor_copy(rows_hi, f2_twice).then_inc(parts_ready, 1)
                pool.wait_ge(parts_ready, c * 2 + 1)
                nc.gpsimd.tensor_tensor(rows_lo, f2_twice, rows_hi, ALU.subtract).then_inc(parts_ready, 1)
                if weight:
                    wait_alone(pool, w_raw_in, 16 * (n_w + 1))
                    nc.gpsimd.tensor_copy(dst[0], w_raw[:, :, :]).then_inc(w_split, 1)
                    pool.wait_ge(w_split, 2 * n_w + 1)
                    nc.gpsimd.tensor_tensor(dst[1], w_raw[:, :, :], dst[0], ALU.subtract).then_inc(w_split, 1)
                    pool.wait_ge(w_split, 2 * n_w + 2)
                scatter_rows(c)

            def scatter_rows(c):
                wait_alone(pool, parts_ready, c * 2 + 2)
                wait_alone(pool, tails_ready, c + 1)
                wait_alone(pool, places_ready, c + 1)
                for j in range(4):
                    pool.indirect_dma_start(out=routed[:, :], out_offset=bass.IndirectOffsetOnAxis(ap=row_i[:, j:j + 1], axis=0),
                                            in_=rows[:, j, :], in_offset=None).then_inc(rows_stored, 16)
                wait_alone(pool, rows_stored, 64 * (c + 1))

            assert G - 1 == 3 * (E // 4)
            with pool.Fori(0, E // 4) as lot:
                for kind in range(3):
                    epilogue(lot * 3 + kind, (kind, lot * 4, lot * 3 + kind))
            c = G - 1
            pool.wait_ge(var2_ready, c + 1)
            nc.gpsimd.tensor_tensor(small[:, 6, :], small[:, 5, :], neg_half[:, 0:2], ALU.pow).then_inc(rstd2_ready, 1)
            scatter_rows(c)
            pool.wait_ge(pads_ready, 1)
            pool.indirect_dma_start(out=routed[:, :].rearrange("(b r) n -> b (r n)", r=BLOCK),
                                    out_offset=bass.IndirectOffsetOnAxis(ap=pad_idx[:, 2:3], axis=0),
                                    in_=pad_rows[:, :, :].rearrange("p r n -> p (r n)"), in_offset=None).then_inc(pad_stored, 16)
            for j in range(2):
                pool.indirect_dma_start(out=routed[:, :], out_offset=bass.IndirectOffsetOnAxis(ap=pad_idx[:, j:j + 1], axis=0),
                                        in_=pad_rows[:, 0, :], in_offset=None,
                                        bounds_check=(E + 1) * REGION - 1, oob_is_err=False).then_inc(pad_stored, 16)

            def store_rows(t, b):
                wait_alone(pool, idx_done, t + 1)
                wait_alone(pool, y_done, t + 1)
                pool.indirect_dma_start(out=expert_out[:, :],
                                        out_offset=bass.IndirectOffsetOnAxis(ap=y_idx[:, b:b + 1], axis=0),
                                        in_=y_sb[:, b % 4, :], in_offset=None,
                                        bounds_check=2 * NP - 1, oob_is_err=False).then_inc(y_stored[b % 4], 16)

            spread(pool, store_rows, SLOTS, 8, 0, 0)

        @block.tensor
        def _(pe):
            pe.wait_ge(id_ready, 1)
            pe.wait_ge(w_in, 32)
            for k in range(2):
                last = nc.tensor.transpose(misc[0][:, k * P:(k + 1) * P], wqk[:, k, :], id32[:, :])
            last.then_inc(wt_ps, 1)
            pe.wait_ge(wt_done, 1)

            def project(i, b):
                o = 1 - b
                if i < G:
                    pe.wait_ge(f_done, 2 * i + 2)
                    if i >= 2:
                        pe.wait_ge(ft_copied, i - 1)
                    for k in range(2):
                        last = nc.tensor.transpose(misc[b][:, k * P:(k + 1) * P],
                                                   f_sb[:, (2 * i + k) * D:(2 * i + k + 1) * D], id32[:, :])
                    last.then_inc(ft_ps, 1)
                if 1 <= i < G + 1:
                    g = i - 1
                    pe.wait_ge(ft_copied, g + 1)
                    if g >= 2:
                        pe.wait_ge(qn_scaled, g - 1)
                    for k in range(2):
                        last = nc.tensor.matmul(bank[o][:, k * CH:(k + 1) * CH], ft_sb[:, o, k * P:(k + 1) * P],
                                                wqk_t[:, :], start=True, stop=True)
                    last.then_inc(proj_ps, 1)
                if i >= 3:
                    g = i - 3
                    pe.wait_ge(qn_scaled, g + 1)
                    if g >= 2:
                        pe.wait_ge(q_lo_done, g - 1)
                    for a in range(2):
                        for k in range(2):
                            last = nc.tensor.transpose(bank[2 + o][:, (2 * k + a) * P:(2 * k + a + 1) * P],
                                                       qn_sb[:, o, (2 * a + k) * P:(2 * a + k + 1) * P], id32[:, :])
                    last.then_inc(qt_ps, 1)

            for i in range(G + 3):
                project(i, i % 2)
            pe.wait_ge(gate_in, 32)
            pe.wait_ge(consts, 1)

            def scores(c, u):
                if isinstance(c, int) and c == 0:
                    pe.wait_ge(q_lo_done, G)
                    if u == 0:
                        pe.wait_ge(q_hi_done, G)
                    pe.wait_ge(mask0_done, u + 1)
                else:
                    pe.wait_ge(mask_done, (c - 1) * G + u + 1)
                s = bank[BUF[u]]
                k_hi = qk_hi[:, bass.ds(c, 1), 1, :]
                k_lo = qk_lo[:, bass.ds(c, 1), 1, :]
                for j in range(2):
                    to = s[:, j * CH:(j + 1) * CH]
                    q_hi = qk_hi[:, u, 0, j * P:(j + 1) * P]
                    q_lo = qk_lo[:, u, 0, j * P:(j + 1) * P]
                    nc.tensor.matmul(to, q_hi, k_hi, start=True, stop=False)
                    nc.tensor.matmul(to, q_hi, k_lo, start=False, stop=False)
                    nc.tensor.matmul(to, q_lo, k_hi, start=False, stop=False)
                    for a in range(2):
                        key = (2 * u + j) * P
                        last = nc.tensor.matmul(s[:, j * CH + a * P:j * CH + (a + 1) * P], mask[:, a, key:key + P],
                                                id16[:, :], start=False, stop=(a == 1))
                last.then_inc(s_done, 1)

            def values(c, u):
                if u == 0 and at_least(c, 1):
                    pe.wait_ge(o_evac, c)
                pe.wait_ge(p_lo_done, c * G + u + 1)
                b = BUF[u]
                for a in range(2):
                    for j in range(2):
                        at = slice(j * CH + a * P, j * CH + (a + 1) * P)
                        first, final = u == 0 and j == 0, u == G - 1 and j == 1
                        f = f_aug[:, 2 * u + j, :]
                        nc.tensor.matmul(o_ps[:, a, 0:2 * D + 1], p_hi[:, b, at], f[:, 0:2 * D + 1], start=first, stop=False)
                        last = nc.tensor.matmul(o_ps[:, a, 0:D + 1], p_lo[:, b, at], f[:, 0:D + 1], start=False, stop=final)
                last.then_inc(pv_done, 1)

            def transpose_f2(c):
                pe.wait_ge(f2_ready, c + 1)
                for a in range(2):
                    last = nc.tensor.transpose(misc[0][:, a * P:(a + 1) * P], f2[:, a, :], id32[:, :])
                last.then_inc(f2t_ps, 1)

            def gate_logits(c):
                pe.wait_ge(f2t_done, c + 1)
                for a in range(2):
                    to = misc[1][:, a * E:(a + 1) * E]
                    nc.tensor.matmul(to, f2_t[:, a * P:(a + 1) * P], gate_sb[:, :], start=True, stop=False)
                    last = nc.tensor.matmul(to, one_row[:, :], gate_bias[:, :], start=False, stop=True)
                last.then_inc(logits_ps, 1)

            def ranks(c):
                pe.wait_ge(one_hot_ready, c + 1)
                r = misc[1][:, 64:64 + 3 * E]
                oh = [one_hot_sum[:, a, :] for a in range(2)]
                nc.tensor.matmul(r[:, 0:E], before16[:, :], oh[0], start=True, stop=True)
                nc.tensor.matmul(r[:, E:2 * E], before16[:, :], oh[1], start=True, stop=False)
                nc.tensor.matmul(r[:, E:2 * E], ones16[:, :], oh[0], start=False, stop=True)
                nc.tensor.matmul(r[:, 2 * E:3 * E], ones16[:, :], oh[0], start=True, stop=False)
                nc.tensor.matmul(r[:, 2 * E:3 * E], ones16[:, :], oh[1], start=False, stop=True).then_inc(rank_ps, 1)

            def chunk(c, last=False):
                for u in range(G):
                    if u + 2 < G:
                        scores(c, u + 2)
                    elif not last:
                        scores(c + 1, u + 2 - G)
                    values(c, u)
                    if at_least(c, 1):
                        if u == 7:
                            transpose_f2(c - 1)
                        if u == 8:
                            gate_logits(c - 1)
                        if u == 11:
                            ranks(c - 1)

            pe.wait_ge(f_hi_done, len(PARTS) - 1)
            pe.wait_ge(f_lo_done, G)
            scores(0, 0)
            scores(0, 1)
            chunk(0)
            with pe.Fori(1, G - 1) as c:
                chunk(c)
            chunk(G - 1, last=True)
            transpose_f2(G - 1)
            gate_logits(G - 1)
            ranks(G - 1)

            pe.wait_ge(slots_ready, 1)
            for k in range(2):
                last = nc.tensor.transpose(misc[0][0:1, k * P:(k + 1) * P], sched[:, 6 + k:7 + k], id32[:, :])
            last.then_inc(slots_ps, 1)

            pe.wait_ge(sched_done, 1)
            pe.wait_ge(w_split, 2 * 3 * (E // 4))

            def expert(i, k8):
                b = k8 % 2
                if at_least(i, 1) and before(i, SLOTS + 1):
                    e_in = pe.value_load(slot_table[0:1, 1, bass.ds(i - 1, 1)], min_val=0, max_val=E - 1)
                if at_least(i, 3):
                    e_out = pe.value_load(slot_table[0:1, 1, bass.ds(i - 3, 1)], min_val=0, max_val=E - 1)
                if before(i, SLOTS):
                    pe.wait_ge(x_rows_in[k8], 2 * (i - k8) + 16)
                    if at_least(i, 2):
                        pe.wait_ge(xt_done, i - 1)
                    half = misc[b][:, 0:P].bitcast(F16)
                    for k in range(2):
                        last = nc.tensor.transpose(half[:, k * P:(k + 1) * P],
                                                   x_rows[:, k8, k * D // 2:(k + 1) * D // 2].bitcast(F16), id16[:, :])
                    last.then_inc(xt_ps, 1)
                if at_least(i, 1) and before(i, SLOTS + 1):
                    t, o = i - 1, 1 - b
                    pe.wait_ge(xt_done, t + 1)
                    if at_least(i, 3):
                        pe.wait_ge(hid_done, t - 1)
                    nc.tensor.matmul(bank[o][:, :], xt_sb[:, o, 0:P], w12_hi[:, bass.ds(e_in, 1), :], start=True, stop=False)
                    nc.tensor.matmul(bank[o][:, :], xt_sb[:, o, P:2 * P], w12_hi[:, bass.ds(e_in, 1), :], start=False, stop=False)
                    nc.tensor.matmul(bank[o][:, :], xt_sb[:, o, 0:P], w12_lo[:, bass.ds(e_in, 1), :], start=False, stop=True).then_inc(h_ps, 1)
                if at_least(i, 2) and before(i, SLOTS + 2):
                    t = i - 2
                    pe.wait_ge(hid_done, t + 1)
                    if at_least(i, 4):
                        pe.wait_ge(ht_lo_done, t - 1)
                    for k in range(2):
                        last = nc.tensor.transpose(bank[2 + b][:, k * P:(k + 1) * P], hid_sb[:, b, k * P:(k + 1) * P], id32[:, :])
                    last.then_inc(ht_ps, 1)
                if at_least(i, 3):
                    t, o = i - 3, 1 - b
                    pe.wait_ge(ht_lo_done, t + 1)
                    if at_least(i, 5):
                        pe.wait_ge(y_done, t - 1)
                    for k in range(2):
                        hh, hl = ht_hi[:, o, k * P:(k + 1) * P], ht_lo[:, o, k * P:(k + 1) * P]
                        wh = w3_hi[:, bass.ds(e_out, 1), k * D:(k + 1) * D]
                        wl = w3_lo[:, bass.ds(e_out, 1), k * D:(k + 1) * D]
                        nc.tensor.matmul(o_ps[:, o, 0:D], hh, wh, start=(k == 0), stop=False)
                        nc.tensor.matmul(o_ps[:, o, 0:D], hl, wh, start=False, stop=False)
                        last = nc.tensor.matmul(o_ps[:, o, 0:D], hh, wl, start=False, stop=(k == 1))
                    last.then_inc(y_ps, 1)

            spread(pe, expert, SLOTS + 3, 8, 8, 3)

        @block.scalar
        def _(act):
            act.wait_ge(wt_ps, 1)
            nc.scalar.copy(wqk_t[:, :], misc[0][:, 0:CH]).then_inc(wt_done, 1)
            def f_high(i):
                at = slice(PARTS[i], PARTS[i + 1])
                act.wait_ge(f_done, PARTS[i + 1])
                nc.scalar.copy(f_aug[:, at, 0:D], f_sb[:, at.start * D:at.stop * D].rearrange("p (t d) -> p t d", d=D)).then_inc(f_hi_done, 1)

            def project(i, b):
                o = 1 - b
                if before(i, G):
                    act.wait_ge(ft_ps, i + 1)
                    if at_least(i, 2):
                        act.wait_ge(proj_ps, i - 1)
                    nc.scalar.copy(ft_sb[:, b, :], misc[b][:, 0:CH]).then_inc(ft_copied, 1)
                if at_least(i, 1) and before(i, G + 1):
                    act.wait_ge(proj_ps, i)
                    if at_least(i, 2):
                        act.wait_ge(ss_summed, i - 1)
                    nc.scalar.activation(sq_sb, bank[o][:, :], ACT.Square).then_inc(squared, 1)
                if at_least(i, 3):
                    act.wait_ge(qt_ps, i - 2)
                    nc.scalar.copy(qk_hi[:, bass.ds(i - 3, 1), :, :],
                                   bank[2 + o][:, :].rearrange("p (o a n) -> p o a n", o=1, a=2)).then_inc(q_hi_done, 1)

            f_high(0)
            project(0, 0)
            f_high(1)
            for i in range(1, 4):
                project(i, i % 2)
            f_high(2)
            with act.Fori(2, G // 2) as turn:
                for k in range(2):
                    project(turn * 2 + k, k)
            for i in range(G - G % 2, G + 3):
                project(i, i % 2)

            def probabilities(c, u):
                act.wait_ge(s_done, c * G + u + 1)
                if u < 3 and at_least(c, 1):
                    act.wait_ge(pv_done, c * G + u - 3)
                elif 3 <= u < G - 1:
                    act.wait_ge(pv_done, c * G + u - 2)
                elif u == G - 1 and at_least(c, 1):
                    act.wait_ge(pv_done, c * G)
                if isinstance(c, int) and c == 0 and u < 3:
                    act.wait_ge(q_lo_done, G)
                b = BUF[u]
                nc.scalar.activation(p_full[:, b, :], bank[b][:, :], ACT.Exp).then_inc(p_done, 1)
                nc.scalar.activation(p_hi[:, b, :], bank[b][:, :], ACT.Exp).then_inc(p_hi_done, 1)

            def evacuate(c):
                act.wait_ge(pv_done, (c + 1) * G)
                nc.scalar.copy(o_sb[:, :, :], o_ps[:, :, 0:2 * D + 1]).then_inc(o_evac, 1)

            def copy_f2t(c):
                act.wait_ge(f2t_ps, c + 1)
                nc.scalar.copy(f2_t[:, :], misc[0][:, 0:CH]).then_inc(f2t_done, 1)

            def exp_gate(c):
                act.wait_ge(gap_ready, c + 1)
                nc.scalar.activation(small[:, 8, :], small[:, 7, :], ACT.Exp).then_inc(gate_exp, 1)

            def chunk(c):
                for u in range(G):
                    probabilities(c, u)
                    if at_least(c, 1):
                        if u == 1:
                            evacuate(c - 1)
                        if u == 8:
                            copy_f2t(c - 1)
                        if u == 11:
                            exp_gate(c - 1)

            chunk(0)
            with act.Fori(1, G) as c:
                chunk(c)
            evacuate(G - 1)
            copy_f2t(G - 1)
            exp_gate(G - 1)

            def expert(i, k8):
                b = k8 % 2
                if before(i, SLOTS):
                    act.wait_ge(h_ps, i + 1)
                    if at_least(i, 2):
                        act.wait_ge(hid_done, i - 1)
                    nc.scalar.activation(act_sb[:, b, :], bank[b][:, 0:H], ACT.Silu).then_inc(act_done, 1)
                if at_least(i, 1) and before(i, SLOTS + 1):
                    o = 1 - b
                    act.wait_ge(ht_ps, i)
                    if at_least(i, 3):
                        act.wait_ge(y_ps, i - 2)
                    nc.scalar.copy(ht_hi[:, o, :], bank[2 + o][:, 0:H]).then_inc(ht_hi_done, 1)
                if at_least(i, 2):
                    t, b8 = i - 2, (k8 - 2) % 8
                    b4 = b8 % 4
                    act.wait_ge(y_ps, t + 1)
                    if at_least(i, 6):
                        act.wait_ge(y_stored[b4], 4 * (t - b4))
                    nc.scalar.mul(y_sb[:, b4, :], o_ps[:, b, 0:D], x_rows[:, b8, D:D + 1]).then_inc(y_done, 1)

            spread(act, expert, SLOTS + 2, 8, 8, 2)
            for b in range(4):
                act.wait_ge(y_stored[b], 16 * len(range(b, SLOTS, 4)))
            for i in range(5):
                a, b = CUTS[i], CUTS[i + 1]
                act.dma_start(yb_sb[:, a * D:b * D].rearrange("p (t d) -> p t d", d=D),
                              expert_out[NP + a * P:NP + b * P, :].rearrange("(t p) d -> p t d", p=P)).then_inc(yb_in[i], 16)

        @block.vector
        def _(dve):
            def statistics(i):
                dve.wait_ge(x_in[i], 48 if i == len(PARTS) - 2 else 16)
                for t in range(PARTS[i], PARTS[i + 1]):
                    nc.vector.bn_stats(stats[:, t, :], x_sb[:, t * D:(t + 1) * D]).then_inc(stats_done, 1)
                for t in range(PARTS[i], PARTS[i + 1]):
                    dve.wait_ge(stats_done, t + 1)
                    nc.vector.bn_aggr(mean_var[:, t, :], stats[:, t, :]).then_inc(aggr_done, 1)
                dve.wait_ge(aggr_done, PARTS[i + 1])
                at = slice(PARTS[i], PARTS[i + 1])
                nc.vector.tensor_scalar(var_eps[:, at], mean_var[:, at, 1], LN_EPS, None, ALU.add).then_inc(var_done, 1)

            def normalise(i):
                dve.wait_ge(rstd_done, i + 1)
                for t in range(PARTS[i], PARTS[i + 1]):
                    nc.vector.tensor_scalar(f_sb[:, t * D:(t + 1) * D], x_sb[:, t * D:(t + 1) * D], mean_var[:, t, 0:1],
                                            rstd[:, t:t + 1], ALU.subtract, ALU.mult).then_inc(f_done, 1)

            def q_low(g, b):
                dve.wait_ge(q_hi_done, g + 1)
                nc.vector.tensor_tensor(qk_lo[:, bass.ds(g, 1), :, :], bank[2 + b][:, :].rearrange("p (o a n) -> p o a n", o=1, a=2),
                                        qk_hi[:, bass.ds(g, 1), :, :], ALU.subtract).then_inc(q_lo_done, 1)

            def project(i, b):
                o = 1 - b
                if before(i, G):
                    dve.wait_ge(squared, i + 1)
                    if at_least(i, 2):
                        dve.wait_ge(ss_clamped, i - 1)
                    nc.vector.tensor_reduce(ss[:, b, :], sq_sb.rearrange("p (a n) -> p a n", a=4),
                                            axis=AX_X, op=ALU.add).then_inc(ss_summed, 1)
                    dve.wait_ge(ss_summed, i + 1)
                    if at_least(i, 2):
                        dve.wait_ge(rnorm_done, i - 1)
                    nc.vector.tensor_scalar(ss_max[:, b, :], ss[:, b, :], COS_EPS * COS_EPS, None, ALU.max).then_inc(ss_clamped, 1)
                if at_least(i, 1) and before(i, G + 1):
                    dve.wait_ge(rnorm_done, i)
                    if at_least(i, 3):
                        dve.wait_ge(qt_ps, i - 2)
                    nc.vector.tensor_tensor(qn_sb[:, o, :].rearrange("p (a n) -> p a n", a=4),
                                            bank[o][:, :].rearrange("p (a n) -> p a n", a=4),
                                            rnorm[:, o, :].unsqueeze(2).to_broadcast([P, 4, P]), ALU.mult).then_inc(qn_scaled, 1)
                if at_least(i, 2):
                    q_low(i - 2, b)

            statistics(0)
            statistics(1)
            normalise(0)
            statistics(2)
            normalise(1)
            project(0, 0)
            project(1, 1)
            normalise(2)
            with dve.Fori(1, G // 2) as turn:
                for k in range(2):
                    project(turn * 2 + k, k)
            for i in range(G - G % 2, G + 2):
                project(i, i % 2)

            def make_mask(c, u):
                s = next(s for s in range(len(SEGS) - 1) if u < SEGS[s + 1])
                if u == SEGS[s]:
                    if isinstance(c, int) and c == G - 1:
                        dve.wait_ge(adj_in[s], 16 * (c + 3))
                    else:
                        dve.wait_ge(adj_in[s], 16 * (c + 1))
                if at_least(c, 1):
                    dve.wait_ge(s_done, (c - 1) * G + u + 1)
                at = slice(u * CH, (u + 1) * CH)
                nc.vector.tensor_scalar(mask[:, :, at], adj_sb[:, :, at], 0.0, MASKED, ALU.is_le,
                                        ALU.mult).then_inc(mask0_done if isinstance(c, int) and c == 0 else mask_done, 1)

            def low_part(c, u):
                b = BUF[u]
                dve.wait_ge(p_hi_done, c * G + u + 1)
                dve.wait_ge(p_done, c * G + u + 1)
                nc.vector.tensor_tensor(p_lo[:, b, :], p_full[:, b, :], p_hi[:, b, :], ALU.subtract).then_inc(p_lo_done, 1)

            k = [0]

            def ep(c, ins, alone=False):
                k[0] += 1
                ins.then_inc(dve_ep, 1)
                (wait_alone(dve, dve_ep, c * DVE_EP + k[0]) if alone else dve.wait_ge(dve_ep, c * DVE_EP + k[0]))

            def epilogue_weights(c):
                k[0] = 0
                dve.wait_ge(o_evac, c + 1)
                total = o_sb[:, :, D]
                ep(c, nc.vector.tensor_scalar(small[:, 0, :], total, 1e-30, None, ALU.max))
                ep(c, nc.vector.reciprocal(small[:, 1, :], small[:, 0, :]))
                ep(c, nc.vector.tensor_scalar(small[:, 2, :], total, 0.0, 0.5, ALU.is_gt, ALU.mult))
                ep(c, nc.vector.tensor_tensor(small[:, 3, :], small[:, 1, :], small[:, 2, :], ALU.mult))
                nc.vector.tensor_scalar(small[:, 4, :], small[:, 2, :], -1.0, 1.0, ALU.mult, ALU.add).then_inc(weights_ready, 1)

            def epilogue_stats(c):
                dve.wait_ge(x2_ready, c + 1)
                for a in range(2):
                    ep(c, nc.vector.bn_stats(stats2[:, a, :], x_sb[:, bass.ds(c * CH + a * D, D)]), a == 1)
                for a in range(2):
                    ep(c, nc.vector.bn_aggr(mean_var2[:, a, :], stats2[:, a, :]), a == 0)
                nc.vector.tensor_scalar(small[:, 5, :], mean_var2[:, :, 1], LN_EPS, None, ALU.add).then_inc(var2_ready, 1)

            def epilogue_norm(c):
                dve.wait_ge(rstd2_ready, c + 1)
                for a in range(2):
                    last = nc.vector.tensor_scalar(f2[:, a, :], x_sb[:, bass.ds(c * CH + a * D, D)], mean_var2[:, a, 0:1],
                                                   small[:, 6, a:a + 1], ALU.subtract, ALU.mult)
                last.then_inc(f2_ready, 1)

            def epilogue_route(c):
                dve.wait_ge(logits_ps, c + 1)
                ep(c, nc.vector.tensor_copy(logits[:, :, :], misc[1][:, 0:2 * E].rearrange("p (a e) -> p a e", a=2)), True)
                for a in range(2):
                    ep(c, nc.vector.max(top_v[:, a, :], logits[:, a, :]), a == 0)
                nc.vector.tensor_tensor(small[:, 7, :], top_v[:, :, 1], top_v[:, :, 0], ALU.subtract).then_inc(gap_ready, 1)
                for a in range(2):
                    ep(c, nc.vector.max_index(top_i[:, a, :], top_v[:, a, :], logits[:, a, :]), a == 0)
                ep(c, nc.vector.tensor_copy(top_f[:, :, :], top_i[:, :, 0:2]))
                ep(c, nc.vector.tensor_tensor(one_hot[:, :, :].rearrange("p (a k) e -> p a k e", a=2),
                                              expert_f[:, :].unsqueeze(1).unsqueeze(1).to_broadcast([P, 2, 2, E]),
                                              top_f[:, :, :].unsqueeze(3).to_broadcast([P, 2, 2, E]), ALU.is_equal))
                oh = one_hot[:, :, :].rearrange("p (a k) e -> p a k e", a=2)
                nc.vector.tensor_tensor(one_hot_sum[:, :, :], oh[:, :, 0, :], oh[:, :, 1, :], ALU.add).then_inc(one_hot_ready, 1)

            def epilogue_tails(c):
                tail = rows[:, :, :].rearrange("p (a k) n -> p a k n", a=2)
                dve.wait_ge(gate_exp, c + 1)
                ep(c, nc.vector.tensor_scalar(small[:, 9, :], small[:, 8, :], 1.0, None, ALU.add))
                ep(c, nc.vector.reciprocal(small[:, 10, :], small[:, 9, :]))
                nc.vector.tensor_copy(tail[:, :, 0, D], small[:, 10, :])
                nc.vector.tensor_tensor(tail[:, :, 1, D], small[:, 8, :], small[:, 10, :], ALU.mult)
                ep(c, nc.vector.tensor_copy(tail[:, :, :, D + 1].bitcast(I32), dest_f[:, :, :]))
                nc.vector.tensor_scalar(dest_f[:, :, :], dest_f[:, :, :], float(CH), None, ALU.add).then_inc(tails_ready, 1)

            def epilogue_places(c):
                oh = one_hot[:, :, :].rearrange("p (a k) e -> p a k e", a=2)
                dve.wait_ge(rank_ps, c + 1)
                ep(c, nc.vector.tensor_tensor(row_of[:, :, :], misc[1][:, 64:64 + 2 * E].rearrange("p (a e) -> p a e", a=2),
                                              next_row[:, :].unsqueeze(1).to_broadcast([P, 2, E]), ALU.add))
                ep(c, nc.vector.tensor_tensor(row_pick[:, :, :].rearrange("p (a k) e -> p a k e", a=2), oh,
                                              row_of[:, :, :].unsqueeze(2).to_broadcast([P, 2, 2, E]), ALU.mult))
                ep(c, nc.vector.tensor_tensor(next_row[:, :], next_row[:, :], misc[1][:, 64 + 2 * E:64 + 3 * E], ALU.add))
                ep(c, nc.vector.tensor_reduce(row_f[:, :], row_pick[:, :, :], axis=AX_X, op=ALU.add))
                nc.vector.tensor_copy(row_i[:, :], row_f[:, :]).then_inc(places_ready, 1)

            def chunk(c, last=False):
                for u in range(G):
                    if isinstance(c, int) and c == 0 and u + 3 < G:
                        make_mask(0, u + 3)
                    low_part(c, u)
                    if not last:
                        make_mask(c + 1, u)
                    if at_least(c, 1):
                        if u == 2:
                            epilogue_weights(c - 1)
                        if u == 5:
                            epilogue_stats(c - 1)
                        if u == 6:
                            epilogue_norm(c - 1)
                        if u == 9:
                            epilogue_route(c - 1)
                        if u == 11:
                            epilogue_tails(c - 1)
                        if u == 12:
                            epilogue_places(c - 1)
                            assert k[0] == DVE_EP, k[0]

            dve.wait_ge(adj_padded, 1)
            dve.wait_ge(consts, 1)
            for u in range(3):
                make_mask(0, u)
            chunk(0)
            with dve.Fori(1, G - 2) as c:
                chunk(c)
            m = [0]

            def step(ins):
                m[0] += 1
                ins.then_inc(sched_steps, 1)
                dve.wait_ge(sched_steps, m[0])

            dve.wait_ge(consts, 2)
            step(nc.vector.tensor_reduce(sched[:, 0:1], pad_pick[:, 1, :], axis=AX_X, op=ALU.add))
            step(nc.vector.tensor_tensor(pad_of[:, :], sched[:, 0:1], part_f[:, :], ALU.add))
            for j in range(2):
                step(nc.vector.tensor_scalar(pad_of2[:, j:j + 1], pad_of[:, :], 2.0, float(j), ALU.mult, ALU.add))
            chunk(G - 2)
            chunk(G - 1, last=True)
            c = G - 1
            epilogue_weights(c)
            dve.wait_ge(weights_ready, c + 1)
            step(nc.vector.tensor_tensor(mix[:, :, :], o_sb[:, :, 0:D], o_sb[:, :, D + 1:2 * D + 1], ALU.add))
            mix_output(c, nc.vector, step)
            epilogue_stats(c)
            epilogue_norm(c)
            dve.wait_ge(f2_ready, c + 1)
            nc.vector.tensor_copy(rows_hi, f2_twice).then_inc(parts_ready, 1)
            dve.wait_ge(parts_ready, c * 2 + 1)
            nc.vector.tensor_tensor(rows_lo, f2_twice, rows_hi, ALU.subtract).then_inc(parts_ready, 1)
            epilogue_route(c)
            epilogue_places(c)
            epilogue_tails(c)
            assert k[0] == DVE_EP, k[0]

            step(nc.vector.tensor_scalar(ends_i[:, :], next_row[:, :], float(BLOCK - 1), None, ALU.add))
            step(nc.vector.tensor_scalar(ends_i[:, :], ends_i[:, :], BLOCK.bit_length() - 1, None, ALU.arith_shift_right))
            step(nc.vector.tensor_copy(ends[:, 1, :], ends_i[:, :]))
            step(nc.vector.tensor_copy(ends[:, 0, :], next_row[:, :]))
            step(nc.vector.tensor_tensor(pad_pick[:, :, :], ends[:, :, :], pad_e[:, :].unsqueeze(1).to_broadcast([P, 2, E]), ALU.mult))
            step(nc.vector.tensor_reduce(pad_end[:, :], pad_pick[:, :, :], axis=AX_X, op=ALU.add))
            step(nc.vector.tensor_tensor(pad_idx[:, 2:3], pad_end[:, 1:2], pad_of[:, :], ALU.add))
            step(nc.vector.tensor_tensor(pad_row[:, 0, :], pad_of2[:, :], pad_end[:, 0:1].to_broadcast([P, 2]), ALU.add))
            step(nc.vector.tensor_scalar(sched[:, 0:1], pad_end[:, 1:2], float(BLOCK), None, ALU.mult))
            step(nc.vector.tensor_tensor(pad_row[:, 1, :], pad_row[:, 0, :], sched[:, 0:1].to_broadcast([P, 2]), ALU.is_ge))
            step(nc.vector.tensor_scalar(pad_row[:, 1, :], pad_row[:, 1, :], float(NO_ROW), None, ALU.mult))
            nc.vector.tensor_tensor(pad_idx[:, 0:2], pad_row[:, 0, :], pad_row[:, 1, :], ALU.add).then_inc(pads_ready, 1)

            step(nc.vector.tensor_tensor(cum_f[:, :], next_row[:, :], start_f[:, :], ALU.subtract))
            step(nc.vector.tensor_scalar(tiles_i[:, :], cum_f[:, :], float(P - 1), None, ALU.add))
            step(nc.vector.tensor_scalar(tiles_i[:, :], tiles_i[:, :], P.bit_length() - 1, None, ALU.arith_shift_right))
            step(nc.vector.tensor_copy(tiles_f[:, :], tiles_i[:, :]))
            step(nc.vector.tensor_tensor(grid[:, :, :], tri_e[:, :, :], tiles_f[:, :].unsqueeze(1).to_broadcast([P, E, E]), ALU.mult))
            step(nc.vector.tensor_reduce(cum_f[:, :], grid[:, :, :], axis=AX_X, op=ALU.add))
            step(nc.vector.tensor_scalar(done_e[:, 0, :], cum_f[:, :], part_f[:, 0:1], None, ALU.is_le))
            step(nc.vector.tensor_tensor(done_e[:, 1, :], done_e[:, 0, :], tiles_f[:, :], ALU.mult))
            step(nc.vector.tensor_reduce(sched[:, 0:2], done_e[:, :, :], axis=AX_X, op=ALU.add))
            step(nc.vector.tensor_tensor(sched[:, 2:3], part_f[:, :], sched[:, 1:2], ALU.subtract))
            step(nc.vector.tensor_scalar(sched[:, 3:4], sched[:, 0:1], float(E), float(P), ALU.is_lt, ALU.mult))
            step(nc.vector.tensor_tensor(sched[:, 4:5], sched[:, 2:3], sched[:, 3:4], ALU.mult))
            step(nc.vector.tensor_scalar(sched[:, 5:6], sched[:, 0:1], float(REGION), None, ALU.mult))
            step(nc.vector.tensor_tensor(sched[:, 6:7], sched[:, 5:6], sched[:, 4:5], ALU.add))
            nc.vector.tensor_scalar(sched[:, 7:8], sched[:, 0:1], float(E - 1), None, ALU.min).then_inc(slots_ready, 1)
            dve.wait_ge(slots_ps, 1)
            nc.vector.tensor_copy(slot_table[:, :, :], misc[0][0:1, 0:2 * P].rearrange("p (k t) -> p k t", k=2)).then_inc(sched_done, 1)

            def expert(i, k8):
                b = k8 % 2
                if before(i, SLOTS):
                    dve.wait_ge(xt_ps, i + 1)
                    if at_least(i, 2):
                        dve.wait_ge(h_ps, i - 1)
                    nc.vector.tensor_copy(xt_sb[:, b, :], misc[b][:, 0:P].bitcast(F16)).then_inc(xt_done, 1)
                    if at_least(i, 8):
                        dve.wait_ge(y_stored[k8 % 4], 4 * (i - k8 % 4) - 16)
                    nc.vector.tensor_copy(y_idx[:, k8:k8 + 1], x_rows[:, k8, D + 1:D + 2].bitcast(I32)).then_inc(idx_done, 1)
                if at_least(i, 1) and before(i, SLOTS + 1):
                    o = 1 - b
                    dve.wait_ge(act_done, i)
                    if at_least(i, 3):
                        dve.wait_ge(ht_ps, i - 2)
                    nc.vector.tensor_tensor(hid_sb[:, o, :], act_sb[:, o, :], bank[o][:, H:2 * H], ALU.mult).then_inc(hid_done, 1)
                if at_least(i, 2):
                    dve.wait_ge(ht_hi_done, i - 1)
                    if at_least(i, 4):
                        dve.wait_ge(y_ps, i - 3)
                    nc.vector.tensor_tensor(ht_lo[:, b, :], bank[2 + b][:, 0:H], ht_hi[:, b, :], ALU.subtract).then_inc(ht_lo_done, 1)

            spread(dve, expert, SLOTS + 2, 8, 8, 2)

            for i in range(5):
                at = slice(CUTS[i] * D, CUTS[i + 1] * D)
                dve.wait_ge(ya_in[i], 16)
                nc.vector.tensor_tensor(x_sb[:, at], x_sb[:, at], ya_sb[:, at], ALU.add).then_inc(sum_a, 1)
                dve.wait_ge(yb_in[i], 16)
                dve.wait_ge(sum_a, i + 1)
                nc.vector.tensor_tensor(x_sb[:, at], x_sb[:, at], yb_sb[:, at], ALU.add).then_inc(sum_done, 1)


_INS = ["x", "adj", "L0_gnn_Wq", "L0_gnn_Wk", "L0_ffn_gate_w", "L0_ffn_gate_b", "L0_ffn_w1", "L0_ffn_w2", "L0_ffn_w3"]


def kernel(**inputs):
    import numpy as _np
    import concourse.bacc as _bacc
    from concourse import mybir as _mybir
    from concourse.bass_utils import run_bass_kernel_spmd as _run

    nc = _bacc.Bacc("TRN2", target_bir_lowering=False, num_devices=1)
    arrays, args = {}, []
    for name in _INS:
        a = _np.ascontiguousarray(inputs[name])
        arrays[f"in_{name}_dram"] = a
        args.append(nc.dram_tensor(f"in_{name}_dram", a.shape, _mybir.dt.from_np(a.dtype), kind="ExternalInput").ap())
    result = nc.dram_tensor("out_dram", inputs["x"].shape, _mybir.dt.float32, kind="ExternalOutput").ap()
    graph_attention_moe(nc, *args, result)
    r = _run(nc, [arrays], core_ids=[0])
    return r.results[0]["out_dram"]
```

```python
from contextlib import ExitStack

import concourse.bass as bass
from concourse import mybir

F32 = mybir.dt.float32
F16 = mybir.dt.float16
I32 = mybir.dt.int32
U32 = mybir.dt.uint32
ALU = mybir.AluOpType
ACT = mybir.ActivationFunctionType
AX_X = mybir.AxisListType.X

P = 128
LN_EPS = 1e-5
COS_EPS = 1e-4
MASKED = -30000.0
NO_ROW = 1 << 20


def spread(eng, body, count, unroll, lead, trail):
    assert lead % unroll == 0
    turns = (count - trail - lead) // unroll
    for i in range(lead):
        body(i, i % unroll)
    if turns > 0:
        with eng.Fori(0, turns) as turn:
            for k in range(unroll):
                body(turn * unroll + (lead + k), k)
    for i in range(lead + max(turns, 0) * unroll, count):
        body(i, i % unroll)


def at_least(i, n):
    return not isinstance(i, int) or i >= n


def before(i, n):
    return not isinstance(i, int) or i < n


def graph_attention_moe(nc, x, adj, Wq, Wk, gate_w, gate_b, w1, w2, w3, out):
    N, D = x.shape
    E, _, H = w1.shape
    T = -(-N // P)
    NP = T * P
    G = T // 2
    CH = 2 * P
    LAST = N - (T - 1) * P
    LAST16 = LAST // 16 * 16
    assert D == P and Wq.shape[0] == P and T % 2 == 0 and H == 2 * P and 0 < LAST < P and LAST > LAST16
    ROW = D + 2
    REGION = NP + P
    SLOTS = (2 * NP + E * (P - 1)) // P
    SLOTS += SLOTS % 2
    BLOCK = P // (P // E)
    PARTS = [0, 4, 14, T]
    OWN = 10
    AW = 2 * D + 2
    SEGS = [0, 4, 7, 10, G]
    AHEAD, BEHIND = SEGS[1], 3
    BUF = [u % 3 for u in range(G - 1)] + [3]
    assert G % 3 == 1 and REGION % BLOCK == 0 and SLOTS <= P and BLOCK == 16

    with ExitStack() as ctx:
        def sb(name, shape, dt):
            return ctx.enter_context(nc.sbuf_tensor(name, shape, dt))

        def sem(name):
            return ctx.enter_context(nc.semaphore(name))

        routed = nc.dram_tensor("routed_rows", [(E + 1) * REGION, ROW], F32).ap()
        expert_out = nc.dram_tensor("expert_rows", [2 * NP, D], F32).ap()

        x_sb = sb("x_sb", [P, T * D], F32)
        f_sb = sb("f_sb", [P, T * D], F32)
        f_aug = sb("f_aug", [P, T, AW], F16)
        qk_hi = sb("qk_hi", [P, G, 2, CH], F16)
        qk_lo = sb("qk_lo", [P, G, 2, CH], F16)
        adj_sb = sb("adj_sb", [P, 2, NP], I32)
        mask = sb("mask", [P, 2, NP], F16)
        p_full = sb("p_full", [P, 4, 2 * CH], F32)
        p_hi = sb("p_hi", [P, 4, 2 * CH], F16)
        p_lo = sb("p_lo", [P, 4, 2 * CH], F16)
        w12_hi = sb("w12_hi", [P, E, 2 * H], F16)
        w12_lo = sb("w12_lo", [P, E, 2 * H], F16)
        w3_hi = sb("w3_hi", [P, E, 2 * D], F16)
        w3_lo = sb("w3_lo", [P, E, 2 * D], F16)
        w_raw = sb("w_raw", [P, 4, H], F32)
        id32 = sb("id32", [P, P], F32)
        id16 = sb("id16", [P, P], F16)
        before16 = sb("before16", [P, P], F16)
        ones16 = sb("ones16", [P, P], F16)
        wqk = sb("wqk", [P, 2, D], F32)
        wqk_t = sb("wqk_t", [P, 2 * P], F32)
        gate_sb = sb("gate_sb", [P, E], F32)
        gate_bias = sb("gate_bias", [P, E], F32)
        expert_i = sb("expert_i", [P, E], I32)
        expert_f = sb("expert_f", [P, E], F32)
        start_f = sb("start_f", [P, E], F32)
        next_row = sb("next_row", [P, E], F32)
        dest_i = sb("dest_i", [P, 2, 2], I32)
        dest_f = sb("dest_f", [P, 2, 2], F32)
        neg_half = sb("neg_half", [P, T], F32)
        stats = sb("stats", [P, T, 6], F32)
        mean_var = sb("mean_var", [P, T, 2], F32)
        var_eps = sb("var_eps", [P, T], F32)
        rstd = sb("rstd", [P, T], F32)
        neg_mean = sb("neg_mean", [P, T], F32)
        shift = sb("shift", [P, T], F32)
        ft_sb = p_full[:, 0:1, :].rearrange("p a (b n) -> p (a b) n", b=2)
        sq_sb = p_full[:, 1, :]
        qn_sb = p_full[:, 2:4, :]
        ss = sb("ss", [P, 2, 4], F32)
        ss_max = sb("ss_max", [P, 2, 4], F32)
        rnorm = sb("rnorm", [P, 2, 4], F32)
        o_sb = sb("o_sb", [P, 2, 2 * D + 1], F32)
        mix = sb("mix", [P, 2, D], F32)
        keep = sb("keep", [P, 2, D], F32)
        small = sb("small", [P, 16, 2], F32)
        stats2 = sb("stats2", [P, 2, 6], F32)
        mean_var2 = sb("mean_var2", [P, 2, 2], F32)
        f2 = sb("f2", [P, 2, D], F32)
        f2_t = sb("f2_t", [P, CH], F32)
        logits = sb("logits", [P, 2, E], F32)
        top_v = sb("top_v", [P, 2, 8], F32)
        top_i = sb("top_i", [P, 2, 8], U32)
        top_f = sb("top_f", [P, 2, 2], F32)
        one_hot = sb("one_hot", [P, 4, E], F32)
        one_hot_sum = sb("one_hot_sum", [P, 2, E], F16)
        row_of = sb("row_of", [P, 2, E], F32)
        row_pick = sb("row_pick", [P, 4, E], F32)
        row_f = sb("row_f", [P, 4], F32)
        row_i = sb("row_i", [P, 4], I32)
        rows = sb("rows", [P, 4, ROW], F32)
        pad_rows = sb("pad_rows", [P, BLOCK, ROW], F32)
        tri_e = sb("tri_e", [P, E, E], F32)
        grid = sb("grid", [P, E, E], F32)
        part_i = sb("part_i", [P, 4], I32)
        part_f = sb("part_f", [P, 1], F32)
        pad_of = sb("pad_of", [P, 1], F32)
        pad_of2 = sb("pad_of2", [P, 2], F32)
        pad_e = sb("pad_e", [P, E], F32)
        ends = sb("ends", [P, 2, E], F32)
        ends_i = sb("ends_i", [P, E], I32)
        pad_pick = sb("pad_pick", [P, 2, E], F32)
        pad_end = sb("pad_end", [P, 2], F32)
        pad_row = sb("pad_row", [P, 2, 2], F32)
        pad_idx = sb("pad_idx", [P, 3], I32)
        tiles_i = sb("tiles_i", [P, E], I32)
        tiles_f = sb("tiles_f", [P, E], F32)
        cum_f = sb("cum_f", [P, E], F32)
        done_e = sb("done_e", [P, 2, E], F32)
        sched = sb("sched", [P, 8], F32)
        slot_table = sb("slot_table", [1, 2, P], I32)
        y_idx = sb("y_idx", [P, 8], I32)
        y_gate = sb("y_gate", [P, 8], F32)
        adj_f = adj_sb[:, :, :].bitcast(F32).rearrange("p a n -> p (a n)")
        x_rows = adj_f[:, 0:8 * ROW].rearrange("p (b n) -> p b n", b=8)
        y_sb = adj_f[:, 2048:2048 + 4 * D].rearrange("p (b n) -> p b n", b=4)
        act_sb = adj_f[:, 3072:3072 + 4 * H].rearrange("p (b n) -> p b n", b=4)
        hid_sb = adj_f[:, 4096:4096 + 4 * H].rearrange("p (b n) -> p b n", b=4)
        mask_flat = mask[:, :, :].rearrange("p a n -> p (a n)")
        xt_sb = mask_flat[:, 0:4 * CH].rearrange("p (b n) -> p b n", b=4)
        ht_hi = mask_flat[:, 1024:1024 + 4 * H].rearrange("p (b n) -> p b n", b=4)
        ht_lo = mask_flat[:, 2048:2048 + 4 * H].rearrange("p (b n) -> p b n", b=4)
        ya_sb = qk_hi[:, :, :, :].rearrange("p g a n -> p (g a n)").bitcast(F32)
        yb_sb = qk_lo[:, :, :, :].rearrange("p g a n -> p (g a n)").bitcast(F32)

        bank = [ctx.enter_context(nc.psum_tensor(f"bank{i}", [P, 512], F32)) for i in range(4)]
        o_ps = ctx.enter_context(nc.psum_tensor("o_ps", [P, 2, 512], F32))
        misc = [ctx.enter_context(nc.psum_tensor(f"misc{i}", [P, 512], F32)) for i in range(2)]

        xt_bank = [misc[b % 2][:, b // 2 * P:(b // 2 + 1) * P] for b in range(4)]
        y_bank = [o_ps[:, b % 2, b // 2 * D:(b // 2 + 1) * D] for b in range(4)]

        x_in = [sem(f"x_in{i}") for i in range(len(PARTS) - 1)]
        w_in, gate_in = sem("w_in"), sem("gate_in")
        adj_in = [sem(f"adj_in{s}") for s in range(len(SEGS) - 1)]
        w_raw_in, w_hi_done, w_lo_done = sem("w_raw_in"), sem("w_hi_done"), sem("w_lo_done")
        waited = sem("waited")
        x_padded, adj_padded, const_steps, consts = sem("x_padded"), sem("adj_padded"), sem("const_steps"), sem("consts")
        stats_done, aggr_done, var_done, rstd_done = sem("stats_done"), sem("aggr_done"), sem("var_done"), sem("rstd_done")
        id_ready, shift_done = sem("id_ready"), sem("shift_done")
        f_done, f_done2 = sem("f_done"), sem("f_done2")
        f_hi_done, f_lo_done = sem("f_hi_done"), sem("f_lo_done")
        wt_ps, wt_done = sem("wt_ps"), sem("wt_done")
        ft_ps, ft_copied, proj_ps, squared = sem("ft_ps"), sem("ft_copied"), sem("proj_ps"), sem("squared")
        ss_summed, ss_clamped, rnorm_done = sem("ss_summed"), sem("ss_clamped"), sem("rnorm_done")
        qn_scaled, qt_ps, q_hi_done, q_lo_done = sem("qn_scaled"), sem("qt_ps"), sem("q_hi_done"), sem("q_lo_done")
        mask0_done = sem("mask0_done")
        mask_done, s_done, p_done, p_hi_done = sem("mask_done"), sem("s_done"), sem("p_done"), sem("p_hi_done")
        p_lo_done, pv_done, o_evac = sem("p_lo_done"), sem("pv_done"), sem("o_evac")
        pool_ep, dve_ep = sem("pool_ep"), sem("dve_ep")
        weights_ready, x2_ready, var2_ready, rstd2_ready = sem("weights_ready"), sem("x2_ready"), sem("var2_ready"), sem("rstd2_ready")
        f2_ready, gap_ready, one_hot_ready = sem("f2_ready"), sem("gap_ready"), sem("one_hot_ready")
        tails_ready, places_ready, place_steps = sem("tails_ready"), sem("places_ready"), sem("place_steps")
        rows_free, rows_hi_ready, rows_lo_ready = sem("rows_free"), sem("rows_hi_ready"), sem("rows_lo_ready")
        f2t_ps, f2t_done, logits_ps, gate_exp, rank_ps = sem("f2t_ps"), sem("f2t_done"), sem("logits_ps"), sem("gate_exp"), sem("rank_ps")
        rows_stored, pad_stored = sem("rows_stored"), sem("pad_stored")
        sched_steps, slots_ready, slots_ps, sched_done, pads_ready = sem("sched_steps"), sem("slots_ready"), sem("slots_ps"), sem("sched_done"), sem("pads_ready")
        x_rows_in = [sem(f"x_rows_in{b}") for b in range(8)]
        idx_done, gate_done = sem("idx_done"), sem("gate_done")
        xt_ps, xt_done, h_ps, act_done, hid_done = sem("xt_ps"), sem("xt_done"), sem("h_ps"), sem("act_done"), sem("hid_done")
        ht_ps, ht_hi_done, ht_lo_done, y_ps, y_done = sem("ht_ps"), sem("ht_hi_done"), sem("ht_lo_done"), sem("y_ps"), sem("y_done")
        y_stored = [sem(f"y_stored{b}") for b in range(4)]
        ya_in = [sem(f"ya_in{i}") for i in range(5)]
        yb_in = [sem(f"yb_in{i}") for i in range(5)]
        CUTS = [0, 5, 10, 15, 20, T]
        sum_a, sum_done, out_stored = sem("sum_a"), sem("sum_done"), sem("out_stored")

        POOL_EP = 4
        DVE_EP = 18
        PLACE_STEPS = 4

        def wait_alone(eng, what, value):
            eng.wait_ge(what, value)
            if not isinstance(value, int):
                eng.sem_inc(waited, 1)

        def load_values(eng, row, t, count, max_val):
            _, values = nc.values_load_multi_w_load_instructions(
                slot_table[0:1, row, bass.ds(t, count)], engines=[eng], min_val=0, max_val=max_val,
                skip_runtime_bounds_check_because="VectorE made the table, with experts clamped and rows inside their regions")
            return values

        block = ctx.enter_context(nc.Block())

        @block.sync
        def _(sp):
            for i in range(len(PARTS) - 1):
                a, b = PARTS[i], min(PARTS[i + 1], T - 1)
                sp.dma_start(x_sb[:, a * D:b * D].rearrange("p (t d) -> p t d", d=D),
                             x[a * P:b * P, :].rearrange("(t p) d -> p t d", p=P)).then_inc(x_in[i], 16)
                if i == 0:
                    sp.dma_start(wqk[:, 0, :], Wq[:, :]).then_inc(w_in, 16)
                    sp.dma_start(wqk[:, 1, :], Wk[:, :]).then_inc(w_in, 16)
            sp.wait_ge(x_padded, 1)
            for a, b in ((0, LAST16), (LAST16, LAST)):
                sp.dma_start(x_sb[a:b, (T - 1) * D:], x[(T - 1) * P + a:(T - 1) * P + b, :]).then_inc(x_in[-1], 16)
            sp.dma_start(gate_sb[:, :], gate_w[:, :]).then_inc(gate_in, 16)
            sp.dma_start(gate_bias[:, :], gate_b.rearrange("(a e) -> a e", a=1).to_broadcast([P, E])).then_inc(gate_in, 16)

            def load_adj(c, last=False):
                for s in range(len(SEGS) - 1):
                    a, b = SEGS[s] * CH, min(SEGS[s + 1] * CH, N)
                    if isinstance(c, int) and c == 1:
                        sp.wait_ge(mask0_done, SEGS[s + 1])
                    elif at_least(c, 2):
                        wait_alone(sp, mask_done, (c - 2) * G + SEGS[s + 1])
                    if last:
                        r = c * CH
                        sp.dma_start(adj_sb[:, 0, a:b], adj[r:r + P, a:b]).then_inc(adj_in[s], 16)
                        sp.dma_start(adj_sb[0:LAST16, 1, a:b], adj[r + P:r + P + LAST16, a:b]).then_inc(adj_in[s], 16)
                        sp.dma_start(adj_sb[LAST16:LAST, 1, a:b], adj[r + P + LAST16:N, a:b]).then_inc(adj_in[s], 16)
                    else:
                        sp.dma_start(adj_sb[:, :, a:b],
                                     adj[bass.ds(c * CH, CH), a:b].rearrange("(i p) n -> p i n", p=P)).then_inc(adj_in[s], 16)

            sp.wait_ge(adj_padded, 1)
            load_adj(0)
            load_adj(1)
            with sp.Fori(2, G - 1) as c:
                load_adj(c)
            load_adj(G - 1, last=True)
            sp.wait_ge(rows_stored, 16 * 4 * G)
            sp.wait_ge(pad_stored, 16 * 4)
            sp.wait_ge(sched_done, 1)

            def load_rows(t, b, at):
                if at_least(t, 8):
                    wait_alone(sp, xt_ps, t - 7)
                    wait_alone(sp, idx_done, t - 7)
                    wait_alone(sp, gate_done, t - 7)
                sp.dma_start(x_rows[:, b, :], routed[bass.ds(at, P), :]).then_inc(x_rows_in[b], 16)

            def eight_loads(t):
                at = load_values(mybir.EngineType.SP, 0, t, 8, (E + 1) * REGION - P)
                for b in range(8):
                    if before(t, SLOTS - b):
                        load_rows(t + b, b, at[b])

            eight_loads(0)
            with sp.Fori(1, SLOTS // 8) as turn:
                eight_loads(turn * 8)
            eight_loads(SLOTS // 8 * 8)
            for b in range(4):
                sp.wait_ge(y_stored[b], 16 * len(range(b, SLOTS, 4)))
            for i in range(5):
                a, b = CUTS[i], CUTS[i + 1]
                sp.dma_start(ya_sb[:, a * D:b * D].rearrange("p (t d) -> p t d", d=D),
                             expert_out[a * P:b * P, :].rearrange("(t p) d -> p t d", p=P)).then_inc(ya_in[i], 16)
            for i in range(5):
                a, b = CUTS[i], min(CUTS[i + 1], T - 1)
                sp.wait_ge(sum_done, i + 1)
                sp.dma_start(out[a * P:b * P, :].rearrange("(t p) d -> p t d", p=P),
                             x_sb[:, a * D:b * D].rearrange("p (t d) -> p t d", d=D)).then_inc(out_stored, 16)
            for a, b in ((0, LAST16), (LAST16, LAST)):
                sp.dma_start(out[(T - 1) * P + a:(T - 1) * P + b, :], x_sb[a:b, (T - 1) * D:]).then_inc(out_stored, 16)
            sp.wait_ge(out_stored, 16 * 7)

        def mix_output(c, ns, ep):
            xc = x_sb[:, bass.ds(c * CH, CH)].rearrange("p (a d) -> p a d", a=2)
            fc = f_sb[:, bass.ds(c * CH, CH)].rearrange("p (a d) -> p a d", a=2)
            wide = [P, 2, D]
            ep(ns.tensor_tensor(mix[:, :, :], mix[:, :, :], small[:, 3, :].unsqueeze(2).to_broadcast(wide), ALU.mult))
            ep(ns.tensor_tensor(keep[:, :, :], fc, small[:, 4, :].unsqueeze(2).to_broadcast(wide), ALU.mult))
            ep(ns.tensor_tensor(mix[:, :, :], mix[:, :, :], keep[:, :, :], ALU.add))
            ns.tensor_tensor(xc, xc, mix[:, :, :], ALU.add).then_inc(x2_ready, 1)

        def weight_parts(kind, e):
            if kind < 2:
                return [t[:, bass.ds(e, 4), kind * H:(kind + 1) * H] for t in (w12_hi, w12_lo)]
            return [t[:, bass.ds(e, 4), :] for t in (w3_hi, w3_lo)]

        rows_hi = rows[:, :, 0:D // 2].bitcast(F16).rearrange("p (a k) d -> p a k d", a=2)
        rows_lo = rows[:, :, D // 2:D].bitcast(F16).rearrange("p (a k) d -> p a k d", a=2)
        f2_twice = f2[:, :, :].unsqueeze(2).to_broadcast([P, 2, 2, D])

        @block.gpsimd
        def _(pool):
            n = [0]

            def step(ins):
                n[0] += 1
                ins.then_inc(const_steps, 1)
                pool.wait_ge(const_steps, n[0])

            nc.gpsimd.memset(x_sb[:, (T - 1) * D:], 0.0).then_inc(x_padded, 1)
            nc.gpsimd.memset(adj_sb[:, :, N:NP], 0).then_inc(adj_padded, 1)
            step(nc.gpsimd.memset(neg_half[:, :], -0.5))
            step(nc.gpsimd.memset(id32[:, :], 0.0))
            nc.gpsimd.affine_select(out=id32[:, :], in_=id32[:, :], compare_op=ALU.not_equal, fill=1.0,
                                    base=0, pattern=[[-1, P]], channel_multiplier=1).then_inc(id_ready, 1)
            step(nc.gpsimd.memset(f_aug[:, :, D:D + 1], 1.0))
            step(nc.gpsimd.memset(ones16[:, :], 1.0))
            step(nc.gpsimd.affine_select(out=before16[:, :], in_=ones16[:, :], compare_op=ALU.is_gt, fill=0.0,
                                         base=0, pattern=[[1, P]], channel_multiplier=-1))
            pool.wait_ge(id_ready, 1)
            step(nc.gpsimd.tensor_copy(id16[:, :], id32[:, :]))
            step(nc.gpsimd.iota(expert_i[:, :], pattern=[[1, E]], base=0, channel_multiplier=0))
            step(nc.gpsimd.tensor_copy(expert_f[:, :], expert_i[:, :]))
            step(nc.gpsimd.tensor_scalar(start_f[:, :], expert_f[:, :], float(REGION), 0.0, ALU.mult, ALU.add))
            step(nc.gpsimd.tensor_copy(next_row[:, :], start_f[:, :]))
            step(nc.gpsimd.iota(dest_i[:, :, :], pattern=[[P, 2], [NP, 2]], base=0, channel_multiplier=1))
            nc.gpsimd.tensor_copy(dest_f[:, :, :], dest_i[:, :, :]).then_inc(consts, 1)

            def rstd_part(i):
                pool.wait_ge(var_done, i + 1)
                at = slice(PARTS[i], PARTS[i + 1])
                nc.gpsimd.tensor_tensor(rstd[:, at], var_eps[:, at], neg_half[:, at], ALU.pow).then_inc(rstd_done, 1)
                if i > 0:
                    pool.wait_ge(rstd_done, i + 1)
                    nc.gpsimd.tensor_tensor(shift[:, at], neg_mean[:, at], rstd[:, at], ALU.mult).then_inc(shift_done, 1)

            def norms(g, b):
                pool.wait_ge(ss_clamped, g + 1)
                if at_least(g, 2):
                    pool.wait_ge(qn_scaled, g - 1)
                nc.gpsimd.tensor_tensor(rnorm[:, b, :], ss_max[:, b, :], neg_half[:, 0:4], ALU.pow).then_inc(rnorm_done, 1)

            for i in range(len(PARTS) - 1):
                rstd_part(i)
            spread(pool, norms, G, 2, 2, 1)

            def f_low(g):
                pool.wait_ge(f_hi_done, next(i for i in range(1, len(PARTS)) if 2 * g + 2 <= PARTS[i]))
                two = f_aug[:, 2 * g:2 * g + 2, :]
                nc.gpsimd.tensor_tensor(two[:, :, D + 1:2 * D + 1], f_sb[:, g * CH:(g + 1) * CH].rearrange("p (a d) -> p a d", a=2),
                                        two[:, :, 0:D], ALU.subtract).then_inc(f_lo_done, 1)

            for g in range(G):
                f_low(g)

            step(nc.gpsimd.memset(pad_rows[:, :, :], 0.0))
            step(nc.gpsimd.memset(pad_rows[:, :, D + 1:D + 2].bitcast(I32), NO_ROW))
            step(nc.gpsimd.memset(tri_e[:, :, :], 1.0))
            step(nc.gpsimd.affine_select(out=tri_e[:, :, :], in_=tri_e[:, :, :], compare_op=ALU.is_ge, fill=0.0,
                                         base=0, pattern=[[1, E], [-1, E]], channel_multiplier=0))
            step(nc.gpsimd.iota(part_i[:, 0:1], pattern=[[0, 1]], base=0, channel_multiplier=1))
            step(nc.gpsimd.tensor_copy(part_f[:, :], part_i[:, 0:1]))
            per = P // E
            step(nc.gpsimd.memset(pad_e[:, :], 1.0))
            step(nc.gpsimd.affine_select(out=pad_e[:, :], in_=pad_e[:, :], compare_op=ALU.is_ge, fill=0.0,
                                         base=0, pattern=[[-per, E]], channel_multiplier=1))
            step(nc.gpsimd.affine_select(out=pad_e[:, :], in_=pad_e[:, :], compare_op=ALU.is_ge, fill=0.0,
                                         base=per - 1, pattern=[[per, E]], channel_multiplier=-1))
            step(nc.gpsimd.tensor_tensor(pad_pick[:, 0, :], pad_e[:, :], expert_f[:, :], ALU.mult))
            nc.gpsimd.tensor_scalar(pad_pick[:, 1, :], pad_pick[:, 0, :], float(-per), 0.0, ALU.mult, ALU.add).then_inc(consts, 1)
            pool.dma_start(routed[E * REGION:E * REGION + P, :], pad_rows[:, 0, :]).then_inc(pad_stored, 16)

            def epilogue(c, kind, e):
                k = [0]

                def ep(ins):
                    k[0] += 1
                    ins.then_inc(pool_ep, 1)
                    pool.wait_ge(pool_ep, c * POOL_EP + k[0])

                pool.wait_ge(o_evac, c + 1)
                ep(nc.gpsimd.tensor_tensor(mix[:, :, :], o_sb[:, :, 0:D], o_sb[:, :, D + 1:2 * D + 1], ALU.add))
                pool.wait_ge(weights_ready, c + 1)
                mix_output(c, nc.gpsimd, ep)
                assert k[0] == POOL_EP
                if at_least(c, 1):
                    scatter_rows(c - 1, 0)
                pool.wait_ge(var2_ready, c + 1)
                nc.gpsimd.tensor_tensor(small[:, 6, :], small[:, 5, :], neg_half[:, 0:2], ALU.pow).then_inc(rstd2_ready, 1)
                if at_least(c, 1):
                    scatter_rows(c - 1, 1)
                if kind < 2:
                    pool.dma_start(w_raw[:, :, :], (w1, w2)[kind][bass.ds(e, 4)].rearrange("e d h -> d e h")).then_inc(w_raw_in, 16)
                else:
                    pool.dma_start(w_raw[:, :, :].rearrange("p e (c o) -> p e c o", c=2),
                                   w3[bass.ds(e, 4)].rearrange("e (c p) o -> p e c o", p=P)).then_inc(w_raw_in, 16)
                free_rows(c)
                pool.wait_ge(rows_hi_ready, c + 1)
                nc.gpsimd.tensor_tensor(rows_lo, f2_twice, rows_hi, ALU.subtract).then_inc(rows_lo_ready, 1)
                pool.wait_ge(w_hi_done, c + 1)
                hi, lo = weight_parts(kind, e)
                nc.gpsimd.tensor_tensor(lo, w_raw[:, :, :], hi, ALU.subtract).then_inc(w_lo_done, 1)
                pool.wait_ge(w_lo_done, c + 1)

            def scatter_rows(c, half):
                if half == 0:
                    wait_alone(pool, rows_lo_ready, c + 1)
                    wait_alone(pool, tails_ready, c + 1)
                    wait_alone(pool, places_ready, c + 1)
                for j in (2 * half, 2 * half + 1):
                    pool.indirect_dma_start(out=routed[:, :], out_offset=bass.IndirectOffsetOnAxis(ap=row_i[:, j:j + 1], axis=0),
                                            in_=rows[:, j, :], in_offset=None).then_inc(rows_stored, 16)

            def free_rows(c):
                if at_least(c, 1):
                    pool.wait_ge(rows_stored, 64 * c)
                pool.sem_inc(rows_free, 1)

            assert G - 1 == 3 * (E // 4)
            for kind in range(3):
                epilogue(kind, kind, 0)
            with pool.Fori(1, E // 4) as lot:
                for kind in range(3):
                    epilogue(lot * 3 + kind, kind, lot * 4)
            c = G - 1
            for half in range(2):
                scatter_rows(c - 1, half)
            free_rows(c)
            pool.wait_ge(var2_ready, c + 1)
            nc.gpsimd.tensor_tensor(small[:, 6, :], small[:, 5, :], neg_half[:, 0:2], ALU.pow).then_inc(rstd2_ready, 1)
            for half in range(2):
                scatter_rows(c, half)
            pool.wait_ge(pads_ready, 1)
            pool.indirect_dma_start(out=routed[:, :].rearrange("(b r) n -> b (r n)", r=BLOCK),
                                    out_offset=bass.IndirectOffsetOnAxis(ap=pad_idx[:, 2:3], axis=0),
                                    in_=pad_rows[:, :, :].rearrange("p r n -> p (r n)"), in_offset=None).then_inc(pad_stored, 16)
            for j in range(2):
                pool.indirect_dma_start(out=routed[:, :], out_offset=bass.IndirectOffsetOnAxis(ap=pad_idx[:, j:j + 1], axis=0),
                                        in_=pad_rows[:, 0, :], in_offset=None,
                                        bounds_check=(E + 1) * REGION - 1, oob_is_err=False).then_inc(pad_stored, 16)

            def store_rows(t, b):
                wait_alone(pool, idx_done, t + 1)
                wait_alone(pool, y_done, t + 1)
                pool.indirect_dma_start(out=expert_out[:, :],
                                        out_offset=bass.IndirectOffsetOnAxis(ap=y_idx[:, b:b + 1], axis=0),
                                        in_=y_sb[:, b % 4, :], in_offset=None,
                                        bounds_check=2 * NP - 1, oob_is_err=False).then_inc(y_stored[b % 4], 16)

            spread(pool, store_rows, SLOTS, 8, 0, 0)

        @block.tensor
        def _(pe):
            pe.wait_ge(id_ready, 1)
            pe.wait_ge(w_in, 32)
            for k in range(2):
                last = nc.tensor.transpose(misc[0][:, k * P:(k + 1) * P], wqk[:, k, :], id32[:, :])
            last.then_inc(wt_ps, 1)
            pe.wait_ge(wt_done, 1)

            def project(i, b):
                o = 1 - b
                if i < G:
                    if 2 * i + 2 <= OWN:
                        pe.wait_ge(f_done, 2 * i + 2)
                    else:
                        pe.wait_ge(f_done2, 2 * i + 2 - OWN)
                    if i >= 2:
                        pe.wait_ge(ft_copied, i - 1)
                    for k in range(2):
                        last = nc.tensor.transpose(misc[b][:, k * P:(k + 1) * P],
                                                   f_sb[:, (2 * i + k) * D:(2 * i + k + 1) * D], id32[:, :])
                    last.then_inc(ft_ps, 1)
                if 1 <= i < G + 1:
                    g = i - 1
                    pe.wait_ge(ft_copied, g + 1)
                    for k in range(2):
                        last = nc.tensor.matmul(bank[g % 4][:, k * CH:(k + 1) * CH], ft_sb[:, o, k * P:(k + 1) * P],
                                                wqk_t[:, :], start=True, stop=True)
                    last.then_inc(proj_ps, 1)
                if i >= 3:
                    g = i - 3
                    pe.wait_ge(qn_scaled, g + 1)
                    if g >= 2:
                        pe.wait_ge(q_lo_done, g - 1)
                    for a in range(2):
                        for k in range(2):
                            last = nc.tensor.transpose(o_ps[:, o, (2 * k + a) * P:(2 * k + a + 1) * P],
                                                       qn_sb[:, o, (2 * a + k) * P:(2 * a + k + 1) * P], id32[:, :])
                    last.then_inc(qt_ps, 1)

            for i in range(G + 3):
                project(i, i % 2)
            pe.wait_ge(gate_in, 32)
            pe.wait_ge(consts, 1)

            def scores(c, u):
                if isinstance(c, int) and c == 0:
                    pe.wait_ge(q_lo_done, u + 1)
                    pe.wait_ge(mask0_done, u + 1)
                else:
                    pe.wait_ge(mask_done, (c - 1) * G + u + 1)
                s = bank[BUF[u]]
                k_hi = qk_hi[:, bass.ds(c, 1), 1, :]
                k_lo = qk_lo[:, bass.ds(c, 1), 1, :]
                for j in range(2):
                    to = s[:, j * CH:(j + 1) * CH]
                    q_hi = qk_hi[:, u, 0, j * P:(j + 1) * P]
                    q_lo = qk_lo[:, u, 0, j * P:(j + 1) * P]
                    nc.tensor.matmul(to, q_hi, k_hi, start=True, stop=False)
                    nc.tensor.matmul(to, q_hi, k_lo, start=False, stop=False)
                    nc.tensor.matmul(to, q_lo, k_hi, start=False, stop=False)
                    for a in range(2):
                        key = (2 * u + j) * P
                        last = nc.tensor.matmul(s[:, j * CH + a * P:j * CH + (a + 1) * P], mask[:, a, key:key + P],
                                                id16[:, :], start=False, stop=(a == 1))
                last.then_inc(s_done, 1)

            def values(c, u):
                if u == 0 and at_least(c, 1):
                    pe.wait_ge(o_evac, c)
                pe.wait_ge(p_lo_done, c * G + u + 1)
                if isinstance(c, int) and c == 0:
                    pe.wait_ge(f_lo_done, u + 1)
                    if u == 0:
                        pe.wait_ge(q_lo_done, G)
                b = BUF[u]
                for a in range(2):
                    for j in range(2):
                        at = slice(j * CH + a * P, j * CH + (a + 1) * P)
                        first, final = u == 0 and j == 0, u == G - 1 and j == 1
                        f = f_aug[:, 2 * u + j, :]
                        nc.tensor.matmul(o_ps[:, a, 0:2 * D + 1], p_hi[:, b, at], f[:, 0:2 * D + 1], start=first, stop=False)
                        last = nc.tensor.matmul(o_ps[:, a, 0:D + 1], p_lo[:, b, at], f[:, 0:D + 1], start=False, stop=final)
                last.then_inc(pv_done, 1)

            def transpose_f2(c):
                pe.wait_ge(f2_ready, c + 1)
                for a in range(2):
                    last = nc.tensor.transpose(misc[0][:, a * P:(a + 1) * P], f2[:, a, :], id32[:, :])
                last.then_inc(f2t_ps, 1)

            def gate_logits(c):
                pe.wait_ge(f2t_done, c + 1)
                for a in range(2):
                    last = nc.tensor.matmul(misc[1][:, a * E:(a + 1) * E], f2_t[:, a * P:(a + 1) * P], gate_sb[:, :],
                                            start=True, stop=True)
                last.then_inc(logits_ps, 1)

            def ranks(c):
                pe.wait_ge(one_hot_ready, c + 1)
                r = misc[1][:, 64:64 + 3 * E]
                oh = [one_hot_sum[:, a, :] for a in range(2)]
                nc.tensor.matmul(r[:, 0:E], before16[:, :], oh[0], start=True, stop=True)
                nc.tensor.matmul(r[:, E:2 * E], before16[:, :], oh[1], start=True, stop=False)
                nc.tensor.matmul(r[:, E:2 * E], ones16[:, :], oh[0], start=False, stop=True)
                nc.tensor.matmul(r[:, 2 * E:3 * E], ones16[:, :], oh[0], start=True, stop=False)
                nc.tensor.matmul(r[:, 2 * E:3 * E], ones16[:, :], oh[1], start=False, stop=True).then_inc(rank_ps, 1)

            def chunk(c, last=False):
                for u in range(G):
                    if u + 2 < G:
                        scores(c, u + 2)
                    elif not last:
                        scores(c + 1, u + 2 - G)
                    values(c, u)
                    if at_least(c, 1):
                        if u == 8:
                            transpose_f2(c - 1)
                        if u == 9:
                            gate_logits(c - 1)
                        if u == 12:
                            ranks(c - 1)

            scores(0, 0)
            scores(0, 1)
            chunk(0)
            with pe.Fori(1, G - 1) as c:
                chunk(c)
            chunk(G - 1, last=True)
            transpose_f2(G - 1)
            gate_logits(G - 1)
            ranks(G - 1)

            pe.wait_ge(slots_ready, 1)
            for k in range(2):
                last = nc.tensor.transpose(misc[0][0:1, k * P:(k + 1) * P], sched[:, 6 + k:7 + k], id32[:, :])
            last.then_inc(slots_ps, 1)

            pe.wait_ge(sched_done, 1)
            pe.wait_ge(w_lo_done, 3 * (E // 4))

            def expert(i, k8, e_in, e_out):
                if before(i, SLOTS):
                    pe.wait_ge(x_rows_in[k8], 2 * (i - k8) + 16)
                    half = xt_bank[k8 % 4].bitcast(F16)
                    for k in range(2):
                        last = nc.tensor.transpose(half[:, k * P:(k + 1) * P],
                                                   x_rows[:, k8, k * D // 2:(k + 1) * D // 2].bitcast(F16), id16[:, :])
                    last.then_inc(xt_ps, 1)
                if at_least(i, 1) and before(i, SLOTS + 1):
                    t, b4, b2 = i - 1, (k8 - 1) % 4, (k8 - 1) % 2
                    pe.wait_ge(xt_done, t + 1)
                    nc.tensor.matmul(bank[b2][:, :], xt_sb[:, b4, 0:P], w12_hi[:, bass.ds(e_in, 1), :], start=True, stop=False)
                    nc.tensor.matmul(bank[b2][:, :], xt_sb[:, b4, P:2 * P], w12_hi[:, bass.ds(e_in, 1), :], start=False, stop=False)
                    nc.tensor.matmul(bank[b2][:, :], xt_sb[:, b4, 0:P], w12_lo[:, bass.ds(e_in, 1), :], start=False, stop=True).then_inc(h_ps, 1)
                if at_least(i, 2) and before(i, SLOTS + 2):
                    t, b4, b2 = i - 2, (k8 - 2) % 4, k8 % 2
                    pe.wait_ge(hid_done, t + 1)
                    for k in range(2):
                        last = nc.tensor.transpose(bank[2 + b2][:, k * P:(k + 1) * P], hid_sb[:, b4, k * P:(k + 1) * P], id32[:, :])
                    last.then_inc(ht_ps, 1)
                if at_least(i, 3):
                    t, b4 = i - 3, (k8 - 3) % 4
                    pe.wait_ge(ht_lo_done, t + 1)
                    for k in range(H // P):
                        hh, hl = ht_hi[:, b4, k * P:(k + 1) * P], ht_lo[:, b4, k * P:(k + 1) * P]
                        wh = w3_hi[:, bass.ds(e_out, 1), k * D:(k + 1) * D]
                        wl = w3_lo[:, bass.ds(e_out, 1), k * D:(k + 1) * D]
                        nc.tensor.matmul(y_bank[b4], hh, wh, start=(k == 0), stop=False)
                        nc.tensor.matmul(y_bank[b4], hl, wh, start=False, stop=False)
                        last = nc.tensor.matmul(y_bank[b4], hh, wl, start=False, stop=(k == 1))
                    last.then_inc(y_ps, 1)

            def eight_tiles(i):
                back = 3 if at_least(i, 1) else 0
                experts = load_values(mybir.EngineType.PE, 1, i - back, 7 + back, E - 1)
                for k8 in range(8):
                    if before(i, SLOTS + 3 - k8):
                        e_in = experts[k8 - 1 + back] if k8 + back >= 1 else None
                        e_out = experts[k8 - 3 + back] if k8 + back >= 3 else None
                        expert(i + k8, k8, e_in, e_out)

            eight_tiles(0)
            with pe.Fori(1, SLOTS // 8) as turn:
                eight_tiles(turn * 8)
            eight_tiles(SLOTS // 8 * 8)

        @block.scalar
        def _(act):
            act.wait_ge(wt_ps, 1)
            nc.scalar.copy(wqk_t[:, :], misc[0][:, 0:CH]).then_inc(wt_done, 1)
            def f_high(i):
                at = slice(PARTS[i], PARTS[i + 1])
                act.wait_ge(f_done, min(OWN, PARTS[i + 1]))
                if PARTS[i + 1] > OWN:
                    act.wait_ge(f_done2, PARTS[i + 1] - OWN)
                nc.scalar.copy(f_aug[:, at, 0:D], f_sb[:, at.start * D:at.stop * D].rearrange("p (t d) -> p t d", d=D)).then_inc(f_hi_done, 1)

            def project(i, k4):
                b, o = k4 % 2, 1 - k4 % 2
                if before(i, G):
                    act.wait_ge(ft_ps, i + 1)
                    if at_least(i, 2):
                        act.wait_ge(proj_ps, i - 1)
                    nc.scalar.copy(ft_sb[:, b, :], misc[b][:, 0:CH]).then_inc(ft_copied, 1)
                if at_least(i, 1) and before(i, G + 1):
                    act.wait_ge(proj_ps, i)
                    if at_least(i, 2):
                        act.wait_ge(ss_summed, i - 1)
                    nc.scalar.activation(sq_sb, bank[(k4 - 1) % 4][:, :], ACT.Square).then_inc(squared, 1)
                if at_least(i, 3):
                    act.wait_ge(qt_ps, i - 2)
                    nc.scalar.copy(qk_hi[:, bass.ds(i - 3, 1), :, :],
                                   o_ps[:, o, :].rearrange("p (o a n) -> p o a n", o=1, a=2)).then_inc(q_hi_done, 1)

            def normalise(first, last):
                act.wait_ge(shift_done, 1 if last <= PARTS[2] else 2)
                for t in range(first, last):
                    nc.scalar.activation(f_sb[:, t * D:(t + 1) * D], x_sb[:, t * D:(t + 1) * D], ACT.Identity,
                                         scale=rstd[:, t:t + 1], bias=shift[:, t:t + 1]).then_inc(f_done2, 1)

            project(0, 0)
            project(1, 1)
            normalise(OWN, PARTS[2])
            project(2, 2)
            normalise(PARTS[2], PARTS[2] + 6)
            project(3, 3)
            normalise(PARTS[2] + 6, T)
            f_high(0)
            with act.Fori(1, G // 4) as turn:
                for k in range(4):
                    project(turn * 4 + k, k)
            f_high(1)
            for i in range(G // 4 * 4, G + 3):
                project(i, i % 4)

            def probabilities(c, u):
                act.wait_ge(s_done, c * G + u + 1)
                if u < 3 and at_least(c, 1):
                    act.wait_ge(pv_done, c * G + u - 3)
                elif 3 <= u < G - 1:
                    act.wait_ge(pv_done, c * G + u - 2)
                elif u == G - 1 and at_least(c, 1):
                    act.wait_ge(pv_done, c * G)
                b = BUF[u]
                nc.scalar.activation(p_full[:, b, :], bank[b][:, :], ACT.Exp).then_inc(p_done, 1)
                nc.scalar.activation(p_hi[:, b, :], bank[b][:, :], ACT.Exp).then_inc(p_hi_done, 1)

            def evacuate(c):
                act.wait_ge(pv_done, (c + 1) * G)
                nc.scalar.copy(o_sb[:, :, :], o_ps[:, :, 0:2 * D + 1]).then_inc(o_evac, 1)

            def copy_f2t(c):
                act.wait_ge(f2t_ps, c + 1)
                nc.scalar.copy(f2_t[:, :], misc[0][:, 0:CH]).then_inc(f2t_done, 1)

            def exp_gate(c):
                act.wait_ge(gap_ready, c + 1)
                nc.scalar.activation(small[:, 8, :], small[:, 7, :], ACT.Exp).then_inc(gate_exp, 1)

            def rows_high(c):
                act.wait_ge(f2_ready, c + 1)
                act.wait_ge(rows_free, c + 1)
                nc.scalar.copy(rows_hi, f2_twice).then_inc(rows_hi_ready, 1)

            def weight_high(c, kind, e):
                act.wait_ge(w_raw_in, 16 * (c + 1))
                nc.scalar.copy(weight_parts(kind, e)[0], w_raw[:, :, :]).then_inc(w_hi_done, 1)

            def chunk(c, kind, e):
                for u in range(G):
                    probabilities(c, u)
                    if isinstance(c, int) and c == 0 and u == 1:
                        f_high(2)
                    if at_least(c, 1):
                        if u == 1:
                            evacuate(c - 1)
                        if u == 9:
                            copy_f2t(c - 1)
                        if u == 10:
                            rows_high(c - 1)
                        if u == 11:
                            weight_high(c - 1, kind, e)
                        if u == 12:
                            exp_gate(c - 1)

            chunk(0, None, None)
            with act.Fori(0, E // 4) as lot:
                for kind in range(3):
                    chunk(lot * 3 + (kind + 1), kind, lot * 4)
            evacuate(G - 1)
            rows_high(G - 1)
            copy_f2t(G - 1)
            exp_gate(G - 1)

            def expert(i, k8):
                if before(i, SLOTS):
                    act.wait_ge(x_rows_in[k8], 2 * (i - k8) + 16)
                    nc.scalar.copy(y_gate[:, k8:k8 + 1], x_rows[:, k8, D:D + 1]).then_inc(gate_done, 1)
                    act.wait_ge(h_ps, i + 1)
                    nc.scalar.activation(act_sb[:, k8 % 4, :], bank[k8 % 2][:, 0:H], ACT.Silu).then_inc(act_done, 1)
                if at_least(i, 1) and before(i, SLOTS + 1):
                    act.wait_ge(ht_ps, i)
                    nc.scalar.copy(ht_hi[:, (k8 - 1) % 4, :], bank[2 + (k8 - 1) % 2][:, 0:H]).then_inc(ht_hi_done, 1)
                if at_least(i, 2):
                    t, b = i - 2, (k8 - 2) % 4
                    act.wait_ge(y_ps, t + 1)
                    if at_least(i, 6):
                        act.wait_ge(y_stored[b], 4 * (t - b))
                    nc.scalar.mul(y_sb[:, b, :], y_bank[b], y_gate[:, (k8 - 2) % 8:(k8 - 2) % 8 + 1]).then_inc(y_done, 1)

            spread(act, expert, SLOTS + 2, 8, 8, 2)
            for b in range(4):
                act.wait_ge(y_stored[b], 16 * len(range(b, SLOTS, 4)))
            for i in range(5):
                a, b = CUTS[i], CUTS[i + 1]
                act.dma_start(yb_sb[:, a * D:b * D].rearrange("p (t d) -> p t d", d=D),
                              expert_out[NP + a * P:NP + b * P, :].rearrange("(t p) d -> p t d", p=P)).then_inc(yb_in[i], 16)

        @block.vector
        def _(dve):
            def statistics(i):
                dve.wait_ge(x_in[i], 48 if i == len(PARTS) - 2 else 16)
                for t in range(PARTS[i], PARTS[i + 1]):
                    nc.vector.bn_stats(stats[:, t, :], x_sb[:, t * D:(t + 1) * D]).then_inc(stats_done, 1)
                for t in range(PARTS[i], PARTS[i + 1]):
                    dve.wait_ge(stats_done, t + 1)
                    nc.vector.bn_aggr(mean_var[:, t, :], stats[:, t, :]).then_inc(aggr_done, 1)
                dve.wait_ge(aggr_done, PARTS[i + 1])
                at = slice(PARTS[i], PARTS[i + 1])
                nc.vector.tensor_scalar(neg_mean[:, at], mean_var[:, at, 0], -1.0, None, ALU.mult)
                nc.vector.tensor_scalar(var_eps[:, at], mean_var[:, at, 1], LN_EPS, None, ALU.add).then_inc(var_done, 1)

            def normalise(first, last):
                dve.wait_ge(rstd_done, 2 if last > PARTS[1] else 1)
                for t in range(first, last):
                    nc.vector.tensor_scalar(f_sb[:, t * D:(t + 1) * D], x_sb[:, t * D:(t + 1) * D], mean_var[:, t, 0:1],
                                            rstd[:, t:t + 1], ALU.subtract, ALU.mult).then_inc(f_done, 1)

            def q_low(g, b):
                dve.wait_ge(q_hi_done, g + 1)
                nc.vector.tensor_tensor(qk_lo[:, bass.ds(g, 1), :, :], o_ps[:, b, :].rearrange("p (o a n) -> p o a n", o=1, a=2),
                                        qk_hi[:, bass.ds(g, 1), :, :], ALU.subtract).then_inc(q_lo_done, 1)

            def project(i, k4):
                b, o = k4 % 2, 1 - k4 % 2
                if before(i, G):
                    dve.wait_ge(squared, i + 1)
                    if at_least(i, 2):
                        dve.wait_ge(ss_clamped, i - 1)
                    nc.vector.tensor_reduce(ss[:, b, :], sq_sb.rearrange("p (a n) -> p a n", a=4),
                                            axis=AX_X, op=ALU.add).then_inc(ss_summed, 1)
                    dve.wait_ge(ss_summed, i + 1)
                    if at_least(i, 2):
                        dve.wait_ge(rnorm_done, i - 1)
                    nc.vector.tensor_scalar(ss_max[:, b, :], ss[:, b, :], COS_EPS * COS_EPS, None, ALU.max).then_inc(ss_clamped, 1)
                if at_least(i, 1) and before(i, G + 1):
                    dve.wait_ge(rnorm_done, i)
                    if at_least(i, 3):
                        dve.wait_ge(qt_ps, i - 2)
                    nc.vector.tensor_tensor(qn_sb[:, o, :].rearrange("p (a n) -> p a n", a=4),
                                            bank[(k4 - 1) % 4][:, :].rearrange("p (a n) -> p a n", a=4),
                                            rnorm[:, o, :].unsqueeze(2).to_broadcast([P, 4, P]), ALU.mult).then_inc(qn_scaled, 1)
                if at_least(i, 2):
                    q_low(i - 2, b)

            def make_mask(c, u):
                s = next(s for s in range(len(SEGS) - 1) if u < SEGS[s + 1])
                if u == SEGS[s]:
                    if isinstance(c, int) and c == G - 1:
                        dve.wait_ge(adj_in[s], 16 * (c + 3))
                    else:
                        dve.wait_ge(adj_in[s], 16 * (c + 1))
                if at_least(c, 1):
                    dve.wait_ge(s_done, (c - 1) * G + u + 1)
                at = slice(u * CH, (u + 1) * CH)
                nc.vector.tensor_scalar(mask[:, :, at], adj_sb[:, :, at], 0.0, MASKED, ALU.is_le,
                                        ALU.mult).then_inc(mask0_done if isinstance(c, int) and c == 0 else mask_done, 1)

            statistics(0)
            statistics(1)
            normalise(0, PARTS[1])
            statistics(2)
            normalise(PARTS[1], OWN)
            for i in range(4):
                project(i, i)
            with dve.Fori(1, G // 4) as turn:
                for k in range(4):
                    project(turn * 4 + k, k)
            dve.wait_ge(adj_padded, 1)
            for i in range(G // 4 * 4, G + 2):
                make_mask(0, i - G // 4 * 4)
                project(i, i % 4)
            for u in range(G + 2 - G // 4 * 4, AHEAD):
                make_mask(0, u)

            def low_part(c, u):
                b = BUF[u]
                dve.wait_ge(p_hi_done, c * G + u + 1)
                dve.wait_ge(p_done, c * G + u + 1)
                nc.vector.tensor_tensor(p_lo[:, b, :], p_full[:, b, :], p_hi[:, b, :], ALU.subtract).then_inc(p_lo_done, 1)

            k = [0]

            def ep(c, ins, alone=False):
                k[0] += 1
                ins.then_inc(dve_ep, 1)
                (wait_alone(dve, dve_ep, c * DVE_EP + k[0]) if alone else dve.wait_ge(dve_ep, c * DVE_EP + k[0]))

            def epilogue_weights(c):
                k[0] = 0
                dve.wait_ge(o_evac, c + 1)
                total = o_sb[:, :, D]
                ep(c, nc.vector.tensor_scalar(small[:, 0, :], total, 1e-30, None, ALU.max))
                ep(c, nc.vector.reciprocal(small[:, 1, :], small[:, 0, :]))
                ep(c, nc.vector.tensor_scalar(small[:, 2, :], total, 0.0, 0.5, ALU.is_gt, ALU.mult))
                ep(c, nc.vector.tensor_tensor(small[:, 3, :], small[:, 1, :], small[:, 2, :], ALU.mult))
                nc.vector.tensor_scalar(small[:, 4, :], small[:, 2, :], -1.0, 1.0, ALU.mult, ALU.add).then_inc(weights_ready, 1)

            def epilogue_stats(c):
                dve.wait_ge(x2_ready, c + 1)
                for a in range(2):
                    ep(c, nc.vector.bn_stats(stats2[:, a, :], x_sb[:, bass.ds(c * CH + a * D, D)]), a == 1)
                for a in range(2):
                    ep(c, nc.vector.bn_aggr(mean_var2[:, a, :], stats2[:, a, :]), a == 0)
                nc.vector.tensor_scalar(small[:, 5, :], mean_var2[:, :, 1], LN_EPS, None, ALU.add).then_inc(var2_ready, 1)

            def epilogue_norm(c):
                dve.wait_ge(rstd2_ready, c + 1)
                for a in range(2):
                    last = nc.vector.tensor_scalar(f2[:, a, :], x_sb[:, bass.ds(c * CH + a * D, D)], mean_var2[:, a, 0:1],
                                                   small[:, 6, a:a + 1], ALU.subtract, ALU.mult)
                last.then_inc(f2_ready, 1)

            def epilogue_route(c):
                dve.wait_ge(logits_ps, c + 1)
                ep(c, nc.vector.tensor_tensor(logits[:, :, :], misc[1][:, 0:2 * E].rearrange("p (a e) -> p a e", a=2),
                                              gate_bias[:, :].unsqueeze(1).to_broadcast([P, 2, E]), ALU.add), True)
                for a in range(2):
                    ep(c, nc.vector.max(top_v[:, a, :], logits[:, a, :]), a == 0)
                nc.vector.tensor_tensor(small[:, 7, :], top_v[:, :, 1], top_v[:, :, 0], ALU.subtract).then_inc(gap_ready, 1)
                for a in range(2):
                    ep(c, nc.vector.max_index(top_i[:, a, :], top_v[:, a, :], logits[:, a, :]), a == 0)
                ep(c, nc.vector.tensor_copy(top_f[:, :, :], top_i[:, :, 0:2]))
                ep(c, nc.vector.tensor_tensor(one_hot[:, :, :].rearrange("p (a k) e -> p a k e", a=2),
                                              expert_f[:, :].unsqueeze(1).unsqueeze(1).to_broadcast([P, 2, 2, E]),
                                              top_f[:, :, :].unsqueeze(3).to_broadcast([P, 2, 2, E]), ALU.is_equal))
                oh = one_hot[:, :, :].rearrange("p (a k) e -> p a k e", a=2)
                nc.vector.tensor_tensor(one_hot_sum[:, :, :], oh[:, :, 0, :], oh[:, :, 1, :], ALU.add).then_inc(one_hot_ready, 1)

            def epilogue_tails(c):
                tail = rows[:, :, :].rearrange("p (a k) n -> p a k n", a=2)
                dve.wait_ge(gate_exp, c + 1)
                ep(c, nc.vector.tensor_scalar(small[:, 9, :], small[:, 8, :], 1.0, None, ALU.add))
                ep(c, nc.vector.reciprocal(small[:, 10, :], small[:, 9, :]))
                nc.vector.tensor_copy(tail[:, :, 0, D], small[:, 10, :])
                nc.vector.tensor_tensor(tail[:, :, 1, D], small[:, 8, :], small[:, 10, :], ALU.mult)
                ep(c, nc.vector.tensor_copy(tail[:, :, :, D + 1].bitcast(I32), dest_f[:, :, :]))
                nc.vector.tensor_scalar(dest_f[:, :, :], dest_f[:, :, :], float(CH), None, ALU.add).then_inc(tails_ready, 1)

            def epilogue_places(c):
                m = [0]

                def ep(c, ins):
                    m[0] += 1
                    ins.then_inc(place_steps, 1)
                    dve.wait_ge(place_steps, c * PLACE_STEPS + m[0])

                oh = one_hot[:, :, :].rearrange("p (a k) e -> p a k e", a=2)
                dve.wait_ge(rank_ps, c + 1)
                ep(c, nc.vector.tensor_tensor(row_of[:, :, :], misc[1][:, 64:64 + 2 * E].rearrange("p (a e) -> p a e", a=2),
                                              next_row[:, :].unsqueeze(1).to_broadcast([P, 2, E]), ALU.add))
                ep(c, nc.vector.tensor_tensor(row_pick[:, :, :].rearrange("p (a k) e -> p a k e", a=2), oh,
                                              row_of[:, :, :].unsqueeze(2).to_broadcast([P, 2, 2, E]), ALU.mult))
                ep(c, nc.vector.tensor_tensor(next_row[:, :], next_row[:, :], misc[1][:, 64 + 2 * E:64 + 3 * E], ALU.add))
                ep(c, nc.vector.tensor_reduce(row_f[:, :], row_pick[:, :, :], axis=AX_X, op=ALU.add))
                nc.vector.tensor_copy(row_i[:, :], row_f[:, :]).then_inc(places_ready, 1)
                assert m[0] == PLACE_STEPS

            def chunk(c, last=False):
                for u in range(G):
                    if isinstance(c, int) and c == 0:
                        if u + AHEAD < G:
                            make_mask(0, u + AHEAD)
                        low_part(c, u)
                        if u >= BEHIND:
                            make_mask(1, u - BEHIND)
                    else:
                        if isinstance(c, int) and c == 1 and u == 0:
                            for v in range(G - BEHIND, G):
                                make_mask(1, v)
                        low_part(c, u)
                        if not last:
                            make_mask(c + 1, u)
                    if at_least(c, 2) and u == 1:
                        epilogue_places(c - 2)
                    if at_least(c, 1):
                        if u == 2:
                            epilogue_weights(c - 1)
                        if u == 5:
                            epilogue_stats(c - 1)
                        if u == 7:
                            epilogue_norm(c - 1)
                        if u == 11:
                            epilogue_route(c - 1)
                        if u == 12:
                            epilogue_tails(c - 1)
                            assert k[0] == DVE_EP, k[0]

            dve.wait_ge(consts, 1)
            dve.wait_ge(gate_in, 32)
            chunk(0)
            chunk(1)
            with dve.Fori(2, G - 2) as c:
                chunk(c)
            m = [0]

            def step(ins):
                m[0] += 1
                ins.then_inc(sched_steps, 1)
                dve.wait_ge(sched_steps, m[0])

            dve.wait_ge(consts, 2)
            step(nc.vector.tensor_reduce(sched[:, 0:1], pad_pick[:, 1, :], axis=AX_X, op=ALU.add))
            step(nc.vector.tensor_tensor(pad_of[:, :], sched[:, 0:1], part_f[:, :], ALU.add))
            for j in range(2):
                step(nc.vector.tensor_scalar(pad_of2[:, j:j + 1], pad_of[:, :], 2.0, float(j), ALU.mult, ALU.add))
            chunk(G - 2)
            chunk(G - 1, last=True)
            epilogue_places(G - 2)
            c = G - 1
            epilogue_weights(c)
            dve.wait_ge(weights_ready, c + 1)
            step(nc.vector.tensor_tensor(mix[:, :, :], o_sb[:, :, 0:D], o_sb[:, :, D + 1:2 * D + 1], ALU.add))
            mix_output(c, nc.vector, step)
            epilogue_stats(c)
            epilogue_norm(c)
            dve.wait_ge(rows_hi_ready, c + 1)
            nc.vector.tensor_tensor(rows_lo, f2_twice, rows_hi, ALU.subtract).then_inc(rows_lo_ready, 1)
            epilogue_route(c)
            epilogue_places(c)
            epilogue_tails(c)
            assert k[0] == DVE_EP, k[0]

            step(nc.vector.tensor_scalar(ends_i[:, :], next_row[:, :], float(BLOCK - 1), None, ALU.add))
            step(nc.vector.tensor_scalar(ends_i[:, :], ends_i[:, :], BLOCK.bit_length() - 1, None, ALU.arith_shift_right))
            step(nc.vector.tensor_copy(ends[:, 1, :], ends_i[:, :]))
            step(nc.vector.tensor_copy(ends[:, 0, :], next_row[:, :]))
            step(nc.vector.tensor_tensor(pad_pick[:, :, :], ends[:, :, :], pad_e[:, :].unsqueeze(1).to_broadcast([P, 2, E]), ALU.mult))
            step(nc.vector.tensor_reduce(pad_end[:, :], pad_pick[:, :, :], axis=AX_X, op=ALU.add))
            step(nc.vector.tensor_tensor(pad_idx[:, 2:3], pad_end[:, 1:2], pad_of[:, :], ALU.add))
            step(nc.vector.tensor_tensor(pad_row[:, 0, :], pad_of2[:, :], pad_end[:, 0:1].to_broadcast([P, 2]), ALU.add))
            step(nc.vector.tensor_scalar(sched[:, 0:1], pad_end[:, 1:2], float(BLOCK), None, ALU.mult))
            step(nc.vector.tensor_tensor(pad_row[:, 1, :], pad_row[:, 0, :], sched[:, 0:1].to_broadcast([P, 2]), ALU.is_ge))
            step(nc.vector.tensor_scalar(pad_row[:, 1, :], pad_row[:, 1, :], float(NO_ROW), None, ALU.mult))
            nc.vector.tensor_tensor(pad_idx[:, 0:2], pad_row[:, 0, :], pad_row[:, 1, :], ALU.add).then_inc(pads_ready, 1)

            step(nc.vector.tensor_tensor(cum_f[:, :], next_row[:, :], start_f[:, :], ALU.subtract))
            step(nc.vector.tensor_scalar(tiles_i[:, :], cum_f[:, :], float(P - 1), None, ALU.add))
            step(nc.vector.tensor_scalar(tiles_i[:, :], tiles_i[:, :], P.bit_length() - 1, None, ALU.arith_shift_right))
            step(nc.vector.tensor_copy(tiles_f[:, :], tiles_i[:, :]))
            step(nc.vector.tensor_tensor(grid[:, :, :], tri_e[:, :, :], tiles_f[:, :].unsqueeze(1).to_broadcast([P, E, E]), ALU.mult))
            step(nc.vector.tensor_reduce(cum_f[:, :], grid[:, :, :], axis=AX_X, op=ALU.add))
            step(nc.vector.tensor_scalar(done_e[:, 0, :], cum_f[:, :], part_f[:, 0:1], None, ALU.is_le))
            step(nc.vector.tensor_tensor(done_e[:, 1, :], done_e[:, 0, :], tiles_f[:, :], ALU.mult))
            step(nc.vector.tensor_reduce(sched[:, 0:2], done_e[:, :, :], axis=AX_X, op=ALU.add))
            step(nc.vector.tensor_tensor(sched[:, 2:3], part_f[:, :], sched[:, 1:2], ALU.subtract))
            step(nc.vector.tensor_scalar(sched[:, 3:4], sched[:, 0:1], float(E), float(P), ALU.is_lt, ALU.mult))
            step(nc.vector.tensor_tensor(sched[:, 4:5], sched[:, 2:3], sched[:, 3:4], ALU.mult))
            step(nc.vector.tensor_scalar(sched[:, 5:6], sched[:, 0:1], float(REGION), None, ALU.mult))
            step(nc.vector.tensor_tensor(sched[:, 6:7], sched[:, 5:6], sched[:, 4:5], ALU.add))
            nc.vector.tensor_scalar(sched[:, 7:8], sched[:, 0:1], float(E - 1), None, ALU.min).then_inc(slots_ready, 1)
            dve.wait_ge(slots_ps, 1)
            nc.vector.tensor_copy(slot_table[:, :, :], misc[0][0:1, 0:2 * P].rearrange("p (k t) -> p k t", k=2)).then_inc(sched_done, 1)

            def expert(i, k8):
                if before(i, SLOTS):
                    dve.wait_ge(xt_ps, i + 1)
                    nc.vector.tensor_copy(xt_sb[:, k8 % 4, :], xt_bank[k8 % 4].bitcast(F16)).then_inc(xt_done, 1)
                    if at_least(i, 8):
                        dve.wait_ge(y_stored[k8 % 4], 4 * (i - k8 % 4) - 16)
                    nc.vector.tensor_copy(y_idx[:, k8:k8 + 1], x_rows[:, k8, D + 1:D + 2].bitcast(I32)).then_inc(idx_done, 1)
                if at_least(i, 1) and before(i, SLOTS + 1):
                    b4 = (k8 - 1) % 4
                    dve.wait_ge(act_done, i)
                    nc.vector.tensor_tensor(hid_sb[:, b4, :], act_sb[:, b4, :], bank[b4 % 2][:, H:2 * H], ALU.mult).then_inc(hid_done, 1)
                if at_least(i, 2):
                    b4 = (k8 - 2) % 4
                    dve.wait_ge(ht_hi_done, i - 1)
                    nc.vector.tensor_tensor(ht_lo[:, b4, :], bank[2 + b4 % 2][:, 0:H], ht_hi[:, b4, :], ALU.subtract).then_inc(ht_lo_done, 1)

            spread(dve, expert, SLOTS + 2, 8, 8, 2)

            for i in range(5):
                at = slice(CUTS[i] * D, CUTS[i + 1] * D)
                dve.wait_ge(ya_in[i], 16)
                nc.vector.tensor_tensor(x_sb[:, at], x_sb[:, at], ya_sb[:, at], ALU.add).then_inc(sum_a, 1)
                dve.wait_ge(yb_in[i], 16)
                dve.wait_ge(sum_a, i + 1)
                nc.vector.tensor_tensor(x_sb[:, at], x_sb[:, at], yb_sb[:, at], ALU.add).then_inc(sum_done, 1)


_INS = ["x", "adj", "L0_gnn_Wq", "L0_gnn_Wk", "L0_ffn_gate_w", "L0_ffn_gate_b", "L0_ffn_w1", "L0_ffn_w2", "L0_ffn_w3"]


def kernel(**inputs):
    import numpy as _np
    import concourse.bacc as _bacc
    from concourse import mybir as _mybir
    from concourse.bass_utils import run_bass_kernel_spmd as _run

    nc = _bacc.Bacc("TRN2", target_bir_lowering=False, num_devices=1)
    arrays, args = {}, []
    for name in _INS:
        a = _np.ascontiguousarray(inputs[name])
        arrays[f"in_{name}_dram"] = a
        args.append(nc.dram_tensor(f"in_{name}_dram", a.shape, _mybir.dt.from_np(a.dtype), kind="ExternalInput").ap())
    result = nc.dram_tensor("out_dram", inputs["x"].shape, _mybir.dt.float32, kind="ExternalOutput").ap()
    graph_attention_moe(nc, *args, result)
    r = _run(nc, [arrays], core_ids=[0])
    return r.results[0]["out_dram"]
```

```python
from contextlib import ExitStack

import concourse.bass as bass
from concourse import mybir

F32 = mybir.dt.float32
F16 = mybir.dt.float16
I32 = mybir.dt.int32
U32 = mybir.dt.uint32
ALU = mybir.AluOpType
ACT = mybir.ActivationFunctionType
AX_X = mybir.AxisListType.X

P = 128
LN_EPS = 1e-5
COS_EPS = 1e-4
MASKED = -30000.0
NO_ROW = 1 << 20


def spread(eng, body, count, unroll, lead, trail, done=0):
    turns = (count - trail - lead) // unroll
    for i in range(done, lead):
        body(i, i % unroll)
    if turns > 0:
        with eng.Fori(0, turns) as turn:
            for k in range(unroll):
                body(turn * unroll + (lead + k), (lead + k) % unroll)
    for i in range(lead + max(turns, 0) * unroll, count):
        body(i, i % unroll)


def at_least(i, n):
    return not isinstance(i, int) or i >= n


def before(i, n):
    return not isinstance(i, int) or i < n


def graph_attention_moe(nc, x, adj, Wq, Wk, gate_w, gate_b, w1, w2, w3, out):
    N, D = x.shape
    E, _, H = w1.shape
    T = -(-N // P)
    NP = T * P
    G = T // 2
    CH = 2 * P
    LAST = N - (T - 1) * P
    LAST16 = LAST // 16 * 16
    assert D == P and Wq.shape[0] == P and T % 2 == 0 and H == 2 * P and 0 < LAST < P and LAST > LAST16
    ROW = D + 2
    REGION = NP + P
    SLOTS = (2 * NP + E * (P - 1)) // P
    EARLY = ((G - 2) * 2 * CH - E * (P - 1)) // P
    EARLY -= (EARLY - SLOTS) % 8
    BLOCK = P // (P // E)
    PARTS = [0, 4, 14, T]
    BY_VECTOR = [(0, 10), (14, 20)]
    AW = 2 * D + 2
    SEGS = [0, 4, 7, 10, G]
    AHEAD, BEHIND = SEGS[1], 3
    BUF = [u % 3 for u in range(G - 1)] + [3]
    assert G % 3 == 1 and REGION % BLOCK == 0 and SLOTS <= P and BLOCK == 16

    with ExitStack() as ctx:
        def sb(name, shape, dt):
            return ctx.enter_context(nc.sbuf_tensor(name, shape, dt))

        def sem(name):
            return ctx.enter_context(nc.semaphore(name))

        routed = nc.dram_tensor("routed_rows", [(E + 1) * REGION, ROW], F32).ap()
        expert_out = nc.dram_tensor("expert_rows", [2 * NP, D], F32).ap()

        x_sb = sb("x_sb", [P, T * D], F32)
        f_sb = sb("f_sb", [P, T * D], F32)
        f_aug = sb("f_aug", [P, T, AW], F16)
        qk_hi = sb("qk_hi", [P, G, 2, CH], F16)
        qk_lo = sb("qk_lo", [P, G, 2, CH], F16)
        adj_sb = sb("adj_sb", [P, 2, NP], I32)
        mask = sb("mask", [P, 2, NP], F16)
        p_full = sb("p_full", [P, 4, 2 * CH], F32)
        p_hi = sb("p_hi", [P, 4, 2 * CH], F16)
        p_lo = sb("p_lo", [P, 4, 2 * CH], F16)
        w12_hi = sb("w12_hi", [P, E, 2 * H], F16)
        w12_lo = sb("w12_lo", [P, E, 2 * H], F16)
        w3_hi = sb("w3_hi", [P, E, 2 * D], F16)
        w3_lo = sb("w3_lo", [P, E, 2 * D], F16)
        w_raw = sb("w_raw", [P, 4, H], F32)
        id32 = sb("id32", [P, P], F32)
        id16 = sb("id16", [P, P], F16)
        before16 = sb("before16", [P, P], F16)
        ones16 = sb("ones16", [P, P], F16)
        wqk = sb("wqk", [P, 2, D], F32)
        wqk_t = sb("wqk_t", [P, 2 * P], F32)
        gate_sb = sb("gate_sb", [P, E], F32)
        gate_bias = sb("gate_bias", [P, E], F32)
        expert_i = sb("expert_i", [P, E], I32)
        expert_f = sb("expert_f", [P, E], F32)
        start_f = sb("start_f", [P, E], F32)
        base_f = sb("base_f", [P, E], F32)
        next_row = sb("next_row", [P, E], F32)
        dest_i = sb("dest_i", [P, 2, 2], I32)
        dest_f = sb("dest_f", [P, 2, 2], F32)
        neg_half = sb("neg_half", [P, T], F32)
        stats = sb("stats", [P, T, 6], F32)
        mean_var = sb("mean_var", [P, T, 2], F32)
        var_eps = sb("var_eps", [P, T], F32)
        rstd = sb("rstd", [P, T], F32)
        neg_mean = sb("neg_mean", [P, T], F32)
        shift = sb("shift", [P, T], F32)
        ft_sb = p_full[:, 0:1, :].rearrange("p a (b n) -> p (a b) n", b=2)
        sq_sb = p_full[:, 1, :]
        qn_sb = p_full[:, 2:4, :]
        ss = sb("ss", [P, 2, 4], F32)
        ss_max = sb("ss_max", [P, 2, 4], F32)
        rnorm = sb("rnorm", [P, 2, 4], F32)
        o_sb = sb("o_sb", [P, 2, 2 * D + 1], F32)
        mix = sb("mix", [P, 2, D], F32)
        keep = sb("keep", [P, 2, D], F32)
        small = sb("small", [P, 16, 2], F32)
        stats2 = sb("stats2", [P, 2, 6], F32)
        mean_var2 = sb("mean_var2", [P, 2, 2], F32)
        f2 = sb("f2", [P, 2, D], F32)
        f2_t = sb("f2_t", [P, CH], F32)
        logits = sb("logits", [P, 2, E], F32)
        top_v = sb("top_v", [P, 2, 8], F32)
        top_i = sb("top_i", [P, 2, 8], U32)
        top_f = sb("top_f", [P, 2, 2], F32)
        one_hot = sb("one_hot", [P, 4, E], F32)
        one_hot_sum = sb("one_hot_sum", [P, 2, E], F16)
        row_of = sb("row_of", [P, 2, E], F32)
        row_pick = sb("row_pick", [P, 4, E], F32)
        row_f = sb("row_f", [P, 4], F32)
        row_i = sb("row_i", [P, 4], I32)
        rows = sb("rows", [P, 4, ROW], F32)
        pad_rows = sb("pad_rows", [P, BLOCK, ROW], F32)
        tri_e = sb("tri_e", [P, E, E], F32)
        grid = sb("grid", [P, E, E], F32)
        part_i = sb("part_i", [P, 4], I32)
        part_f = sb("part_f", [P, 1], F32)
        pad_of = sb("pad_of", [P, 1], F32)
        pad_of2 = sb("pad_of2", [P, 2], F32)
        pad_e = sb("pad_e", [P, E], F32)
        ends = sb("ends", [P, 2, E], F32)
        ends_i = sb("ends_i", [P, E], I32)
        pad_pick = sb("pad_pick", [P, 2, E], F32)
        pad_end = sb("pad_end", [P, 2], F32)
        pad_row = sb("pad_row", [P, 2, 2], F32)
        pad_idx = sb("pad_idx", [P, 3], I32)
        tiles_i = sb("tiles_i", [P, E], I32)
        tiles_f = sb("tiles_f", [P, E], F32)
        cum_f = sb("cum_f", [P, E], F32)
        done_e = sb("done_e", [P, 2, E], F32)
        taken = sb("taken", [P, 2, E], F32)
        at_expert = sb("at_expert", [P, 2, E], F32)
        euler = sb("euler", [P, 2], F32)
        sched = sb("sched", [P, 8], F32)
        slot_table = sb("slot_table", [1, 2, P], I32)
        y_idx = sb("y_idx", [P, 8], I32)
        y_gate = sb("y_gate", [P, 8], F32)
        adj_f = adj_sb[:, :, :].bitcast(F32).rearrange("p a n -> p (a n)")
        x_rows = adj_f[:, 0:8 * ROW].rearrange("p (b n) -> p b n", b=8)
        y_sb = adj_f[:, 2048:2048 + 8 * D].rearrange("p (b n) -> p b n", b=8)
        act_sb = adj_f[:, 3072:3072 + 4 * H].rearrange("p (b n) -> p b n", b=4)
        hid_sb = adj_f[:, 4096:4096 + 4 * H].rearrange("p (b n) -> p b n", b=4)
        mask_flat = mask[:, :, :].rearrange("p a n -> p (a n)")
        xt_sb = mask_flat[:, 0:4 * CH].rearrange("p (b n) -> p b n", b=4)
        ht_hi = mask_flat[:, 1024:1024 + 4 * H].rearrange("p (b n) -> p b n", b=4)
        ht_lo = mask_flat[:, 2048:2048 + 4 * H].rearrange("p (b n) -> p b n", b=4)
        ya_sb = qk_hi[:, :, :, :].rearrange("p g a n -> p (g a n)").bitcast(F32)
        yb_sb = qk_lo[:, :, :, :].rearrange("p g a n -> p (g a n)").bitcast(F32)

        bank = [ctx.enter_context(nc.psum_tensor(f"bank{i}", [P, 512], F32)) for i in range(4)]
        o_ps = ctx.enter_context(nc.psum_tensor("o_ps", [P, 2, 512], F32))
        misc = [ctx.enter_context(nc.psum_tensor(f"misc{i}", [P, 512], F32)) for i in range(2)]

        xt_bank = [misc[0][:, b * P:(b + 1) * P] for b in range(4)]
        f2t_bank = misc[1][:, 0:CH]
        slots_bank = [misc[0][0:1, 0:2 * P], misc[1][0:1, 0:2 * P]]
        logits_bank, rank_bank = misc[1][:, CH:CH + 2 * E], misc[1][:, CH + P // 2:CH + P // 2 + 3 * E]
        y_bank = [o_ps[:, b % 2, b // 2 * D:(b // 2 + 1) * D] for b in range(4)]

        x_in = [sem(f"x_in{i}") for i in range(len(PARTS) - 1)]
        w_in, gate_in = sem("w_in"), sem("gate_in")
        adj_in = [sem(f"adj_in{s}") for s in range(len(SEGS) - 1)]
        w_raw_in, w_hi_done, w_lo_done = sem("w_raw_in"), sem("w_hi_done"), sem("w_lo_done")
        waited = sem("waited")
        x_padded, adj_padded, const_steps, consts = sem("x_padded"), sem("adj_padded"), sem("const_steps"), sem("consts")
        stats_done, aggr_done, var_done, rstd_done = sem("stats_done"), sem("aggr_done"), sem("var_done"), sem("rstd_done")
        id_ready, shift_done = sem("id_ready"), sem("shift_done")
        f_done, f_done2 = sem("f_done"), sem("f_done2")
        f_hi_done, f_lo_done = sem("f_hi_done"), sem("f_lo_done")
        wt_ps, wt_done = sem("wt_ps"), sem("wt_done")
        ft_ps, ft_copied, proj_ps, squared = sem("ft_ps"), sem("ft_copied"), sem("proj_ps"), sem("squared")
        ss_summed, ss_clamped, rnorm_done = sem("ss_summed"), sem("ss_clamped"), sem("rnorm_done")
        qn_scaled, qt_ps, q_hi_done, q_lo_done = sem("qn_scaled"), sem("qt_ps"), sem("q_hi_done"), sem("q_lo_done")
        mask0_done = sem("mask0_done")
        mask_done, s_done, p_done, p_hi_done = sem("mask_done"), sem("s_done"), sem("p_done"), sem("p_hi_done")
        p_lo_done, pv_done, o_evac = sem("p_lo_done"), sem("pv_done"), sem("o_evac")
        pool_ep, dve_ep = sem("pool_ep"), sem("dve_ep")
        weights_ready, x2_ready, var2_ready, rstd2_ready = sem("weights_ready"), sem("x2_ready"), sem("var2_ready"), sem("rstd2_ready")
        f2_ready, gap_ready, one_hot_ready = sem("f2_ready"), sem("gap_ready"), sem("one_hot_ready")
        tails_ready, places_ready, place_steps = sem("tails_ready"), sem("places_ready"), sem("place_steps")
        rows_free, rows_hi_ready, rows_lo_ready = sem("rows_free"), sem("rows_hi_ready"), sem("rows_lo_ready")
        f2t_ps, f2t_done, logits_ps, gate_exp, rank_ps = sem("f2t_ps"), sem("f2t_done"), sem("logits_ps"), sem("gate_exp"), sem("rank_ps")
        rows_stored, pad_stored = sem("rows_stored"), sem("pad_stored")
        sched_steps, slots_ready, slots_ps, sched_done, pads_ready = sem("sched_steps"), sem("slots_ready"), sem("slots_ps"), sem("sched_done"), sem("pads_ready")
        x_rows_in = [sem(f"x_rows_in{b}") for b in range(8)]
        tail_done = sem("tail_done")
        xt_ps, xt_done, h_ps, act_done, hid_done = sem("xt_ps"), sem("xt_done"), sem("h_ps"), sem("act_done"), sem("hid_done")
        ht_ps, ht_hi_done, ht_lo_done, y_ps, y_done = sem("ht_ps"), sem("ht_hi_done"), sem("ht_lo_done"), sem("y_ps"), sem("y_done")
        y_stored = [sem(f"y_stored{b}") for b in range(8)]
        ya_in = [sem(f"ya_in{i}") for i in range(5)]
        yb_in = [sem(f"yb_in{i}") for i in range(5)]
        CUTS = [0, 5, 10, 15, 20, T]
        sum_a, sum_done, out_stored = sem("sum_a"), sem("sum_done"), sem("out_stored")

        POOL_EP = 4
        DVE_EP = 18
        PLACE_STEPS = 4

        def proj_bank(g):
            return bank[(g - G) % 4]

        def normed(n):
            by_vector = sum(max(0, min(b, n) - a) for a, b in BY_VECTOR)
            return by_vector, n - by_vector

        def wait_alone(eng, what, value):
            eng.wait_ge(what, value)
            if not isinstance(value, int):
                eng.sem_inc(waited, 1)

        def load_values(eng, row, t, count, max_val):
            _, values = nc.values_load_multi_w_load_instructions(
                slot_table[0:1, row, bass.ds(t, count)], engines=[eng], min_val=0, max_val=max_val,
                skip_runtime_bounds_check_because="VectorE made the table, with experts clamped and rows inside their regions")
            return values

        block = ctx.enter_context(nc.Block())

        @block.sync
        def _(sp):
            for i in range(len(PARTS) - 1):
                a, b = PARTS[i], min(PARTS[i + 1], T - 1)
                sp.dma_start(x_sb[:, a * D:b * D].rearrange("p (t d) -> p t d", d=D),
                             x[a * P:b * P, :].rearrange("(t p) d -> p t d", p=P)).then_inc(x_in[i], 16)
                if i == 0:
                    sp.dma_start(wqk[:, 0, :], Wq[:, :]).then_inc(w_in, 16)
                    sp.dma_start(wqk[:, 1, :], Wk[:, :]).then_inc(w_in, 16)
            sp.wait_ge(x_padded, 1)
            for a, b in ((0, LAST16), (LAST16, LAST)):
                sp.dma_start(x_sb[a:b, (T - 1) * D:], x[(T - 1) * P + a:(T - 1) * P + b, :]).then_inc(x_in[-1], 16)
            sp.dma_start(gate_sb[:, :], gate_w[:, :]).then_inc(gate_in, 16)
            sp.dma_start(gate_bias[:, :], gate_b.rearrange("(a e) -> a e", a=1).to_broadcast([P, E])).then_inc(gate_in, 16)

            def load_adj(c, last=False):
                for s in range(len(SEGS) - 1):
                    a, b = SEGS[s] * CH, min(SEGS[s + 1] * CH, N)
                    if isinstance(c, int) and c == 1:
                        sp.wait_ge(mask0_done, SEGS[s + 1])
                    elif at_least(c, 2):
                        wait_alone(sp, mask_done, (c - 2) * G + SEGS[s + 1])
                    if last:
                        r = c * CH
                        sp.dma_start(adj_sb[:, 0, a:b], adj[r:r + P, a:b]).then_inc(adj_in[s], 16)
                        sp.dma_start(adj_sb[0:LAST16, 1, a:b], adj[r + P:r + P + LAST16, a:b]).then_inc(adj_in[s], 16)
                        sp.dma_start(adj_sb[LAST16:LAST, 1, a:b], adj[r + P + LAST16:N, a:b]).then_inc(adj_in[s], 16)
                    else:
                        sp.dma_start(adj_sb[:, :, a:b],
                                     adj[bass.ds(c * CH, CH), a:b].rearrange("(i p) n -> p i n", p=P)).then_inc(adj_in[s], 16)

            sp.wait_ge(adj_padded, 1)
            load_adj(0)
            load_adj(1)
            with sp.Fori(2, G - 1) as c:
                load_adj(c)
            load_adj(G - 1, last=True)
            def load_rows(t, b, at):
                if at_least(t, 8):
                    wait_alone(sp, xt_ps, t - 7)
                    wait_alone(sp, tail_done, t - 7)
                sp.dma_start(x_rows[:, b, :], routed[bass.ds(at, P), :]).then_inc(x_rows_in[b], 16)

            def load_tiles(t, b, count):
                at = load_values(mybir.EngineType.SP, 0, t, count, (E + 1) * REGION - P)
                for k in range(count):
                    load_rows(t + k, (b + k) % 8, at[k])

            sp.wait_ge(mask_done, (G - 1) * G)
            sp.wait_ge(rows_stored, 16 * 4 * (G - 2))
            sp.wait_ge(sched_done, 1)
            for t in range(0, EARLY, 8):
                load_tiles(t, 0, min(8, EARLY - t))
            sp.wait_ge(rows_stored, 16 * 4 * G)
            sp.wait_ge(pad_stored, 16 * 4)
            sp.wait_ge(sched_done, 2)
            with sp.Fori(0, (SLOTS - EARLY) // 8) as turn:
                load_tiles(turn * 8 + EARLY, EARLY % 8, 8)
            assert (SLOTS - EARLY) % 8 == 0
            for b in range(8):
                sp.wait_ge(y_stored[b], 16 * len(range(b, SLOTS, 8)))
            for i in reversed(range(5)):
                a, b = CUTS[i], CUTS[i + 1]
                sp.dma_start(ya_sb[:, a * D:b * D].rearrange("p (t d) -> p t d", d=D),
                             expert_out[a * P:b * P, :].rearrange("(t p) d -> p t d", p=P)).then_inc(ya_in[i], 16)
            for n, i in enumerate(reversed(range(5))):
                a, b = CUTS[i], min(CUTS[i + 1], T - 1)
                sp.wait_ge(sum_done, n + 1)
                sp.dma_start(out[a * P:b * P, :].rearrange("(t p) d -> p t d", p=P),
                             x_sb[:, a * D:b * D].rearrange("p (t d) -> p t d", d=D)).then_inc(out_stored, 16)
                if i == 4:
                    for a, b in ((0, LAST16), (LAST16, LAST)):
                        sp.dma_start(out[(T - 1) * P + a:(T - 1) * P + b, :], x_sb[a:b, (T - 1) * D:]).then_inc(out_stored, 16)
            sp.wait_ge(out_stored, 16 * 7)

        def mix_output(c, ns, ep):
            xc = x_sb[:, bass.ds(c * CH, CH)].rearrange("p (a d) -> p a d", a=2)
            fc = f_sb[:, bass.ds(c * CH, CH)].rearrange("p (a d) -> p a d", a=2)
            wide = [P, 2, D]
            ep(ns.tensor_tensor(mix[:, :, :], mix[:, :, :], small[:, 3, :].unsqueeze(2).to_broadcast(wide), ALU.mult))
            ep(ns.tensor_tensor(keep[:, :, :], fc, small[:, 4, :].unsqueeze(2).to_broadcast(wide), ALU.mult))
            ep(ns.tensor_tensor(mix[:, :, :], mix[:, :, :], keep[:, :, :], ALU.add))
            ns.tensor_tensor(xc, xc, mix[:, :, :], ALU.add).then_inc(x2_ready, 1)

        def weight_parts(kind, e):
            if kind < 2:
                return [t[:, bass.ds(e, 4), kind * H:(kind + 1) * H] for t in (w12_hi, w12_lo)]
            return [t[:, bass.ds(e, 4), :] for t in (w3_hi, w3_lo)]

        rows_hi = rows[:, :, 0:D // 2].bitcast(F16).rearrange("p (a k) d -> p a k d", a=2)
        rows_lo = rows[:, :, D // 2:D].bitcast(F16).rearrange("p (a k) d -> p a k d", a=2)
        f2_twice = f2[:, :, :].unsqueeze(2).to_broadcast([P, 2, 2, D])

        @block.gpsimd
        def _(pool):
            n = [0]

            def step(ins):
                n[0] += 1
                ins.then_inc(const_steps, 1)
                pool.wait_ge(const_steps, n[0])

            nc.gpsimd.memset(x_sb[:, (T - 1) * D:], 0.0).then_inc(x_padded, 1)
            nc.gpsimd.memset(adj_sb[:, :, N:NP], 0).then_inc(adj_padded, 1)
            step(nc.gpsimd.memset(neg_half[:, :], -0.5))
            step(nc.gpsimd.memset(id32[:, :], 0.0))
            nc.gpsimd.affine_select(out=id32[:, :], in_=id32[:, :], compare_op=ALU.not_equal, fill=1.0,
                                    base=0, pattern=[[-1, P]], channel_multiplier=1).then_inc(id_ready, 1)
            step(nc.gpsimd.memset(f_aug[:, :, D:D + 1], 1.0))
            step(nc.gpsimd.memset(ones16[:, :], 1.0))
            step(nc.gpsimd.affine_select(out=before16[:, :], in_=ones16[:, :], compare_op=ALU.is_gt, fill=0.0,
                                         base=0, pattern=[[1, P]], channel_multiplier=-1))
            pool.wait_ge(id_ready, 1)
            step(nc.gpsimd.tensor_copy(id16[:, :], id32[:, :]))
            step(nc.gpsimd.iota(expert_i[:, :], pattern=[[1, E]], base=0, channel_multiplier=0))
            step(nc.gpsimd.tensor_copy(expert_f[:, :], expert_i[:, :]))
            step(nc.gpsimd.tensor_scalar(start_f[:, :], expert_f[:, :], float(REGION), 0.0, ALU.mult, ALU.add))
            step(nc.gpsimd.tensor_copy(next_row[:, :], start_f[:, :]))
            step(nc.gpsimd.tensor_copy(base_f[:, :], start_f[:, :]))
            step(nc.gpsimd.memset(euler[:, :], 2.718281828459045))
            step(nc.gpsimd.iota(dest_i[:, :, :], pattern=[[P, 2], [NP, 2]], base=0, channel_multiplier=1))
            nc.gpsimd.tensor_copy(dest_f[:, :, :], dest_i[:, :, :]).then_inc(consts, 1)

            def rstd_part(i):
                pool.wait_ge(var_done, i + 1)
                at = slice(PARTS[i], PARTS[i + 1])
                nc.gpsimd.tensor_tensor(rstd[:, at], var_eps[:, at], neg_half[:, at], ALU.pow).then_inc(rstd_done, 1)
                if i > 0:
                    pool.wait_ge(rstd_done, i + 1)
                    nc.gpsimd.tensor_tensor(shift[:, at], neg_mean[:, at], rstd[:, at], ALU.mult).then_inc(shift_done, 1)

            def norms(g, b):
                pool.wait_ge(ss_clamped, g + 1)
                if at_least(g, 2):
                    pool.wait_ge(qn_scaled, g - 1)
                nc.gpsimd.tensor_tensor(rnorm[:, b, :], ss_max[:, b, :], neg_half[:, 0:4], ALU.pow).then_inc(rnorm_done, 1)

            for i in range(len(PARTS) - 1):
                rstd_part(i)
            spread(pool, norms, G, 2, 2, 1)

            def f_low(g):
                pool.wait_ge(f_hi_done, next(i for i in range(1, len(PARTS)) if 2 * g + 2 <= PARTS[i]))
                two = f_aug[:, 2 * g:2 * g + 2, :]
                nc.gpsimd.tensor_tensor(two[:, :, D + 1:2 * D + 1], f_sb[:, g * CH:(g + 1) * CH].rearrange("p (a d) -> p a d", a=2),
                                        two[:, :, 0:D], ALU.subtract).then_inc(f_lo_done, 1)

            for g in range(G):
                f_low(g)

            step(nc.gpsimd.memset(pad_rows[:, :, :], 0.0))
            step(nc.gpsimd.memset(pad_rows[:, :, D + 1:D + 2].bitcast(I32), NO_ROW))
            step(nc.gpsimd.memset(tri_e[:, :, :], 1.0))
            step(nc.gpsimd.affine_select(out=tri_e[:, :, :], in_=tri_e[:, :, :], compare_op=ALU.is_ge, fill=0.0,
                                         base=0, pattern=[[1, E], [-1, E]], channel_multiplier=0))
            step(nc.gpsimd.iota(part_i[:, 0:1], pattern=[[0, 1]], base=0, channel_multiplier=1))
            step(nc.gpsimd.tensor_copy(part_f[:, :], part_i[:, 0:1]))
            per = P // E
            step(nc.gpsimd.memset(pad_e[:, :], 1.0))
            step(nc.gpsimd.affine_select(out=pad_e[:, :], in_=pad_e[:, :], compare_op=ALU.is_ge, fill=0.0,
                                         base=0, pattern=[[-per, E]], channel_multiplier=1))
            step(nc.gpsimd.affine_select(out=pad_e[:, :], in_=pad_e[:, :], compare_op=ALU.is_ge, fill=0.0,
                                         base=per - 1, pattern=[[per, E]], channel_multiplier=-1))
            step(nc.gpsimd.tensor_tensor(pad_pick[:, 0, :], pad_e[:, :], expert_f[:, :], ALU.mult))
            nc.gpsimd.tensor_scalar(pad_pick[:, 1, :], pad_pick[:, 0, :], float(-per), 0.0, ALU.mult, ALU.add).then_inc(consts, 1)
            pool.dma_start(routed[E * REGION:E * REGION + P, :], pad_rows[:, 0, :]).then_inc(pad_stored, 16)

            def attention_output(c):
                k = [0]

                def ep(ins):
                    k[0] += 1
                    ins.then_inc(pool_ep, 1)
                    pool.wait_ge(pool_ep, c * POOL_EP + k[0])

                pool.wait_ge(o_evac, c + 1)
                ep(nc.gpsimd.tensor_tensor(mix[:, :, :], o_sb[:, :, 0:D], o_sb[:, :, D + 1:2 * D + 1], ALU.add))
                pool.wait_ge(weights_ready, c + 1)
                mix_output(c, nc.gpsimd, ep)
                assert k[0] == POOL_EP
                if at_least(c, 1):
                    scatter_rows(c - 1, 0)
                pool.wait_ge(var2_ready, c + 1)
                nc.gpsimd.tensor_tensor(small[:, 6, :], small[:, 5, :], neg_half[:, 0:2], ALU.pow).then_inc(rstd2_ready, 1)
                if at_least(c, 1):
                    scatter_rows(c - 1, 1)

            def epilogue(c, kind, e):
                attention_output(c)
                if kind < 2:
                    pool.dma_start(w_raw[:, :, :], (w1, w2)[kind][bass.ds(e, 4)].rearrange("e d h -> d e h")).then_inc(w_raw_in, 16)
                else:
                    pool.dma_start(w_raw[:, :, :].rearrange("p e (c o) -> p e c o", c=2),
                                   w3[bass.ds(e, 4)].rearrange("e (c p) o -> p e c o", p=P)).then_inc(w_raw_in, 16)
                free_rows(c)
                pool.wait_ge(rows_hi_ready, c + 1)
                nc.gpsimd.tensor_tensor(rows_lo, f2_twice, rows_hi, ALU.subtract).then_inc(rows_lo_ready, 1)
                pool.wait_ge(w_hi_done, c + 1)
                hi, lo = weight_parts(kind, e)
                nc.gpsimd.tensor_tensor(lo, w_raw[:, :, :], hi, ALU.subtract).then_inc(w_lo_done, 1)
                pool.wait_ge(w_lo_done, c + 1)

            def scatter_rows(c, half):
                if half == 0:
                    wait_alone(pool, rows_lo_ready, c + 1)
                    wait_alone(pool, tails_ready, c + 1)
                    wait_alone(pool, places_ready, c + 1)
                for j in (2 * half, 2 * half + 1):
                    pool.indirect_dma_start(out=routed[:, :], out_offset=bass.IndirectOffsetOnAxis(ap=row_i[:, j:j + 1], axis=0),
                                            in_=rows[:, j, :], in_offset=None).then_inc(rows_stored, 16)

            def free_rows(c):
                if at_least(c, 1):
                    pool.wait_ge(rows_stored, 64 * c)
                pool.sem_inc(rows_free, 1)

            assert G - 1 == 3 * (E // 4)
            for kind in range(3):
                epilogue(kind, kind, 0)
            with pool.Fori(1, E // 4) as lot:
                for kind in range(3):
                    epilogue(lot * 3 + kind, kind, lot * 4)
            c = G - 1
            attention_output(c)
            free_rows(c)

            def store_rows(t, b):
                wait_alone(pool, tail_done, t + 1)
                wait_alone(pool, y_done, t + 1)
                pool.indirect_dma_start(out=expert_out[:, :],
                                        out_offset=bass.IndirectOffsetOnAxis(ap=y_idx[:, b:b + 1], axis=0),
                                        in_=y_sb[:, b, :], in_offset=None,
                                        bounds_check=2 * NP - 1, oob_is_err=False).then_inc(y_stored[b], 16)

            def store_padding():
                pool.wait_ge(pads_ready, 1)
                pool.indirect_dma_start(out=routed[:, :].rearrange("(b r) n -> b (r n)", r=BLOCK),
                                        out_offset=bass.IndirectOffsetOnAxis(ap=pad_idx[:, 2:3], axis=0),
                                        in_=pad_rows[:, :, :].rearrange("p r n -> p (r n)"), in_offset=None).then_inc(pad_stored, 16)
                for j in range(2):
                    pool.indirect_dma_start(out=routed[:, :], out_offset=bass.IndirectOffsetOnAxis(ap=pad_idx[:, j:j + 1], axis=0),
                                            in_=pad_rows[:, 0, :], in_offset=None,
                                            bounds_check=(E + 1) * REGION - 1, oob_is_err=False).then_inc(pad_stored, 16)

            for t in range(EARLY):
                store_rows(t, t % 8)
                if t == 6:
                    pool.wait_ge(gap_ready, c + 1)
                    nc.gpsimd.tensor_tensor(small[:, 8, :], euler[:, :], small[:, 7, :], ALU.pow).then_inc(gate_exp, 1)
                if t == 7:
                    pool.wait_ge(rows_hi_ready, c + 1)
                    nc.gpsimd.tensor_tensor(rows_lo, f2_twice, rows_hi, ALU.subtract).then_inc(rows_lo_ready, 1)
                if t == 11:
                    scatter_rows(c, 0)
                if t == 12:
                    scatter_rows(c, 1)
                if t == 14:
                    store_padding()
            spread(pool, store_rows, SLOTS, 8, EARLY, 0, done=EARLY)

        @block.tensor
        def _(pe):
            pe.wait_ge(id_ready, 1)
            pe.wait_ge(w_in, 32)
            for k in range(2):
                last = nc.tensor.transpose(misc[0][:, k * P:(k + 1) * P], wqk[:, k, :], id32[:, :])
            last.then_inc(wt_ps, 1)
            pe.wait_ge(wt_done, 1)

            def project(i, b):
                o = 1 - b
                if i < G:
                    by_vector, by_scalar = normed(2 * i + 2)
                    if any(a <= 2 * i < b for a, b in BY_VECTOR):
                        pe.wait_ge(f_done, by_vector)
                    else:
                        pe.wait_ge(f_done2, by_scalar)
                    if i >= 2:
                        pe.wait_ge(ft_copied, i - 1)
                    for k in range(2):
                        last = nc.tensor.transpose(misc[b][:, k * P:(k + 1) * P],
                                                   f_sb[:, (2 * i + k) * D:(2 * i + k + 1) * D], id32[:, :])
                    last.then_inc(ft_ps, 1)
                if 1 <= i < G + 1:
                    g = i - 1
                    pe.wait_ge(ft_copied, g + 1)
                    for k in range(2):
                        last = nc.tensor.matmul(proj_bank(g)[:, k * CH:(k + 1) * CH], ft_sb[:, o, k * P:(k + 1) * P],
                                                wqk_t[:, :], start=True, stop=True)
                    last.then_inc(proj_ps, 1)
                if i >= 3:
                    g = i - 3
                    pe.wait_ge(qn_scaled, g + 1)
                    if g >= 2:
                        pe.wait_ge(q_lo_done, g - 1)
                    for a in range(2):
                        for k in range(2):
                            last = nc.tensor.transpose(o_ps[:, o, (2 * k + a) * P:(2 * k + a + 1) * P],
                                                       qn_sb[:, o, (2 * a + k) * P:(2 * a + k + 1) * P], id32[:, :])
                    last.then_inc(qt_ps, 1)

            def scores(c, u):
                if isinstance(c, int) and c == 0:
                    pe.wait_ge(q_lo_done, u + 1)
                    pe.wait_ge(mask0_done, u + 1)
                else:
                    pe.wait_ge(mask_done, (c - 1) * G + u + 1)
                s = bank[BUF[u]]
                k_hi = qk_hi[:, bass.ds(c, 1), 1, :]
                k_lo = qk_lo[:, bass.ds(c, 1), 1, :]
                for j in range(2):
                    to = s[:, j * CH:(j + 1) * CH]
                    q_hi = qk_hi[:, u, 0, j * P:(j + 1) * P]
                    q_lo = qk_lo[:, u, 0, j * P:(j + 1) * P]
                    nc.tensor.matmul(to, q_hi, k_hi, start=True, stop=False)
                    nc.tensor.matmul(to, q_hi, k_lo, start=False, stop=False)
                    nc.tensor.matmul(to, q_lo, k_hi, start=False, stop=False)
                    for a in range(2):
                        key = (2 * u + j) * P
                        last = nc.tensor.matmul(s[:, j * CH + a * P:j * CH + (a + 1) * P], mask[:, a, key:key + P],
                                                id16[:, :], start=False, stop=(a == 1))
                last.then_inc(s_done, 1)

            for i in range(G + 3):
                project(i, i % 2)
                if i == G:
                    pe.wait_ge(consts, 1)
                    scores(0, 0)
                if i == G + 1:
                    scores(0, 1)
            pe.wait_ge(gate_in, 32)

            def values(c, u):
                if u == 0 and at_least(c, 1):
                    pe.wait_ge(o_evac, c)
                pe.wait_ge(p_lo_done, c * G + u + 1)
                if isinstance(c, int) and c == 0:
                    pe.wait_ge(f_lo_done, u + 1)
                    if u == 0:
                        pe.wait_ge(q_lo_done, G)
                b = BUF[u]
                for a in range(2):
                    for j in range(2):
                        at = slice(j * CH + a * P, j * CH + (a + 1) * P)
                        first, final = u == 0 and j == 0, u == G - 1 and j == 1
                        f = f_aug[:, 2 * u + j, :]
                        nc.tensor.matmul(o_ps[:, a, 0:2 * D + 1], p_hi[:, b, at], f[:, 0:2 * D + 1], start=first, stop=False)
                        last = nc.tensor.matmul(o_ps[:, a, 0:D + 1], p_lo[:, b, at], f[:, 0:D + 1], start=False, stop=final)
                last.then_inc(pv_done, 1)

            def transpose_f2(c):
                pe.wait_ge(f2_ready, c + 1)
                for a in range(2):
                    last = nc.tensor.transpose(f2t_bank[:, a * P:(a + 1) * P], f2[:, a, :], id32[:, :])
                last.then_inc(f2t_ps, 1)

            def gate_logits(c):
                pe.wait_ge(f2t_done, c + 1)
                for a in range(2):
                    last = nc.tensor.matmul(logits_bank[:, a * E:(a + 1) * E], f2_t[:, a * P:(a + 1) * P], gate_sb[:, :],
                                            start=True, stop=True)
                last.then_inc(logits_ps, 1)

            def ranks(c):
                pe.wait_ge(one_hot_ready, c + 1)
                r = rank_bank
                oh = [one_hot_sum[:, a, :] for a in range(2)]
                nc.tensor.matmul(r[:, 0:E], before16[:, :], oh[0], start=True, stop=True)
                nc.tensor.matmul(r[:, E:2 * E], before16[:, :], oh[1], start=True, stop=False)
                nc.tensor.matmul(r[:, E:2 * E], ones16[:, :], oh[0], start=False, stop=True)
                nc.tensor.matmul(r[:, 2 * E:3 * E], ones16[:, :], oh[0], start=True, stop=False)
                nc.tensor.matmul(r[:, 2 * E:3 * E], ones16[:, :], oh[1], start=False, stop=True).then_inc(rank_ps, 1)

            def transpose_slots(k):
                pe.wait_ge(slots_ready, k)
                for kind in range(2):
                    last = nc.tensor.transpose(slots_bank[k - 1][:, kind * P:(kind + 1) * P], sched[:, 6 + kind:7 + kind], id32[:, :])
                last.then_inc(slots_ps, 1)

            def transpose_rows(i, k8):
                pe.wait_ge(x_rows_in[k8], 2 * (i - k8) + 16)
                half = xt_bank[k8 % 4].bitcast(F16)
                for k in range(2):
                    last = nc.tensor.transpose(half[:, k * P:(k + 1) * P],
                                               x_rows[:, k8, k * D // 2:(k + 1) * D // 2].bitcast(F16), id16[:, :])
                last.then_inc(xt_ps, 1)

            def chunk(c, last=False):
                for u in range(G):
                    if u + 2 < G:
                        scores(c, u + 2)
                    elif not last:
                        scores(c + 1, u + 2 - G)
                    if last and u == G - 1:
                        transpose_rows(0, 0)
                    values(c, u)
                    if at_least(c, 1):
                        if u == 7:
                            transpose_f2(c - 1)
                        if u == 8:
                            gate_logits(c - 1)
                        if u == 11:
                            ranks(c - 1)
                    if last and u == 7:
                        transpose_slots(1)

            chunk(0)
            with pe.Fori(1, G - 1) as c:
                chunk(c)
            chunk(G - 1, last=True)

            pe.wait_ge(sched_done, 1)
            pe.wait_ge(w_lo_done, 3 * (E // 4))

            def expert_in(i, k8, expert):
                rows_first = isinstance(i, int) and i < EARLY
                if at_least(i, 1) and before(i, SLOTS + 1):
                    pe.wait_ge(xt_done, i)
                if rows_first and at_least(i, 1):
                    transpose_rows(i, k8)
                if at_least(i, 1) and before(i, SLOTS + 1):
                    b4, b2 = (k8 - 1) % 4, (k8 - 1) % 2
                    nc.tensor.matmul(bank[b2][:, :], xt_sb[:, b4, 0:P], w12_hi[:, bass.ds(expert, 1), :], start=True, stop=False)
                    nc.tensor.matmul(bank[b2][:, :], xt_sb[:, b4, P:2 * P], w12_hi[:, bass.ds(expert, 1), :], start=False, stop=False)
                    nc.tensor.matmul(bank[b2][:, :], xt_sb[:, b4, 0:P], w12_lo[:, bass.ds(expert, 1), :], start=False, stop=True).then_inc(h_ps, 1)
                if not rows_first and before(i, SLOTS):
                    transpose_rows(i, k8)

            def expert_out(i, k8, expert):
                if at_least(i, 2) and before(i, SLOTS + 2):
                    t, b4, b2 = i - 2, (k8 - 2) % 4, k8 % 2
                    pe.wait_ge(hid_done, t + 1)
                    for k in range(2):
                        last = nc.tensor.transpose(bank[2 + b2][:, k * P:(k + 1) * P], hid_sb[:, b4, k * P:(k + 1) * P], id32[:, :])
                    last.then_inc(ht_ps, 1)
                if at_least(i, 3):
                    t, b4 = i - 3, (k8 - 3) % 4
                    pe.wait_ge(ht_lo_done, t + 1)
                    if isinstance(i, int) and i == 3:
                        pe.wait_ge(o_evac, G)
                    for k in range(H // P):
                        hh, hl = ht_hi[:, b4, k * P:(k + 1) * P], ht_lo[:, b4, k * P:(k + 1) * P]
                        wh = w3_hi[:, bass.ds(expert, 1), k * D:(k + 1) * D]
                        wl = w3_lo[:, bass.ds(expert, 1), k * D:(k + 1) * D]
                        nc.tensor.matmul(y_bank[b4], hh, wh, start=(k == 0), stop=False)
                        nc.tensor.matmul(y_bank[b4], hl, wh, start=False, stop=False)
                        last = nc.tensor.matmul(y_bank[b4], hh, wl, start=False, stop=(k == 1))
                    last.then_inc(y_ps, 1)

            def load_experts(first, count):
                return load_values(mybir.EngineType.PE, 1, first, count, E - 1)

            expert_of = dict(enumerate(load_experts(0, 7)))
            for i in range(EARLY):
                expert_in(i, i % 8, expert_of.get(i - 1))
                if i % 8 == 7:
                    count = min(8, EARLY - i)
                    expert_of.update(zip(range(i, i + count), load_experts(i, count)))
                expert_out(i, i % 8, expert_of.get(i - 3))
                if i == 5:
                    transpose_f2(G - 1)
                if i == 8:
                    gate_logits(G - 1)
                if i == 11:
                    ranks(G - 1)
                if i == 21:
                    transpose_slots(2)
            expert_in(EARLY, EARLY % 8, expert_of[EARLY - 1])
            pe.wait_ge(sched_done, 2)
            turns = (SLOTS - EARLY) // 8 - 1
            with pe.Fori(0, turns) as turn:
                i = turn * 8 + EARLY
                expert_of_turn = load_experts(i - 3, 11)
                for k in range(8):
                    expert_out(i + k, (EARLY + k) % 8, expert_of_turn[k])
                    expert_in(i + (k + 1), (EARLY + k + 1) % 8, expert_of_turn[k + 3])
            first = EARLY + 8 * turns
            expert_of = dict(zip(range(first - 3, SLOTS), load_experts(first - 3, SLOTS + 3 - first)))
            for i in range(first, SLOTS + 3):
                expert_out(i, i % 8, expert_of[i - 3])
                expert_in(i + 1, (i + 1) % 8, expert_of.get(i))

        @block.scalar
        def _(act):
            act.wait_ge(wt_ps, 1)
            nc.scalar.copy(wqk_t[:, :], misc[0][:, 0:CH]).then_inc(wt_done, 1)
            def f_high(i):
                at = slice(PARTS[i], PARTS[i + 1])
                by_vector, by_scalar = normed(PARTS[i + 1])
                act.wait_ge(f_done, by_vector)
                if by_scalar:
                    act.wait_ge(f_done2, by_scalar)
                nc.scalar.copy(f_aug[:, at, 0:D], f_sb[:, at.start * D:at.stop * D].rearrange("p (t d) -> p t d", d=D)).then_inc(f_hi_done, 1)

            def project(i, k4):
                b, o = k4 % 2, 1 - k4 % 2
                if before(i, G):
                    act.wait_ge(ft_ps, i + 1)
                    if at_least(i, 2):
                        act.wait_ge(proj_ps, i - 1)
                    nc.scalar.copy(ft_sb[:, b, :], misc[b][:, 0:CH]).then_inc(ft_copied, 1)
                if at_least(i, 1) and before(i, G + 1):
                    act.wait_ge(proj_ps, i)
                    if at_least(i, 2):
                        act.wait_ge(ss_summed, i - 1)
                    nc.scalar.activation(sq_sb, proj_bank(k4 - 1)[:, :], ACT.Square).then_inc(squared, 1)
                if at_least(i, 3):
                    act.wait_ge(qt_ps, i - 2)
                    nc.scalar.copy(qk_hi[:, bass.ds(i - 3, 1), :, :],
                                   o_ps[:, o, :].rearrange("p (o a n) -> p o a n", o=1, a=2)).then_inc(q_hi_done, 1)

            def normalise(first, last):
                act.wait_ge(shift_done, 1 if last <= PARTS[2] else 2)
                for t in range(first, last):
                    nc.scalar.activation(f_sb[:, t * D:(t + 1) * D], x_sb[:, t * D:(t + 1) * D], ACT.Identity,
                                         scale=rstd[:, t:t + 1], bias=shift[:, t:t + 1]).then_inc(f_done2, 1)

            project(0, 0)
            project(1, 1)
            normalise(10, 14)
            project(2, 2)
            normalise(20, 23)
            project(3, 3)
            normalise(23, T)
            f_high(0)
            with act.Fori(1, G // 4) as turn:
                for k in range(4):
                    project(turn * 4 + k, k)
            f_high(1)
            for i in range(G // 4 * 4, G + 2):
                project(i, i % 4)

            def probabilities(c, u):
                act.wait_ge(s_done, c * G + u + 1)
                if u < 3 and at_least(c, 1):
                    act.wait_ge(pv_done, c * G + u - 3)
                elif 3 <= u < G - 1:
                    act.wait_ge(pv_done, c * G + u - 2)
                elif u == G - 1 and at_least(c, 1):
                    act.wait_ge(pv_done, c * G)
                b = BUF[u]
                nc.scalar.activation(p_full[:, b, :], bank[b][:, :], ACT.Exp).then_inc(p_done, 1)
                nc.scalar.activation(p_hi[:, b, :], bank[b][:, :], ACT.Exp).then_inc(p_hi_done, 1)

            def evacuate(c):
                act.wait_ge(pv_done, (c + 1) * G)
                nc.scalar.copy(o_sb[:, :, :], o_ps[:, :, 0:2 * D + 1]).then_inc(o_evac, 1)

            def copy_f2t(c):
                act.wait_ge(f2t_ps, c + 1)
                nc.scalar.copy(f2_t[:, :], f2t_bank).then_inc(f2t_done, 1)

            def exp_gate(c):
                act.wait_ge(gap_ready, c + 1)
                nc.scalar.activation(small[:, 8, :], small[:, 7, :], ACT.Exp).then_inc(gate_exp, 1)

            def rows_high(c):
                act.wait_ge(f2_ready, c + 1)
                act.wait_ge(rows_free, c + 1)
                nc.scalar.copy(rows_hi, f2_twice).then_inc(rows_hi_ready, 1)

            def weight_high(c, kind, e):
                act.wait_ge(w_raw_in, 16 * (c + 1))
                nc.scalar.copy(weight_parts(kind, e)[0], w_raw[:, :, :]).then_inc(w_hi_done, 1)

            def chunk(c, kind, e):
                for u in range(G):
                    if isinstance(c, int) and c == 0 and u == 0:
                        probabilities(0, 0)
                        project(G + 2, (G + 2) % 4)
                        continue
                    probabilities(c, u)
                    if isinstance(c, int) and c == 0 and u == 1:
                        f_high(2)
                    if at_least(c, 1):
                        if u == 1:
                            evacuate(c - 1)
                        if u == 9:
                            copy_f2t(c - 1)
                        if u == 10:
                            rows_high(c - 1)
                        if u == 11:
                            weight_high(c - 1, kind, e)
                        if u == 12:
                            exp_gate(c - 1)

            chunk(0, None, None)
            with act.Fori(0, E // 4) as lot:
                for kind in range(3):
                    chunk(lot * 3 + (kind + 1), kind, lot * 4)
            nc.scalar.activation(small[:, 11, :], neg_half[:, 0:2], ACT.Silu)
            evacuate(G - 1)

            def expert(i, k8):
                if before(i, SLOTS):
                    act.wait_ge(x_rows_in[k8], 2 * (i - k8) + 16)
                    if at_least(i, 8):
                        act.wait_ge(y_stored[k8], 2 * (i - k8))
                    nc.scalar.copy(y_idx[:, k8:k8 + 1], x_rows[:, k8, D + 1:D + 2].bitcast(I32))
                    nc.scalar.copy(y_gate[:, k8:k8 + 1], x_rows[:, k8, D:D + 1]).then_inc(tail_done, 1)
                    act.wait_ge(h_ps, i + 1)
                    nc.scalar.activation(act_sb[:, k8 % 4, :], bank[k8 % 2][:, 0:H], ACT.Silu).then_inc(act_done, 1)
                if at_least(i, 1) and before(i, SLOTS + 1):
                    act.wait_ge(ht_ps, i)
                    nc.scalar.copy(ht_hi[:, (k8 - 1) % 4, :], bank[2 + (k8 - 1) % 2][:, 0:H]).then_inc(ht_hi_done, 1)
                if at_least(i, 2):
                    t, b = i - 2, (k8 - 2) % 4
                    act.wait_ge(y_ps, t + 1)
                    nc.scalar.mul(y_sb[:, (k8 - 2) % 8, :], y_bank[b], y_gate[:, (k8 - 2) % 8:(k8 - 2) % 8 + 1]).then_inc(y_done, 1)

            for i in range(EARLY):
                expert(i, i % 8)
                if i == 5:
                    copy_f2t(G - 1)
                if i == 7:
                    rows_high(G - 1)
            spread(act, expert, SLOTS + 2, 8, EARLY, 2, done=EARLY)
            for b in range(8):
                act.wait_ge(y_stored[b], 16 * len(range(b, SLOTS, 8)))
            for i in reversed(range(5)):
                a, b = CUTS[i], CUTS[i + 1]
                act.dma_start(yb_sb[:, a * D:b * D].rearrange("p (t d) -> p t d", d=D),
                              expert_out[NP + a * P:NP + b * P, :].rearrange("(t p) d -> p t d", p=P)).then_inc(yb_in[i], 16)

        @block.vector
        def _(dve):
            def statistics(i):
                dve.wait_ge(x_in[i], 48 if i == len(PARTS) - 2 else 16)
                for t in range(PARTS[i], PARTS[i + 1]):
                    nc.vector.bn_stats(stats[:, t, :], x_sb[:, t * D:(t + 1) * D]).then_inc(stats_done, 1)
                for t in range(PARTS[i], PARTS[i + 1]):
                    dve.wait_ge(stats_done, t + 1)
                    nc.vector.bn_aggr(mean_var[:, t, :], stats[:, t, :]).then_inc(aggr_done, 1)
                dve.wait_ge(aggr_done, PARTS[i + 1])
                at = slice(PARTS[i], PARTS[i + 1])
                nc.vector.tensor_scalar(neg_mean[:, at], mean_var[:, at, 0], -1.0, None, ALU.mult)
                nc.vector.tensor_scalar(var_eps[:, at], mean_var[:, at, 1], LN_EPS, None, ALU.add).then_inc(var_done, 1)

            def normalise(first, last):
                dve.wait_ge(rstd_done, next(i for i in range(1, len(PARTS)) if last <= PARTS[i]))
                for t in range(first, last):
                    nc.vector.tensor_scalar(f_sb[:, t * D:(t + 1) * D], x_sb[:, t * D:(t + 1) * D], mean_var[:, t, 0:1],
                                            rstd[:, t:t + 1], ALU.subtract, ALU.mult).then_inc(f_done, 1)

            def q_low(g, b):
                dve.wait_ge(q_hi_done, g + 1)
                nc.vector.tensor_tensor(qk_lo[:, bass.ds(g, 1), :, :], o_ps[:, b, :].rearrange("p (o a n) -> p o a n", o=1, a=2),
                                        qk_hi[:, bass.ds(g, 1), :, :], ALU.subtract).then_inc(q_lo_done, 1)

            def project(i, k4):
                b, o = k4 % 2, 1 - k4 % 2
                if before(i, G):
                    dve.wait_ge(squared, i + 1)
                    if at_least(i, 2):
                        dve.wait_ge(ss_clamped, i - 1)
                    nc.vector.tensor_reduce(ss[:, b, :], sq_sb.rearrange("p (a n) -> p a n", a=4),
                                            axis=AX_X, op=ALU.add).then_inc(ss_summed, 1)
                    dve.wait_ge(ss_summed, i + 1)
                    if at_least(i, 2):
                        dve.wait_ge(rnorm_done, i - 1)
                    nc.vector.tensor_scalar(ss_max[:, b, :], ss[:, b, :], COS_EPS * COS_EPS, None, ALU.max).then_inc(ss_clamped, 1)
                if at_least(i, 1) and before(i, G + 1):
                    dve.wait_ge(rnorm_done, i)
                    if at_least(i, 3):
                        dve.wait_ge(qt_ps, i - 2)
                    nc.vector.tensor_tensor(qn_sb[:, o, :].rearrange("p (a n) -> p a n", a=4),
                                            proj_bank(k4 - 1)[:, :].rearrange("p (a n) -> p a n", a=4),
                                            rnorm[:, o, :].unsqueeze(2).to_broadcast([P, 4, P]), ALU.mult).then_inc(qn_scaled, 1)
                if at_least(i, 2):
                    q_low(i - 2, b)

            def make_mask(c, u):
                s = next(s for s in range(len(SEGS) - 1) if u < SEGS[s + 1])
                if u == SEGS[s]:
                    if isinstance(c, int) and c == G - 1:
                        dve.wait_ge(adj_in[s], 16 * (c + 3))
                    else:
                        dve.wait_ge(adj_in[s], 16 * (c + 1))
                if at_least(c, 1):
                    dve.wait_ge(s_done, (c - 1) * G + u + 1)
                at = slice(u * CH, (u + 1) * CH)
                nc.vector.tensor_scalar(mask[:, :, at], adj_sb[:, :, at], 0.0, MASKED, ALU.is_le,
                                        ALU.mult).then_inc(mask0_done if isinstance(c, int) and c == 0 else mask_done, 1)

            def low_part(c, u):
                b = BUF[u]
                dve.wait_ge(p_hi_done, c * G + u + 1)
                dve.wait_ge(p_done, c * G + u + 1)
                nc.vector.tensor_tensor(p_lo[:, b, :], p_full[:, b, :], p_hi[:, b, :], ALU.subtract).then_inc(p_lo_done, 1)

            statistics(0)
            statistics(1)
            normalise(0, PARTS[1])
            statistics(2)
            normalise(PARTS[1], 10)
            project(0, 0)
            normalise(14, 17)
            project(1, 1)
            normalise(17, 20)
            project(2, 2)
            project(3, 3)
            with dve.Fori(1, G // 4) as turn:
                for k in range(4):
                    project(turn * 4 + k, k)
            dve.wait_ge(adj_padded, 1)
            for i in range(G // 4 * 4, G + 2):
                make_mask(0, i - G // 4 * 4)
                if i == G + 1:
                    low_part(0, 0)
                project(i, i % 4)
            for u in range(G + 2 - G // 4 * 4, AHEAD):
                make_mask(0, u)

            k = [0]

            def ep(c, ins, alone=False):
                k[0] += 1
                ins.then_inc(dve_ep, 1)
                (wait_alone(dve, dve_ep, c * DVE_EP + k[0]) if alone else dve.wait_ge(dve_ep, c * DVE_EP + k[0]))

            def epilogue_weights(c):
                k[0] = 0
                dve.wait_ge(o_evac, c + 1)
                total = o_sb[:, :, D]
                ep(c, nc.vector.tensor_scalar(small[:, 0, :], total, 1e-30, None, ALU.max))
                ep(c, nc.vector.reciprocal(small[:, 1, :], small[:, 0, :]))
                ep(c, nc.vector.tensor_scalar(small[:, 2, :], total, 0.0, 0.5, ALU.is_gt, ALU.mult))
                ep(c, nc.vector.tensor_tensor(small[:, 3, :], small[:, 1, :], small[:, 2, :], ALU.mult))
                nc.vector.tensor_scalar(small[:, 4, :], small[:, 2, :], -1.0, 1.0, ALU.mult, ALU.add).then_inc(weights_ready, 1)

            def epilogue_stats(c):
                dve.wait_ge(x2_ready, c + 1)
                for a in range(2):
                    ep(c, nc.vector.bn_stats(stats2[:, a, :], x_sb[:, bass.ds(c * CH + a * D, D)]), a == 1)
                for a in range(2):
                    ep(c, nc.vector.bn_aggr(mean_var2[:, a, :], stats2[:, a, :]), a == 0)
                nc.vector.tensor_scalar(small[:, 5, :], mean_var2[:, :, 1], LN_EPS, None, ALU.add).then_inc(var2_ready, 1)

            def epilogue_norm(c):
                dve.wait_ge(rstd2_ready, c + 1)
                for a in range(2):
                    last = nc.vector.tensor_scalar(f2[:, a, :], x_sb[:, bass.ds(c * CH + a * D, D)], mean_var2[:, a, 0:1],
                                                   small[:, 6, a:a + 1], ALU.subtract, ALU.mult)
                last.then_inc(f2_ready, 1)

            def epilogue_route(c):
                dve.wait_ge(logits_ps, c + 1)
                ep(c, nc.vector.tensor_tensor(logits[:, :, :], logits_bank.rearrange("p (a e) -> p a e", a=2),
                                              gate_bias[:, :].unsqueeze(1).to_broadcast([P, 2, E]), ALU.add), True)
                for a in range(2):
                    ep(c, nc.vector.max(top_v[:, a, :], logits[:, a, :]), a == 0)
                nc.vector.tensor_tensor(small[:, 7, :], top_v[:, :, 1], top_v[:, :, 0], ALU.subtract).then_inc(gap_ready, 1)

            def epilogue_one_hot(c):
                for a in range(2):
                    ep(c, nc.vector.max_index(top_i[:, a, :], top_v[:, a, :], logits[:, a, :]), a == 0)
                ep(c, nc.vector.tensor_copy(top_f[:, :, :], top_i[:, :, 0:2]))
                ep(c, nc.vector.tensor_tensor(one_hot[:, :, :].rearrange("p (a k) e -> p a k e", a=2),
                                              expert_f[:, :].unsqueeze(1).unsqueeze(1).to_broadcast([P, 2, 2, E]),
                                              top_f[:, :, :].unsqueeze(3).to_broadcast([P, 2, 2, E]), ALU.is_equal))
                oh = one_hot[:, :, :].rearrange("p (a k) e -> p a k e", a=2)
                nc.vector.tensor_tensor(one_hot_sum[:, :, :], oh[:, :, 0, :], oh[:, :, 1, :], ALU.add).then_inc(one_hot_ready, 1)

            def epilogue_tails(c):
                tail = rows[:, :, :].rearrange("p (a k) n -> p a k n", a=2)
                dve.wait_ge(gate_exp, c + 1)
                ep(c, nc.vector.tensor_scalar(small[:, 9, :], small[:, 8, :], 1.0, None, ALU.add))
                ep(c, nc.vector.reciprocal(small[:, 10, :], small[:, 9, :]))
                nc.vector.tensor_copy(tail[:, :, 0, D], small[:, 10, :])
                nc.vector.tensor_tensor(tail[:, :, 1, D], small[:, 8, :], small[:, 10, :], ALU.mult)
                ep(c, nc.vector.tensor_copy(tail[:, :, :, D + 1].bitcast(I32), dest_f[:, :, :]))
                nc.vector.tensor_scalar(dest_f[:, :, :], dest_f[:, :, :], float(CH), None, ALU.add).then_inc(tails_ready, 1)

            def epilogue_places(c):
                m = [0]

                def ep(c, ins):
                    m[0] += 1
                    ins.then_inc(place_steps, 1)
                    dve.wait_ge(place_steps, c * PLACE_STEPS + m[0])

                oh = one_hot[:, :, :].rearrange("p (a k) e -> p a k e", a=2)
                dve.wait_ge(rank_ps, c + 1)
                ep(c, nc.vector.tensor_tensor(row_of[:, :, :], rank_bank[:, 0:2 * E].rearrange("p (a e) -> p a e", a=2),
                                              next_row[:, :].unsqueeze(1).to_broadcast([P, 2, E]), ALU.add))
                ep(c, nc.vector.tensor_tensor(row_pick[:, :, :].rearrange("p (a k) e -> p a k e", a=2), oh,
                                              row_of[:, :, :].unsqueeze(2).to_broadcast([P, 2, 2, E]), ALU.mult))
                ep(c, nc.vector.tensor_tensor(next_row[:, :], next_row[:, :], rank_bank[:, 2 * E:3 * E], ALU.add))
                ep(c, nc.vector.tensor_reduce(row_f[:, :], row_pick[:, :, :], axis=AX_X, op=ALU.add))
                nc.vector.tensor_copy(row_i[:, :], row_f[:, :]).then_inc(places_ready, 1)
                assert m[0] == PLACE_STEPS

            m = [0]

            def step(ins):
                m[0] += 1
                ins.then_inc(sched_steps, 1)
                dve.wait_ge(sched_steps, m[0])

            def count_tiles(rest):
                step(nc.vector.tensor_tensor(cum_f[:, :], next_row[:, :], base_f[:, :], ALU.subtract))
                step(nc.vector.tensor_scalar(tiles_i[:, :], cum_f[:, :], float(P - 1 if rest else 0), None, ALU.add))
                step(nc.vector.tensor_scalar(tiles_i[:, :], tiles_i[:, :], P.bit_length() - 1, None, ALU.arith_shift_right))
                step(nc.vector.tensor_copy(tiles_f[:, :], tiles_i[:, :]))

            def sum_tiles():
                step(nc.vector.tensor_tensor(grid[:, :, :], tri_e[:, :, :], tiles_f[:, :].unsqueeze(1).to_broadcast([P, E, E]), ALU.mult))
                step(nc.vector.tensor_reduce(cum_f[:, :], grid[:, :, :], axis=AX_X, op=ALU.add))

            def find_experts():
                step(nc.vector.tensor_scalar(done_e[:, 0, :], cum_f[:, :], part_f[:, 0:1], None, ALU.is_le))
                step(nc.vector.tensor_tensor(done_e[:, 1, :], done_e[:, 0, :], tiles_f[:, :], ALU.mult))
                step(nc.vector.tensor_reduce(sched[:, 0:2], done_e[:, :, :], axis=AX_X, op=ALU.add))

            def find_bases():
                step(nc.vector.tensor_scalar(at_expert[:, 0, :], expert_f[:, :], sched[:, 0:1], None, ALU.is_equal))
                step(nc.vector.tensor_tensor(at_expert[:, 1, :], at_expert[:, 0, :], base_f[:, :], ALU.mult))
                step(nc.vector.tensor_reduce(sched[:, 2:3], at_expert[:, 1, :], axis=AX_X, op=ALU.add))

            def find_rows():
                spare = float(E * REGION)
                nc.vector.tensor_scalar(sched[:, 4:5], sched[:, 0:1], float(E), None, ALU.is_lt)
                step(nc.vector.tensor_tensor(sched[:, 3:4], part_f[:, :], sched[:, 1:2], ALU.subtract))
                step(nc.vector.tensor_scalar(sched[:, 3:4], sched[:, 3:4], float(P), sched[:, 2:3], ALU.mult, ALU.add))
                step(nc.vector.tensor_scalar(sched[:, 5:6], sched[:, 3:4], -spare, sched[:, 4:5], ALU.add, ALU.mult))
                nc.vector.tensor_scalar(sched[:, 6:7], sched[:, 5:6], spare, None, ALU.add)
                nc.vector.tensor_scalar(sched[:, 7:8], sched[:, 0:1], float(E - 1), None, ALU.min).then_inc(slots_ready, 1)

            def copy_slots(k, first):
                dve.wait_ge(slots_ps, k)
                nc.vector.tensor_copy(slot_table[:, :, first:P],
                                      slots_bank[k - 1].rearrange("p (k t) -> p k t", k=2)[:, :, 0:P - first]).then_inc(sched_done, 1)

            def take_tiles():
                step(nc.vector.tensor_tensor(taken[:, 0, :], cum_f[:, :], tiles_f[:, :], ALU.subtract))
                step(nc.vector.tensor_scalar(taken[:, 0, :], taken[:, 0, :], float(EARLY), None, ALU.min))
                step(nc.vector.tensor_scalar(taken[:, 1, :], cum_f[:, :], float(EARLY), None, ALU.min))
                step(nc.vector.tensor_tensor(taken[:, 1, :], taken[:, 1, :], taken[:, 0, :], ALU.subtract))
                step(nc.vector.tensor_scalar(taken[:, 1, :], taken[:, 1, :], float(P), None, ALU.mult))
                step(nc.vector.tensor_tensor(base_f[:, :], base_f[:, :], taken[:, 1, :], ALU.add))

            def padding_ends():
                step(nc.vector.tensor_scalar(ends_i[:, :], next_row[:, :], float(BLOCK - 1), None, ALU.add))
                step(nc.vector.tensor_scalar(ends_i[:, :], ends_i[:, :], BLOCK.bit_length() - 1, None, ALU.arith_shift_right))
                step(nc.vector.tensor_copy(ends[:, 1, :], ends_i[:, :]))
                step(nc.vector.tensor_copy(ends[:, 0, :], next_row[:, :]))
                step(nc.vector.tensor_tensor(pad_pick[:, :, :], ends[:, :, :], pad_e[:, :].unsqueeze(1).to_broadcast([P, 2, E]), ALU.mult))
                step(nc.vector.tensor_reduce(pad_end[:, :], pad_pick[:, :, :], axis=AX_X, op=ALU.add))

            def place_padding():
                step(nc.vector.tensor_tensor(pad_idx[:, 2:3], pad_end[:, 1:2], pad_of[:, :], ALU.add))
                step(nc.vector.tensor_tensor(pad_row[:, 0, :], pad_of2[:, :], pad_end[:, 0:1].to_broadcast([P, 2]), ALU.add))
                step(nc.vector.tensor_scalar(sched[:, 0:1], pad_end[:, 1:2], float(BLOCK), None, ALU.mult))
                step(nc.vector.tensor_tensor(pad_row[:, 1, :], pad_row[:, 0, :], sched[:, 0:1].to_broadcast([P, 2]), ALU.is_ge))
                step(nc.vector.tensor_scalar(pad_row[:, 1, :], pad_row[:, 1, :], float(NO_ROW), None, ALU.mult))
                nc.vector.tensor_tensor(pad_idx[:, 0:2], pad_row[:, 0, :], pad_row[:, 1, :], ALU.add).then_inc(pads_ready, 1)

            def chunk(c, last=False):
                for u in range(G):
                    if isinstance(c, int) and c == 0:
                        if u > 0:
                            low_part(c, u)
                        if u + AHEAD < G:
                            make_mask(0, u + AHEAD)
                        if u >= BEHIND:
                            make_mask(1, u - BEHIND)
                    else:
                        if isinstance(c, int) and c == 1 and u == 0:
                            for v in range(G - BEHIND, G):
                                make_mask(1, v)
                        low_part(c, u)
                        if not last:
                            make_mask(c + 1, u)
                    if at_least(c, 2) and u == 1:
                        epilogue_places(c - 2)
                    if at_least(c, 1):
                        if u == 2:
                            epilogue_weights(c - 1)
                        if u == 5:
                            epilogue_stats(c - 1)
                        if u == 7:
                            epilogue_norm(c - 1)
                        if u == 10:
                            epilogue_route(c - 1)
                            epilogue_one_hot(c - 1)
                        if u == 12 and not last:
                            epilogue_tails(c - 1)
                            assert k[0] == DVE_EP, k[0]
                    if last:
                        if u == 3:
                            count_tiles(rest=False)
                            sum_tiles()
                        if u == 4:
                            find_experts()
                            find_bases()
                        if u == 6:
                            find_rows()
                        if u == 8:
                            copy_slots(1, 0)
                        if u == 9:
                            take_tiles()

            dve.wait_ge(consts, 1)
            dve.wait_ge(gate_in, 32)
            chunk(0)
            chunk(1)
            with dve.Fori(2, G - 2) as c:
                chunk(c)
            dve.wait_ge(consts, 2)
            step(nc.vector.tensor_reduce(sched[:, 0:1], pad_pick[:, 1, :], axis=AX_X, op=ALU.add))
            step(nc.vector.tensor_tensor(pad_of[:, :], sched[:, 0:1], part_f[:, :], ALU.add))
            for j in range(2):
                step(nc.vector.tensor_scalar(pad_of2[:, j:j + 1], pad_of[:, :], 2.0, float(j), ALU.mult, ALU.add))
            chunk(G - 2)
            chunk(G - 1, last=True)
            def copy_rows(i, k8):
                if before(i, SLOTS):
                    dve.wait_ge(xt_ps, i + 1)
                    nc.vector.tensor_copy(xt_sb[:, k8 % 4, :], xt_bank[k8 % 4].bitcast(F16)).then_inc(xt_done, 1)

            def gate_and_split(i, k8):
                if at_least(i, 1) and before(i, SLOTS + 1):
                    b4 = (k8 - 1) % 4
                    dve.wait_ge(act_done, i)
                    nc.vector.tensor_tensor(hid_sb[:, b4, :], act_sb[:, b4, :], bank[b4 % 2][:, H:2 * H], ALU.mult).then_inc(hid_done, 1)
                if at_least(i, 2):
                    b4 = (k8 - 2) % 4
                    dve.wait_ge(ht_hi_done, i - 1)
                    nc.vector.tensor_tensor(ht_lo[:, b4, :], bank[2 + b4 % 2][:, 0:H], ht_hi[:, b4, :], ALU.subtract).then_inc(ht_lo_done, 1)

            def expert(i, k8):
                copy_rows(i, k8)
                gate_and_split(i, k8)

            for i in range(EARLY):
                copy_rows(i, i % 8)
                if i == 0:
                    epilogue_tails(G - 2)
                    assert k[0] == DVE_EP, k[0]
                    epilogue_weights(G - 1)
                if i == 1:
                    epilogue_places(G - 2)
                if i == 3:
                    epilogue_stats(G - 1)
                if i == 4:
                    epilogue_norm(G - 1)
                if i == 9:
                    epilogue_route(G - 1)
                if i == 10:
                    epilogue_one_hot(G - 1)
                if i == 12:
                    epilogue_tails(G - 1)
                    assert k[0] == DVE_EP, k[0]
                if i == 13:
                    epilogue_places(G - 1)
                if i == 14:
                    padding_ends()
                if i == 15:
                    place_padding()
                if i == 16:
                    count_tiles(rest=True)
                if i == 17:
                    sum_tiles()
                if i == 18:
                    find_experts()
                if i == 19:
                    find_bases()
                if i == 20:
                    find_rows()
                if i == 22:
                    copy_slots(2, EARLY)
                gate_and_split(i, i % 8)
            spread(dve, expert, SLOTS + 2, 8, EARLY, 2, done=EARLY)

            for n, i in enumerate(reversed(range(5))):
                at = slice(CUTS[i] * D, CUTS[i + 1] * D)
                dve.wait_ge(ya_in[i], 16)
                nc.vector.tensor_tensor(x_sb[:, at], x_sb[:, at], ya_sb[:, at], ALU.add).then_inc(sum_a, 1)
                dve.wait_ge(yb_in[i], 16)
                dve.wait_ge(sum_a, n + 1)
                nc.vector.tensor_tensor(x_sb[:, at], x_sb[:, at], yb_sb[:, at], ALU.add).then_inc(sum_done, 1)


_INS = ["x", "adj", "L0_gnn_Wq", "L0_gnn_Wk", "L0_ffn_gate_w", "L0_ffn_gate_b", "L0_ffn_w1", "L0_ffn_w2", "L0_ffn_w3"]


def kernel(**inputs):
    import numpy as _np
    import concourse.bacc as _bacc
    from concourse import mybir as _mybir
    from concourse.bass_utils import run_bass_kernel_spmd as _run

    nc = _bacc.Bacc("TRN2", target_bir_lowering=False, num_devices=1)
    arrays, args = {}, []
    for name in _INS:
        a = _np.ascontiguousarray(inputs[name])
        arrays[f"in_{name}_dram"] = a
        args.append(nc.dram_tensor(f"in_{name}_dram", a.shape, _mybir.dt.from_np(a.dtype), kind="ExternalInput").ap())
    result = nc.dram_tensor("out_dram", inputs["x"].shape, _mybir.dt.float32, kind="ExternalOutput").ap()
    graph_attention_moe(nc, *args, result)
    r = _run(nc, [arrays], core_ids=[0])
    return r.results[0]["out_dram"]
```
